# Optimizing a Trainium2 kernel written in Bass

```python
import numpy as np
import jax
import jax.numpy as jnp

def _softmax(x, axis=-1):
    return jax.nn.softmax(x, axis=axis)

def _gelu(x):
    return jax.nn.gelu(x, approximate=True)

def _silu(x):
    return jax.nn.silu(x)

def _sigmoid(x):
    return jax.nn.sigmoid(x)

def _layernorm(x, axis=-1, eps=1e-05):
    m = jnp.mean(x, axis=axis, keepdims=True)
    v = jnp.var(x, axis=axis, keepdims=True)
    return (x - m) / jnp.sqrt(v + eps)

def _scatter_add(tgt, idx, src, axis=0):
    return tgt.at[idx].add(src)

def _segment_sum(src, seg, n):
    return jax.ops.segment_sum(src, seg, n)
kernel_name = 'mk_conv_attn_hybrid_d2_conv_nhwc256_r2_672dbb'

def setup_inputs(seed: int=0):
    np.random.seed(seed)
    _w = jnp.asarray

    def _rec_inputs():
        import jax
        import jax.numpy as jnp
        _gk = jax.random.key(seed)
        x = -0.0002928 + 1 * jax.random.normal(jax.random.fold_in(_gk, 1), (4, 32, 32, 128), jnp.float32)
        return x
    x = _rec_inputs()

    def _L0_conv_setup():
        import jax, jax.numpy as jnp
        import numpy as np
        import math
        B, H, W, CIN = (4, 32, 32, 128)
        G, C, K = (8, 32, 9)
        MAX_SCALE = 6.0

        def _dcn_sample(v, deform, weights):
            b_, h_, w_, g_, c_ = v.shape
            ww = jnp.arange(w_, dtype=v.dtype)[None, None, :, None, None]
            hh = jnp.arange(h_, dtype=v.dtype)[None, :, None, None, None]
            px = ww + deform[..., 0]
            py = hh + deform[..., 1]
            x0 = jnp.floor(px)
            y0 = jnp.floor(py)
            wx1 = px - x0
            wx0 = 1.0 - wx1
            wy1 = py - y0
            wy0 = 1.0 - wy1
            bidx = jnp.arange(b_)[:, None, None, None, None]
            gidx = jnp.arange(g_)[None, None, None, :, None]

            def gather(yi, xi):
                valid = ((yi >= 0) & (yi < h_) & (xi >= 0) & (xi < w_)).astype(v.dtype)
                yc = jnp.clip(yi, 0, h_ - 1).astype(jnp.int32)
                xc = jnp.clip(xi, 0, w_ - 1).astype(jnp.int32)
                return v[bidx, yc, xc, gidx] * valid[..., None]
            samp = gather(y0, x0) * (wy0 * wx0)[..., None] + gather(y0, x0 + 1) * (wy0 * wx1)[..., None] + gather(y0 + 1, x0) * (wy1 * wx0)[..., None] + gather(y0 + 1, x0 + 1) * (wy1 * wx1)[..., None]
            return jnp.einsum('bhwgkc,bhwgk->bhwgc', samp, weights)
        key = jax.random.key(seed)
        ks = jax.random.split(key, 10)
        s = 0.02
        x = jax.random.normal(ks[0], (B, H, W, CIN), dtype=jnp.float32)
        v_w = jax.random.normal(ks[1], (CIN, G * C), dtype=jnp.float32) * s
        v_b = jax.random.normal(ks[2], (G * C,), dtype=jnp.float32) * s
        qd_w = jax.random.normal(ks[3], (CIN, G * K * 2), dtype=jnp.float32) * s
        qd_b = jax.random.normal(ks[4], (G * K * 2,), dtype=jnp.float32) * s
        qs_w = jax.random.normal(ks[5], (CIN, G * K), dtype=jnp.float32) * s
        qw_w = jax.random.normal(ks[6], (CIN, G * K), dtype=jnp.float32) * s
        qw_b = jax.random.normal(ks[7], (G * K,), dtype=jnp.float32) * s
        out_w = jax.random.normal(ks[8], (G * C, CIN), dtype=jnp.float32) * s
        out_b = jax.random.normal(ks[9], (CIN,), dtype=jnp.float32) * s
        n = int(math.isqrt(K))
        d = np.linspace(-1.0, 1.0, n, dtype=np.float32)
        gx, gy = np.meshgrid(d, d, indexing='xy')
        prior = jnp.asarray(np.stack([gx, gy], axis=-1).reshape(1, 1, 1, 1, K, 2))
        sc = np.array([(i + 1) / G - 0.0001 for i in range(G)], dtype=np.float32)
        dscale = jnp.asarray(np.log(sc / (1.0 - sc)).reshape(1, 1, 1, G, 1, 1))
        return dict(x=x, v_w=v_w, v_b=v_b, qd_w=qd_w, qd_b=qd_b, qs_w=qs_w, qw_w=qw_w, qw_b=qw_b, out_w=out_w, out_b=out_b, prior=prior, dscale=dscale)
    _L0_conv_all = _L0_conv_setup()
    _L0_conv_in = {k: v for k, v in _L0_conv_all.items() if k in ('v_w', 'v_b', 'qd_w', 'qd_b', 'qs_w', 'qw_w', 'qw_b', 'out_w', 'out_b', 'prior', 'dscale')}
    del _L0_conv_all

    def _L1_attn_setup():
        import jax, jax.numpy as jnp
        import numpy as np
        HEADS, DIM_HEAD = (8, 32)
        BASE_TEMP, EPSILON = (0.5, 1e-06)
        key = jax.random.key(seed)
        ks = jax.random.split(key, 6)
        s = lambda k, sh, fan: jax.random.normal(k, sh, jnp.float32) * fan ** (-0.5)
        return {'x': jax.random.normal(ks[0], (2, 50000, 128), jnp.float32), 'W_x': s(ks[1], (256, 128), 128), 'b_x': jnp.zeros((256,), jnp.float32), 'W_slice': s(ks[2], (32, 32), 32), 'b_slice': jnp.zeros((32,), jnp.float32), 'W_temp': s(ks[3], (1, 32), 32), 'b_temp': jnp.zeros((1,), jnp.float32), 'W_out': s(ks[4], (128, 256), 256), 'b_out': jnp.zeros((128,), jnp.float32)}
    _L1_attn_all = _L1_attn_setup()
    _L1_attn_in = {k: v for k, v in _L1_attn_all.items() if k in ('W_x', 'b_x', 'W_slice', 'b_slice', 'W_temp', 'b_temp', 'W_out', 'b_out')}
    del _L1_attn_all

    def _L1_ffn_setup():
        import jax, jax.numpy as jnp
        import numpy as np
        TOP_K = 2
        LN_EPS = 1e-05
        key = jax.random.key(seed)
        ks = jax.random.split(key, 8)
        B, S, D, E, H = (16, 512, 128, 8, 512)
        x = jax.random.normal(ks[0], (B, S, D), dtype=jnp.float32)
        Wr = jax.random.normal(ks[1], (D, E), dtype=jnp.float32) * 0.1
        br = jnp.zeros((E,), dtype=jnp.float32)
        ln_g = jnp.ones((E, D), dtype=jnp.float32)
        ln_b = jnp.zeros((E, D), dtype=jnp.float32)
        W1 = jax.random.normal(ks[2], (E, D, H), dtype=jnp.float32) * (1.0 / np.sqrt(D))
        b1 = jnp.zeros((E, H), dtype=jnp.float32)
        W2 = jax.random.normal(ks[3], (E, H, D), dtype=jnp.float32) * (1.0 / np.sqrt(H))
        b2 = jnp.zeros((E, D), dtype=jnp.float32)
        return {'x': x, 'Wr': Wr, 'br': br, 'ln_g': ln_g, 'ln_b': ln_b, 'W1': W1, 'b1': b1, 'W2': W2, 'b2': b2}
    _L1_ffn_all = _L1_ffn_setup()
    _L1_ffn_in = {k: v for k, v in _L1_ffn_all.items() if k in ('Wr', 'br', 'ln_g', 'ln_b', 'W1', 'b1', 'W2', 'b2')}
    del _L1_ffn_all
    return {'x': x, 'L0_conv_v_w': _L0_conv_in['v_w'], 'L0_conv_v_b': _L0_conv_in['v_b'], 'L0_conv_qd_w': _L0_conv_in['qd_w'], 'L0_conv_qd_b': _L0_conv_in['qd_b'], 'L0_conv_qs_w': _L0_conv_in['qs_w'], 'L0_conv_qw_w': _L0_conv_in['qw_w'], 'L0_conv_qw_b': _L0_conv_in['qw_b'], 'L0_conv_out_w': _L0_conv_in['out_w'], 'L0_conv_out_b': _L0_conv_in['out_b'], 'L0_conv_prior': _L0_conv_in['prior'], 'L0_conv_dscale': _L0_conv_in['dscale'], 'L1_attn_W_x': _L1_attn_in['W_x'], 'L1_attn_b_x': _L1_attn_in['b_x'], 'L1_attn_W_slice': _L1_attn_in['W_slice'], 'L1_attn_b_slice': _L1_attn_in['b_slice'], 'L1_attn_W_temp': _L1_attn_in['W_temp'], 'L1_attn_b_temp': _L1_attn_in['b_temp'], 'L1_attn_W_out': _L1_attn_in['W_out'], 'L1_attn_b_out': _L1_attn_in['b_out'], 'L1_ffn_Wr': _L1_ffn_in['Wr'], 'L1_ffn_br': _L1_ffn_in['br'], 'L1_ffn_ln_g': _L1_ffn_in['ln_g'], 'L1_ffn_ln_b': _L1_ffn_in['ln_b'], 'L1_ffn_W1': _L1_ffn_in['W1'], 'L1_ffn_b1': _L1_ffn_in['b1'], 'L1_ffn_W2': _L1_ffn_in['W2'], 'L1_ffn_b2': _L1_ffn_in['b2']}

def reference(x, L0_conv_v_w, L0_conv_v_b, L0_conv_qd_w, L0_conv_qd_b, L0_conv_qs_w, L0_conv_qw_w, L0_conv_qw_b, L0_conv_out_w, L0_conv_out_b, L0_conv_prior, L0_conv_dscale, L1_attn_W_x, L1_attn_b_x, L1_attn_W_slice, L1_attn_b_slice, L1_attn_W_temp, L1_attn_b_temp, L1_attn_W_out, L1_attn_b_out, L1_ffn_Wr, L1_ffn_br, L1_ffn_ln_g, L1_ffn_ln_b, L1_ffn_W1, L1_ffn_b1, L1_ffn_W2, L1_ffn_b2):
    import jax
    import jax.numpy as jnp

    def _L0_conv_ref(x, v_w, v_b, qd_w, qd_b, qs_w, qw_w, qw_b, out_w, out_b, prior, dscale):
        import jax, jax.numpy as jnp
        import numpy as np
        import math
        B, H, W, CIN = (4, 32, 32, 128)
        G, C, K = (8, 32, 9)
        MAX_SCALE = 6.0

        def _dcn_sample(v, deform, weights):
            b_, h_, w_, g_, c_ = v.shape
            ww = jnp.arange(w_, dtype=v.dtype)[None, None, :, None, None]
            hh = jnp.arange(h_, dtype=v.dtype)[None, :, None, None, None]
            px = ww + deform[..., 0]
            py = hh + deform[..., 1]
            x0 = jnp.floor(px)
            y0 = jnp.floor(py)
            wx1 = px - x0
            wx0 = 1.0 - wx1
            wy1 = py - y0
            wy0 = 1.0 - wy1
            bidx = jnp.arange(b_)[:, None, None, None, None]
            gidx = jnp.arange(g_)[None, None, None, :, None]

            def gather(yi, xi):
                valid = ((yi >= 0) & (yi < h_) & (xi >= 0) & (xi < w_)).astype(v.dtype)
                yc = jnp.clip(yi, 0, h_ - 1).astype(jnp.int32)
                xc = jnp.clip(xi, 0, w_ - 1).astype(jnp.int32)
                return v[bidx, yc, xc, gidx] * valid[..., None]
            samp = gather(y0, x0) * (wy0 * wx0)[..., None] + gather(y0, x0 + 1) * (wy0 * wx1)[..., None] + gather(y0 + 1, x0) * (wy1 * wx0)[..., None] + gather(y0 + 1, x0 + 1) * (wy1 * wx1)[..., None]
            return jnp.einsum('bhwgkc,bhwgk->bhwgc', samp, weights)
        b_, h_, w_, _ = x.shape
        v = (x @ v_w + v_b).reshape(b_, h_, w_, G, C)
        deform = (x @ qd_w + qd_b).reshape(b_, h_, w_, G, K, 2)
        scale = (x @ qs_w).reshape(b_, h_, w_, G, K, 1) + dscale
        deform = (deform + prior) * jax.nn.sigmoid(scale) * MAX_SCALE
        weights = (x @ qw_w + qw_b).reshape(b_, h_, w_, G, K)
        out = _dcn_sample(v, deform, weights)
        out = out.reshape(b_, h_, w_, G * C)
        return out @ out_w + out_b

    def _L1_attn_ref(x, W_x, b_x, W_slice, b_slice, W_temp, b_temp, W_out, b_out):
        import jax, jax.numpy as jnp
        import numpy as np
        HEADS, DIM_HEAD = (8, 32)
        BASE_TEMP, EPSILON = (0.5, 1e-06)
        B, N, C = x.shape
        H, D = (HEADS, DIM_HEAD)
        x_proj = (x @ W_x.T + b_x).reshape(B, N, H, D).transpose(0, 2, 1, 3)
        adaptive_temp = BASE_TEMP + jnp.clip(x_proj @ W_temp.T + b_temp, -0.4, 0.4)
        log_neg_log_eps = jnp.log(-jnp.log(jnp.float32(EPSILON)))
        slice_logits = x_proj @ W_slice.T + b_slice - log_neg_log_eps
        slice_weights = jax.nn.softmax(slice_logits / adaptive_temp, axis=2)
        slice_norm = slice_weights.sum(axis=2)
        eidetic = jnp.einsum('bhnc,bhng->bhgc', x_proj, slice_weights)
        eidetic = eidetic / (slice_norm + 1e-05)[..., None]
        processed = eidetic
        out_x = jnp.einsum('bhgc,bhng->bhnc', processed, slice_weights)
        out_x = out_x.transpose(0, 2, 1, 3).reshape(B, N, H * D)
        return out_x @ W_out.T + b_out

    def _L1_ffn_ref(x, Wr, br, ln_g, ln_b, W1, b1, W2, b2):
        import jax, jax.numpy as jnp
        import numpy as np
        TOP_K = 2
        LN_EPS = 1e-05
        B, S, D = x.shape
        N = B * S
        xt = x.reshape(N, D)
        logits = xt @ Wr + br
        probs = jax.nn.softmax(logits, axis=-1)
        top_p, top_idx = jax.lax.top_k(probs, TOP_K)
        weights = top_p / top_p.sum(axis=-1, keepdims=True)
        mu = xt.mean(axis=-1, keepdims=True)
        var = ((xt - mu) ** 2).mean(axis=-1, keepdims=True)
        xn = (xt - mu) * jax.lax.rsqrt(var + LN_EPS)
        xe = xn[None, :, :] * ln_g[:, None, :] + ln_b[:, None, :]
        h = jax.nn.gelu(jnp.einsum('end,edh->enh', xe, W1) + b1[:, None, :], approximate=False)
        y = jnp.einsum('enh,ehd->end', h, W2) + b2[:, None, :]
        y_tok = jnp.transpose(y, (1, 0, 2))
        sel = jnp.take_along_axis(y_tok, top_idx[:, :, None], axis=1)
        out = (weights[:, :, None] * sel).sum(axis=1)
        return out.reshape(B, S, D)

    def _gn(v, G=32, eps=1e-05):
        B_, H_, W_, C_ = v.shape
        g = v.reshape(B_, H_, W_, G, C_ // G)
        m = jnp.mean(g, axis=(1, 2, 4), keepdims=True)
        s = jnp.var(g, axis=(1, 2, 4), keepdims=True)
        return ((g - m) / jnp.sqrt(s + eps)).reshape(v.shape)

    def _ln_c(v, eps=1e-06):
        m = jnp.mean(v, axis=-1, keepdims=True)
        s = jnp.var(v, axis=-1, keepdims=True)
        return (v - m) / jnp.sqrt(s + eps)

    def _ln_t(v, eps=1e-05):
        m = jnp.mean(v, axis=-1, keepdims=True)
        s = jnp.var(v, axis=-1, keepdims=True)
        return (v - m) / jnp.sqrt(s + eps)

    def _to_tokens(v):
        B_, H_, W_, C_ = v.shape
        return v.reshape(B_, H_ * W_, C_)

    def _from_tokens(t, like):
        return t.reshape(like.shape)
    x = x + _L0_conv_ref(_gn(x), L0_conv_v_w, L0_conv_v_b, L0_conv_qd_w, L0_conv_qd_b, L0_conv_qs_w, L0_conv_qw_w, L0_conv_qw_b, L0_conv_out_w, L0_conv_out_b, L0_conv_prior, L0_conv_dscale)
    t = _to_tokens(x)
    t = t + _L1_attn_ref(_ln_t(t), L1_attn_W_x, L1_attn_b_x, L1_attn_W_slice, L1_attn_b_slice, L1_attn_W_temp, L1_attn_b_temp, L1_attn_W_out, L1_attn_b_out)
    t = t + _L1_ffn_ref(_ln_t(t), L1_ffn_Wr, L1_ffn_br, L1_ffn_ln_g, L1_ffn_ln_b, L1_ffn_W1, L1_ffn_b1, L1_ffn_W2, L1_ffn_b2)
    x = _from_tokens(t, x)
    return x

_drawn_inputs = setup_inputs


def setup_inputs(seed=0):
    import zlib

    import numpy as np

    out = dict(_drawn_inputs(seed))
    spreads = {'L1_attn_b_x': (0.0, 0.1),
     'L1_attn_b_slice': (0.0, 0.268),
     'L1_attn_b_out': (0.0, 0.1),
     'L1_ffn_br': (0.0, 0.1),
     'L1_ffn_ln_g': (1.0, 0.2),
     'L1_ffn_ln_b': (0.0, 0.1),
     'L1_ffn_b1': (0.0, 0.1),
     'L1_ffn_b2': (0.0, 0.1)}
    factors = {'L0_conv_v_b': 3.277, 'L0_conv_qw_b': 3.586, 'L0_conv_qd_b': 2.731}
    for name, (base, spread) in spreads.items():
        noise = np.random.default_rng([zlib.crc32(name.encode()), seed]).standard_normal(out[name].shape)
        drawn = base * np.exp(spread * noise) if base else spread * noise
        out[name] = jnp.asarray(drawn.astype(out[name].dtype))
    for name, factor in factors.items():
        out[name] = (out[name] * factor).astype(out[name].dtype)
    return out
```

```python
from contextlib import ExitStack
from collections import namedtuple

import concourse.bass as bass
from concourse import mybir

F32 = mybir.dt.float32
BF16 = mybir.dt.bfloat16
I32 = mybir.dt.int32
U32 = mybir.dt.uint32
ALU = mybir.AluOpType
ACT = mybir.ActivationFunctionType
AX = mybir.AxisListType.X

P = 128
B, HH, WW, C = 4, 32, 32, 128
N = HH * WW
NT = N // P
TILES = B * NT
ROWS = P // WW
GALL, GC, K = 8, 32, 9
G = 6
ND = GALL - G
GK = G * K
RC_ = G * GC
SETS = 64
NI, NA = 4, 2
TOK = NI * NA
R = TOK * K
STEP = NT // (2 * ND)
EARLY = min(B - 1, NT - 2 * ND)
BIG = 64.0
HALF = N // 2
PW = WW + 1
PITCH = WW + 2
PATCHES = PW * PITCH
PROWS = 3
VT = PW // PROWS
VM = PROWS * PITCH
PAD = (HH + 2) * PITCH + 2
VALL = 2 * VT
MAX_SCALE = 6.0
GN_GROUP = 4
HG, S, DH = 4, 32, 32
LOG_NEG_LOG_EPS = 2.625792
EPS = 1e-5
E, HID = 8, 512
HJ = HID // P
EJ = E * HJ
ROW_MATH = 7
POOL_CONSTS = 22
SCRATCH_SPENT = POOL_CONSTS + 8
DENSE_CONSTS = POOL_CONSTS + 13
MATH = 16

EVENTS = """
constants_made small_constants conv_weights_loaded weights_loaded x_loaded x_tok_loaded
bias_parts weights_turned slice_turned ffn_turned ffn_bias_summed turned_copied ln_cols_copied setup_done
x_transposed channel_stats group_mean spread group_var group_std gn_chain normalised padded
offsets_summed offsets_copied sigmoid_done math patches_summed patches_copied
patch_rows_even patch_rows_odd xnorm_stored values_stored
dense_consts quarters_copied row_bias_summed row_bias_copied
idx_ready products reduced red_turned redT_copied conv_summed conv_added
ln_chain ln_stats ln_std ln_recip tile_normalised
xb_loaded values_loaded rows_summed row_sigmoid row_math parts_made parts_turned parts_copied
dx_summed x_chain x_taken x_ready dy_summed y_chain y_ready a_summed a_taken dense_out spread_made
dense_summed dense_added
tn_turned tnT_copied xpT_summed xpT_copied xp_summed xp_copied logits_summed temp_chain logits_done
max_done exp_done scale_chain scale_done e_turned e_copied slice_sums bdE_done M_summed M_copied attn_out
attn_added bout_added out_bias_added
en_chain en_stats1 en_std1 en_stats2 en_std2 en_ready
own_wait
rows_stored
"""
FFN_EVENTS = """
xt_chain xn_chain turned turned_copied router_summed router_chain exp_ready gate_chain
gate_done gate_turned gateT_copied b2_summed b2_added hidden_summed hidden_ready expert_summed expert_added
"""


def conv_attn_moe(nc, t_in, out):
    x_d = t_in["x"].rearrange("b h w c -> (b h w) c").rearrange("(b t p) c -> b p t c", t=NT, p=P)
    out_d = out.rearrange("b h w c -> (b h w) c").rearrange("(n p) c -> n p c", p=P)

    with ExitStack() as ctx:
        def sb(name, shape, dt=F32):
            return ctx.enter_context(nc.sbuf_tensor(name, shape, dt))

        def sem(name):
            return ctx.enter_context(nc.semaphore(name))

        s = namedtuple("Events", EVENTS.split())(*[sem(n) for n in EVENTS.split()])
        gathered = [sem(f"gathered_group_{g}") for g in range(G)]
        ffn_events = namedtuple("ExpertEvents", FFN_EVENTS.split())
        mid = ffn_events(*[sem(n + "_mid") for n in FFN_EVENTS.split()])
        end = ffn_events(*[sem(n + "_end") for n in FFN_EVENTS.split()])

        tables = [nc.dram_tensor(f"patch_table_{b}", [PATCHES * G, 4 * GC], F32, kind="Internal").ap()
                  for b in range(B)]
        xn_dram = nc.dram_tensor("normalised_images", [B, C, N], F32, kind="Internal").ap()
        values_dram = nc.dram_tensor("dense_values", [B, N, ND * GC], F32, kind="Internal").ap()

        ident = sb("ident", [P, P])
        gn_avg = sb("gn_avg", [P, P])
        head_mask = sb("head_mask", [P, P])
        vw = sb("vw", [C, RC_])
        vb_rows = sb("vb_rows", [96, RC_], BF16)
        inside = sb("inside", [96, PAD], BF16)
        wq = sb("wq", [C, 4 * GK + ND * GC])
        qbias_off = sb("qbias_off", [P, G, K, 2])
        prior_b = sb("prior_b", [P, K, 2])
        dscale_b = sb("dscale_b", [P, G])
        qbias_rest = sb("qbias_rest", [P, 2, G, K])
        outw_a = sb("outw_a", [P, C])
        outw_b = sb("outw_b", [RC_ - P, C])
        outw_d = sb("outw_d", [P, ND, C])
        vbias_d = sb("vbias_d", [P, ND * GC])
        outb_b = sb("outb_b", [P, C])
        boutb_b = sb("boutb_b", [P, C])
        bx_b = sb("bx_b", [P, 256])
        bx_col = sb("bx_col", [P, 2])
        bslice_raw = sb("bslice_raw", [P, 1])
        bslice_col = sb("bslice_col", [P, 1])
        btemp_col = sb("btemp_col", [P, 1])
        wxT = sb("wxT", [C, 256])
        woutT = sb("woutT", [P, 2, C])
        ws_bd = sb("ws_bd", [P, P])
        wt_col = sb("wt_col", [P, 1])
        wt_bd = sb("wt_bd", [P, P])
        wr = sb("wr", [C, E])
        br_b = sb("br_b", [P, E])
        lngT = sb("lngT", [C, E])
        lnbT = sb("lnbT", [C, E])
        w1 = sb("w1", [C, E, HID])
        b1_turned = sb("b1_turned", [P, EJ])
        b1_col = sb("b1_col", [P, EJ])
        w2 = sb("w2", [P, EJ, C])
        b2 = sb("b2", [E, C])
        eps_col = sb("eps_col", [P, 1])
        ofs_i = sb("ofs_i", [P, GK], I32)
        ofs = sb("ofs", [P, GK])
        pos_i = sb("pos_i", [P, NT, 2], I32)
        pos_b = sb("pos_b", [P, NT, 2], I32)
        pos = sb("pos", [P, NT, 2])
        expert_i = sb("expert_i", [P, E], I32)
        expert_no = sb("expert_no", [P, E])

        x_tok = sb("x_tok", [P, TILES, C])
        idx_all = sb("idx_all", [P, TILES + 1, GK], I32)
        w4_all = sb("w4_all", [P, TILES, GK * 4])
        idx_now = sb("idx_now", [P, GK], I32)
        ring = sb("ring", [P, G, K * 4 * GC])
        red = sb("red", [P, RC_])
        redT = sb("redT", [P, 2, P])

        ident_bf = sb("ident_bf", [P, P], BF16)
        zw = sb("zw", [C, ND, 4, 2 * (R - K) + K])
        row_bias = sb("row_bias", [R, ND, 4])
        rep9 = sb("rep9", [K, TOK, K])
        bias9 = sb("bias9", [K, ND, 4])
        prior9 = sb("prior9", [K, 2])
        dscale9 = sb("dscale9", [K, ND])
        r7_i = sb("r7_i", [R, TOK - 1], I32)
        r7 = sb("r7", [R, TOK - 1])
        blk = sb("blk", [R, 1])
        blk_i = sb("blk_i", [R, 3], I32)
        blk_f = sb("blk_f", [R, 2])
        rpos = sb("rpos", [R, 2, 2 * SETS])
        QYW, QXW = 32, 32
        QY = sb("QY", [R, SETS // 4, QYW], BF16)
        QX = sb("QX", [R, SETS // 8, QXW], BF16)
        L = sb("L", [P, 6, R], BF16)
        EY = sb("EY", [P, 512], BF16)
        EX = sb("EX", [P, 512], BF16)
        quad = sb("quad", [P, NI])
        vbd = sb("vbd", [P, WW, P])

        REGION = 11776
        region = sb("region", [P, REGION])
        at = [0]

        def part(n):
            at[0] += n
            assert at[0] <= REGION, at[0]
            return region[:, at[0] - n:at[0]]

        xin = part(NT * C).rearrange("p (t c) -> p t c", t=NT)
        xpad = part(PAD)
        xnorm = part(N)
        vd_sb = part(NT * ND * GC).rearrange("p (t m) -> p t m", t=NT)
        vrows = part(2 * 4 * G * GC).rearrange("p (r g d c) -> p r g d c", r=2, g=G, d=4)
        q_off = part(NT * GK * 2)
        q_rest = part(2 * NT * GK).rearrange("p (s t m) -> p s t m", s=2, t=NT)
        sig = part(NT * GK)
        pxy = part(NT * GK * 2)
        p_i = part(NT * GK * 2).bitcast(I32)
        p_f = part(NT * GK * 2)
        p_w1 = part(NT * GK * 2)
        p_w0 = q_off
        at[0] = 0
        tn_tok = part(NT * C).rearrange("p (t c) -> p t c", t=NT)
        tnT = part(N)
        xpT = part(2 * N).rearrange("p (h n) -> p h n", h=2)
        xp_tok = part(NT * 256).rearrange("p (t c) -> p t c", t=NT)
        eT = part(2 * N).rearrange("p (h n) -> p h n", h=2)
        e_tok = part(NT * 256).rearrange("p (t c) -> p t c", t=NT)
        temp_sb = part(512)
        rtemp = part(512)
        bdE = part(2 * P).rearrange("p (h n) -> p h n", h=2)
        Msb = part(2 * P).rearrange("p (h n) -> p h n", h=2)
        def expert_arrays(n, ntok):
            return dict(
                xt=part(n * C).rearrange("p (t c) -> p t c", t=n), xn=part(n * C).rearrange("p (t c) -> p t c", t=n),
                xtT=part(n * P), xnT=part(n * P), hT=part(2 * HJ * ntok).rearrange("p (r j n) -> p r j n", r=2, j=HJ),
                gateT=part(n * P)[0:E, :])

        at[0] = 0
        end_arrays = expert_arrays(NT, 512)
        at[0] = 0
        tile = expert_arrays(1, P)
        xb = part(N)
        asb = part(WW * SETS * NA).rearrange("p (q n) -> p q n", q=WW)
        ysb = part(4 * 512).rearrange("p (r s n) -> p r s n", r=4, s=4)[0:R]
        xsb = part(2 * 512).rearrange("p (r s n) -> p r s n", r=2, s=8)[0:R]
        osp = part(HALF)
        r_off = part(2 * SETS).rearrange("p (d s) -> p d s", d=2)[0:R]
        r_pos = part(2 * SETS).rearrange("p (d s) -> p d s", d=2)[0:R]
        r_sig = part(SETS)[0:R]
        r_w = part(SETS)[0:R]
        stage = sb("stage", [P, 10 * P])
        wx_raw = stage[:, 0:2 * P].rearrange("p (h c) -> p h c", h=2)
        wout_raw = stage[:, 2 * P:4 * P]
        ws_raw = stage[:, 4 * P:5 * P]
        lng = stage[0:E, 5 * P:6 * P]
        lnb = stage[0:E, 6 * P:7 * P]
        b1_raw = stage[0:EJ, 7 * P:8 * P]
        wqd_raw = stage[:, 8 * P:8 * P + 4 * ND * K]
        vb = ring[0:96, 0, 0:RC_]
        vb_parts = ring[0:96, 1, 0:3 * RC_ // 2].bitcast(BF16).rearrange("p (a c) -> p a c", a=3)
        ey_i = ring[0:32, 2, 0:512].bitcast(I32)
        ey_f = ring[0:32, 3, 0:512]
        ex_f = ring[0:32, 3, 512:1024]
        npos_i = ring[0:R, 4, 0:2 * SETS].bitcast(I32)
        npos_b = ring[0:R, 4, 2 * SETS:6 * SETS].bitcast(I32).rearrange("p (d s) -> p d s", d=2)

        gn_stats = sb("gn_stats", [P, 2, 6])
        gn_mv = sb("gn_mv", [P, 2])
        gn_diff = sb("gn_diff", [P, 1])
        gn_mean = sb("gn_mean", [P, 1])
        gn_spread = sb("gn_spread", [P, 1])
        gn_std = sb("gn_std", [P, 1])
        gn_r = sb("gn_r", [P, 1])
        f_stats = sb("f_stats", [P, NT, 6])
        f_mv = sb("f_mv", [P, NT, 2])
        f_sd = sb("f_sd", [P, NT])
        f_r = sb("f_r", [P, NT])
        norms = sb("norms", [P, NT, 4])
        norms_now = sb("norms_now", [P, 4])
        a_max = sb("a_max", [P, 2])
        a_nmax = sb("a_nmax", [P, 2])
        a_sum = sb("a_sum", [P, 2])
        a_rs = sb("a_rs", [P, 2])
        a_norm = sb("a_norm", [P, 2])
        a_rn = sb("a_rn", [P, 2])
        a_sc = sb("a_sc", [P, 2])
        gate = sb("gate", [P, NT, E])
        gate2 = sb("gate2", [P, NT, E])
        rl = sb("rl", [P, NT, E])
        top_v = sb("top_v", [P, NT, 8])
        top_i = sb("top_i", [P, NT, 8], U32)
        top_f = sb("top_f", [P, NT, 2])
        g_d = sb("g_d", [P, NT])
        g_e = sb("g_e", [P, NT])
        g_den = sb("g_den", [P, NT])
        g_w1 = sb("g_w1", [P, NT])
        g_w2 = sb("g_w2", [P, NT])

        ps = ctx.enter_context(nc.psum_tensor("ps", [P, 8, 512], F32))
        ps_y = ps[:, 2, 0:C]
        TILE_BANK, UP_BANKS = 2, (1, 3)
        Y_BANKS, X_BANK, A_BANKS, OUT_BANK, SUM_BANK = (6, 7), 5, (3, 0), 4, 5
        Y_BANK = [7, 4]

        def pcol(bank, t):
            return ps[:, bank + t // 4, (t % 4) * P:(t % 4 + 1) * P]

        def interior(a):
            return a[:, PITCH:(HH + 1) * PITCH].rearrange("p (h w) -> p h w", w=PITCH)[:, :, 1:WW + 1]

        def tok(T, n=1):
            return x_tok[:, bass.ds(T, n), :]

        def own_wait(eng):
            eng.sem_inc(s.own_wait, 1)

        def tables_stored(eng):
            eng.wait_ge(s.patch_rows_even, 16 * B * ((VT + 1) // 2))
            eng.wait_ge(s.patch_rows_odd, 16 * B * (VT // 2))

        block = ctx.enter_context(nc.Block())
        loads = {"conv": 0, "rest": 0}

        @block.sync
        def _(sp):
            def load(dst, src, which="rest"):
                loads[which] += 1
                sp.dma_start(dst, src).then_inc(s.weights_loaded if which == "rest" else s.conv_weights_loaded, 16)

            def bc(ap, n, rows=P):
                return ap.rearrange("(o n) -> o n", o=1).broadcast_to([rows, n])

            def store_patches(b):
                for v in range(VT):
                    sp.wait_ge(s.patches_copied, VALL * b + 2 * v + 2)
                    sp.dma_start(tables[b].rearrange("(n g) d -> n (g d)", g=G)[v * VM:(v + 1) * VM, :],
                                 vrows[0:VM, v % 2, :, :, :].rearrange("p g d c -> p (g d c)"))\
                      .then_inc(s.patch_rows_odd if v % 2 else s.patch_rows_even, 16)

            def groups(ap, a, b, per):
                return ap[:, a * per:b * per]

            sp.dma_start(xin, x_d[0]).then_inc(s.x_loaded, 16)
            load(wq[:, 0:2 * GK], groups(t_in["L0_conv_qd_w"], 0, G, 2 * K), "conv")
            load(wq[:, 2 * GK:3 * GK], groups(t_in["L0_conv_qs_w"], 0, G, K), "conv")
            load(wq[:, 3 * GK:4 * GK], groups(t_in["L0_conv_qw_w"], 0, G, K), "conv")
            load(wq[:, 4 * GK:4 * GK + ND * GC], groups(t_in["L0_conv_v_w"], G, GALL, GC), "conv")
            load(vw[:, :], groups(t_in["L0_conv_v_w"], 0, G, GC), "conv")
            load(vb, bc(t_in["L0_conv_v_b"][0:RC_], RC_, 96), "conv")
            load(vbias_d[:, :], bc(t_in["L0_conv_v_b"][RC_:], ND * GC), "conv")
            load(qbias_off[:, :, :, :].rearrange("p g k d -> p (g k d)"), bc(t_in["L0_conv_qd_b"][0:2 * GK], 2 * GK),
                 "conv")
            load(prior_b[:, :, :].rearrange("p k d -> p (k d)"),
                 bc(t_in["L0_conv_prior"].rearrange("a b c d k x -> (a b c d k x)"), 2 * K), "conv")
            dscale = t_in["L0_conv_dscale"].rearrange("a b c g k x -> (a b c g k x)")
            load(dscale_b[:, :], bc(dscale[0:G], G), "conv")
            load(qbias_rest[:, 1, :, :].rearrange("p g k -> p (g k)"), bc(t_in["L0_conv_qw_b"][0:GK], GK), "conv")
            load(outb_b[:, :], bc(t_in["L0_conv_out_b"], C), "conv")
            load(wqd_raw[:, 0:2 * ND * K], groups(t_in["L0_conv_qd_w"], G, GALL, 2 * K))
            load(wqd_raw[:, 2 * ND * K:3 * ND * K], groups(t_in["L0_conv_qs_w"], G, GALL, K))
            load(wqd_raw[:, 3 * ND * K:4 * ND * K], groups(t_in["L0_conv_qw_w"], G, GALL, K))
            with nc.allow_non_contiguous_dma(reason="biases of the dense groups, a hundred numbers"):
                for g in range(ND):
                    load(bias9[:, g, 0:2],
                         t_in["L0_conv_qd_b"][(G + g) * 2 * K:(G + g + 1) * 2 * K].rearrange("(k d) -> k d", d=2))
                    load(bias9[:, g, 3:4], t_in["L0_conv_qw_b"][(G + g) * K:(G + g + 1) * K]
                         .rearrange("(k o) -> k o", o=1))
                load(prior9[:, :], t_in["L0_conv_prior"].rearrange("a b c d k x -> (a b c d k) x"))
                load(dscale9[:, :], bc(dscale[G:GALL], ND, K))
            load(outw_a[:, :], t_in["L0_conv_out_w"][0:P, :])
            load(outw_b[:, :], t_in["L0_conv_out_w"][P:RC_, :])
            for d in range(NI):
                load(outw_d[d * GC:(d + 1) * GC, :, :],
                     t_in["L0_conv_out_w"][RC_:, :].rearrange("(g c) o -> c g o", g=ND))
            for b in range(B):
                sp.dma_start(x_tok[:, b * NT:(b + 1) * NT, :], x_d[b]).then_inc(s.x_tok_loaded, 16)

            def load_attention_and_experts():
                load(boutb_b[:, :], bc(t_in["L1_attn_b_out"], C))
                load(bx_b[:, :], bc(t_in["L1_attn_b_x"], 256))
                with nc.allow_non_contiguous_dma(reason="bias columns of a few hundred numbers"):
                    load(bx_col[:, :], t_in["L1_attn_b_x"].rearrange("(h p) -> p h", p=P))
                    for h in range(HG):
                        load(bslice_raw[h * S:(h + 1) * S, :], t_in["L1_attn_b_slice"].rearrange("(p o) -> p o", o=1))
                        load(wt_col[h * S:(h + 1) * S, :], t_in["L1_attn_W_temp"].rearrange("o p -> p o"))
                load(btemp_col[:, :], bc(t_in["L1_attn_b_temp"], 1))
                load(wx_raw, t_in["L1_attn_W_x"].rearrange("(h p) c -> p h c", p=P))
                load(wout_raw, t_in["L1_attn_W_out"])
                for h in range(HG):
                    load(ws_raw[h * S:(h + 1) * S, :].rearrange("p (j d) -> p j d", j=HG),
                         t_in["L1_attn_W_slice"].rearrange("g (o d) -> g o d", o=1).broadcast_to([S, HG, DH]))
                load(wr[:, :], t_in["L1_ffn_Wr"])
                load(br_b[:, :], bc(t_in["L1_ffn_br"], E))
                load(lng, t_in["L1_ffn_ln_g"])
                load(lnb, t_in["L1_ffn_ln_b"])
                load(w1[:, :, :], t_in["L1_ffn_W1"].rearrange("e d h -> d e h"))
                load(b1_raw, t_in["L1_ffn_b1"].rearrange("e (j p) -> (e j) p", p=P))
                load(w2[:, :, :], t_in["L1_ffn_W2"].rearrange("e (j p) d -> p (e j) d", p=P))
                load(b2[:, :], t_in["L1_ffn_b2"])

            sp.wait_ge(s.dense_consts, SCRATCH_SPENT)
            for q in range(1, 4):
                sp.dma_start(EY[32 * q:32 * q + 32, :], EY[0:32, :]).then_inc(s.quarters_copied, 16)
                sp.dma_start(EX[32 * q:32 * q + 32, :], EX[0:32, :]).then_inc(s.quarters_copied, 16)

            for b in range(B):
                if b < B - 1:
                    sp.wait_ge(s.x_transposed, b + 1)
                    sp.dma_start(xin, x_d[b + 1]).then_inc(s.x_loaded, 16)
                sp.wait_ge(s.normalised, b + 1)
                sp.dma_start(xn_dram[b], xnorm).then_inc(s.xnorm_stored, 16)
                sp.wait_ge(s.offsets_copied, NT * (b + 1))
                sp.dma_start(values_dram[b].rearrange("(t p) m -> p t m", p=P), vd_sb).then_inc(s.values_stored, 16)
                store_patches(b)
                if b == 0:
                    load_attention_and_experts()

            def load_dense(b):
                first = isinstance(b, int)
                sp.dma_start(xb, xn_dram[bass.ds(b, 1)].rearrange("o c n -> (o c) n")).then_inc(s.xb_loaded, 16)
                for g in range(ND):
                    if g or not first:
                        sp.wait_ge(s.dense_out, 2 * (ND * b + g))
                    v = values_dram[bass.ds(b, 1)].rearrange("o (y x) (g c) -> (o y) x g c", x=WW, g=ND)[:, :, g, :]
                    for i in range(NI):
                        sp.dma_start(vbd[i * GC:(i + 1) * GC, :, i * GC:(i + 1) * GC], v).then_inc(s.values_loaded, 16)

            sp.wait_ge(s.xnorm_stored, 16 * B)
            sp.wait_ge(s.values_stored, 16 * B)
            sp.wait_ge(s.patches_copied, VALL * B)
            tables_stored(sp)
            sp.wait_ge(s.dense_consts, DENSE_CONSTS)
            load_dense(0)
            with sp.Fori(1, B) as b:
                sp.wait_ge(s.attn_added, b)
                load_dense(b)
                sp.wait_ge(mid.expert_added, E * NT * b)
                sp.dma_start(out_d[bass.ds(b * NT - NT, NT), :, :].rearrange("n p c -> p n c"),
                             tok(b * NT - NT, NT)).then_inc(s.rows_stored, 16)
            for h in range(2):
                T0 = TILES - NT + 4 * h
                sp.wait_ge(end.expert_added, (h + 1) * E * 4)
                sp.dma_start(out_d[T0:T0 + 4, :, :].rearrange("n p c -> p n c"),
                             x_tok[:, T0:T0 + 4, :]).then_inc(s.rows_stored, 16)
            sp.wait_ge(s.rows_stored, 16 * (B - 1 + 2))

        @block.gpsimd
        def _(pl):
            pl.memset(xpad, 0.0).then_inc(s.constants_made, 1)
            pl.memset(ident[:, :], 0.0).then_inc(s.constants_made, 1)
            pl.memset(gn_avg[:, :], 1.0 / GN_GROUP).then_inc(s.constants_made, 1)
            pl.memset(head_mask[:, :], 1.0).then_inc(s.constants_made, 1)
            pl.memset(inside[:, :], 0.0).then_inc(s.constants_made, 1)
            pl.iota(ofs_i[:, :].rearrange("p (g k) -> p g k", g=G), pattern=[[1, G], [0, K]],
                    base=(PITCH + 1) * G, channel_multiplier=0).then_inc(s.constants_made, 1)
            pl.iota(pos_i[:, :, :], pattern=[[P, NT], [0, 2]], base=0, channel_multiplier=1)\
              .then_inc(s.constants_made, 1)
            pl.iota(expert_i[:, :], pattern=[[1, E]], base=0, channel_multiplier=0).then_inc(s.constants_made, 1)
            pl.wait_ge(s.constants_made, 8)
            pl.memset(interior(inside), 1.0).then_inc(s.constants_made, 1)
            pl.affine_select(out=ident[:, :], in_=ident[:, :], compare_op=ALU.not_equal, fill=1.0, base=0,
                             pattern=[[-1, P]], channel_multiplier=1).then_inc(s.constants_made, 1)

            def block_diagonal(m, size, done):
                v = m[:, :].rearrange("p (a c) -> p a c", c=size)
                pl.affine_select(out=v, in_=v, compare_op=ALU.is_ge, fill=0.0, base=0,
                                 pattern=[[-size, P // size], [0, size]], channel_multiplier=1)\
                  .then_inc(s.constants_made, 1)
                pl.wait_ge(s.constants_made, done + 1)
                pl.affine_select(out=v, in_=v, compare_op=ALU.is_ge, fill=0.0, base=size - 1,
                                 pattern=[[size, P // size], [0, size]], channel_multiplier=-1)\
                  .then_inc(s.constants_made, 1)

            block_diagonal(gn_avg, GN_GROUP, 10)
            block_diagonal(head_mask, DH, 12)

            pl.memset(zw[:, :, :, :], 0.0).then_inc(s.dense_consts, 1)
            pl.memset(vbd[:, :, :], 0.0).then_inc(s.dense_consts, 1)
            pl.memset(QY[:, :, :], 0.0).then_inc(s.dense_consts, 1)
            pl.memset(QX[:, :, :], 0.0).then_inc(s.dense_consts, 1)
            pl.memset(quad[:, :], 1.0).then_inc(s.dense_consts, 1)
            pl.iota(r7_i[:, :], pattern=[[-K, TOK - 1]], base=-K, channel_multiplier=1).then_inc(s.dense_consts, 1)
            pl.iota(npos_i, pattern=[[TOK, 2 * SETS]], base=0, channel_multiplier=0).then_inc(s.dense_consts, 1)
            pl.iota(ey_i.rearrange("p (m q) -> p m q", q=HH), pattern=[[0, 16], [-1, HH]], base=-int(BIG),
                    channel_multiplier=0).then_inc(s.dense_consts, 1)
            pl.wait_ge(s.dense_consts, 8)
            pl.tensor_copy(ey_f, ey_i).then_inc(s.dense_consts, 1)
            pl.tensor_copy(ex_f, ey_i).then_inc(s.dense_consts, 1)
            pl.affine_select(out=quad[:, :], in_=quad[:, :], compare_op=ALU.is_ge, fill=0.0, base=0,
                             pattern=[[-GC, NI]], channel_multiplier=1).then_inc(s.dense_consts, 1)
            pl.wait_ge(s.dense_consts, 11)
            pl.affine_select(out=quad[:, :], in_=quad[:, :], compare_op=ALU.is_ge, fill=0.0, base=GC - 1,
                             pattern=[[GC, NI]], channel_multiplier=-1).then_inc(s.dense_consts, 1)
            done = 12
            pl.wait_ge(s.dense_consts, done)
            for e, sets, blocks in ((ey_f, 4, NI), (ex_f, 8, NA)):
                steps = [(ALU.is_equal, 0.0, -3 * sets, [[0, sets], [0, blocks], [0, HH]])]
                steps += [(ALU.not_equal, 1.0, -m * sets, [[-1, sets], [0, blocks], [0, HH]]) for m in range(3)]
                steps += [(ALU.not_equal, BIG, -3 * sets - 1, [[0, sets], [-1, blocks], [0, HH]])]
                for op, fill, base, pattern in steps:
                    v = e.rearrange("p (s b c) -> p s b c", s=sets, b=blocks)
                    pl.affine_select(out=v, in_=v, compare_op=op, fill=fill, base=base, pattern=pattern,
                                     channel_multiplier=1).then_inc(s.dense_consts, 1)
                    done += 1
                    pl.wait_ge(s.dense_consts, done)
            assert done == POOL_CONSTS

            pl.wait_ge(s.dense_consts, SCRATCH_SPENT)
            pl.wait_ge(s.bias_parts, 8)
            for b in range(B):
                pl.wait_ge(s.patch_rows_even, 16 * (VT + 1) // 2 * (b + 1))
                pl.wait_ge(s.patch_rows_odd, 16 * (VT // 2) * (b + 1))
                with pl.Fori(0, NT) as t:
                    for g in range(G):
                        pl.wait_ge(s.idx_ready, G * (NT * b + t) + g + 1)
                        own_wait(pl)
                        for k in range(K):
                            pl.indirect_dma_start(
                                ring[:, g, k * 4 * GC:(k + 1) * 4 * GC], None, tables[b],
                                bass.IndirectOffsetOnAxis(
                                    ap=idx_now[:, g * K + k:g * K + k + 1].bitcast(U32), axis=0))\
                              .then_inc(gathered[g], 16)

        @block.tensor
        def _(pe):
            pe.wait_ge(s.constants_made, 14)

            def prep(b):
                pe.wait_ge(s.x_loaded, 16 * (b + 1))
                pe.wait_ge(s.padded, b)
                for t in range(NT):
                    last = pe.transpose(pcol(0, t), xin[:, t, :], ident[:, :])
                last.then_inc(s.x_transposed, 1)
                pe.wait_ge(s.channel_stats, b + 1)
                pe.matmul(ps[:, 2, 0:1], gn_avg[:, :], gn_mv[:, 0:1], start=True, stop=True)\
                  .then_inc(s.group_mean, 1)
                pe.wait_ge(s.spread, b + 1)
                pe.matmul(ps[:, 2, 1:2], gn_avg[:, :], gn_spread[:, :], start=True, stop=True)\
                  .then_inc(s.group_var, 1)
                pe.wait_ge(s.normalised, b + 1)
                for t in range(NT):
                    pe.wait_ge(s.offsets_copied, NT * b + (t - 1 if t >= 2 else 0))
                    pe.matmul(ps[:, 3 + t % 2, 0:4 * GK + ND * GC], xnorm[:, t * P:(t + 1) * P],
                              wq[:, :], start=True, stop=True).then_inc(s.offsets_summed, 1)
                for i in range(VALL):
                    pe.wait_ge(s.patches_copied, VALL * b + (i - 2 if i >= 3 else 0))
                    if i == 0:
                        pe.wait_ge(s.padded, b + 1)
                    r0 = (PROWS * (i // 2) + i % 2) * PITCH
                    for dx in range(2):
                        o = ps[0:VM, 5 + i % 3, dx * RC_:(dx + 1) * RC_]
                        pe.matmul(o, xpad[:, r0 + dx:r0 + dx + VM], vw[:, :], start=(dx == 0), stop=False,
                                  skip_group_check=True)
                        last = pe.matmul(o, inside[:, r0 + dx:r0 + dx + VM], vb_rows[:, :],
                                         start=False, stop=True, skip_group_check=True)
                    last.then_inc(s.patches_summed, 1)

            def turn_weights():
                pe.wait_ge(s.weights_loaded, 16 * loads["rest"])
                pe.wait_ge(s.padded, B)
                pe.wait_ge(s.offsets_copied, B * NT)
                for h in range(2):
                    pe.transpose(ps[:, 0, h * P:(h + 1) * P], wx_raw[:, h, :], ident[:, :])
                    last = pe.transpose(ps[:, 1, h * P:(h + 1) * P], wout_raw[:, h * P:(h + 1) * P], ident[:, :])
                last.then_inc(s.weights_turned, 1)
                pe.transpose(ps[:, 2, 0:P], ws_raw, ident[:, :]).then_inc(s.slice_turned, 1)
                pe.transpose(ps[:, 3, 0:E], lng, ident[0:E, 0:E])
                pe.transpose(ps[:, 3, E:2 * E], lnb, ident[0:E, 0:E])
                pe.transpose(ps[:, 3, 64:64 + EJ], b1_raw, ident[0:EJ, 0:EJ]).then_inc(s.ffn_turned, 1)
                pe.wait_ge(s.ln_cols_copied, 3)
                for i in range(EJ):
                    last = pe.matmul(ps[:, 4, i:i + 1], w1[:, i // HJ, (i % HJ) * P:(i % HJ + 1) * P],
                                     lnbT[:, i // HJ:i // HJ + 1], start=True, stop=True)
                last.then_inc(s.ffn_bias_summed, 1)
                pe.wait_ge(s.quarters_copied, 16 * 6)
                pe.wait_ge(s.dense_consts, DENSE_CONSTS)
                pe.matmul(ps[0:R, 5, 0:4 * ND], rep9[:, :, :].rearrange("k b j -> k (b j)"),
                          bias9[:, :, :].rearrange("k g q -> k (g q)"), start=True, stop=True)\
                  .then_inc(s.row_bias_summed, 1)
                pe.wait_ge(s.turned_copied, 2)
                pe.wait_ge(s.row_bias_copied, 1)
                pe.wait_ge(s.setup_done, 1)

            def conv_tile(T):
                pe.wait_ge(s.reduced, G * (T + 1))
                pe.transpose(ps[:, 1, 0:P], red[:, 0:P], ident[:, :])
                pe.transpose(ps[0:RC_ - P, 1, P:2 * P], red[:, P:RC_], ident[:, :]).then_inc(s.red_turned, 1)
                pe.wait_ge(s.redT_copied, 2 * (T + 1))
                pe.wait_ge(s.conv_added, T)
                pe.matmul(ps_y, redT[:, 0, :], outw_a[:, :], start=True, stop=False)
                pe.matmul(ps_y, redT[0:RC_ - P, 1, :], outw_b[:, :], start=False, stop=True)\
                  .then_inc(s.conv_summed, 1)

            def dense_tile(b, g, h, T, with_experts):
                v = (b * ND + g) * 2 + h
                u = T - NT
                pe.wait_ge(s.xb_loaded, 16 * (b + 1))
                x_sets = xb[:, bass.ds(h * HALF, HALF)].rearrange("p (s e) -> p s e", e=TOK)
                for q in range(4):
                    for k in range(TOK):
                        first = (R - K) - K * k
                        last = pe.matmul(ps[0:R, 3, q * SETS:(q + 1) * SETS], zw[:, g, q, first:first + R],
                                         x_sets[:, :, k], start=(k == 0), stop=(k == TOK - 1))
                last.then_inc(s.rows_summed, 1)
                if with_experts:
                    tile_turn(u)
                pe.wait_ge(s.parts_made, v + 1)
                lps = ps[:, 4, :].bitcast(BF16)
                for i in range(4):
                    pe.transpose(lps[:, i * R:(i + 1) * R], QY[:, 4 * i:4 * i + 4, :].rearrange("p q n -> p (q n)"),
                                 ident_bf[0:R, 0:R])
                for i in range(2):
                    last = pe.transpose(lps[:, (4 + i) * R:(5 + i) * R],
                                        QX[:, 4 * i:4 * i + 4, :].rearrange("p q n -> p (q n)"), ident_bf[0:R, 0:R])
                last.then_inc(s.parts_turned, 1)
                if with_experts:
                    tile_router(u)
                pe.wait_ge(s.parts_copied, v + 1)
                pe.wait_ge(s.dense_added, v)

                def distances(m):
                    if m:
                        pe.wait_ge(s.x_taken, 8 * v + m)
                    q = 32 * (m % 4)
                    pe.matmul(ps[0:R, X_BANK, :], L[q:q + 32, 4 + m // 4, :], EX[q:q + 32, :], start=True, stop=True)\
                      .then_inc(s.dx_summed, 1)
                    for j in (2 * m, 2 * m + 1):
                        if j >= 2:
                            pe.wait_ge(s.y_ready, 16 * v + j - 1)
                        q = 32 * (j % 4)
                        pe.matmul(ps[0:R, Y_BANKS[j % 2], :], L[q:q + 32, j // 4, :], EY[q:q + 32, :],
                                  start=True, stop=True).then_inc(s.dy_summed, 1)

                distances(0)
                if with_experts:
                    tile_up(u, 0, UP_BANKS[0])
                    tile_gate(u)
                for m in range(8):
                    if m < 7:
                        distances(m + 1)
                    pe.wait_ge(s.x_ready, 8 * v + m + 1)
                    pe.wait_ge(s.y_ready, 16 * v + 2 * m + 2)
                    if m >= 2:
                        pe.wait_ge(s.a_taken, 8 * v + m - 1)
                    for e in range(8):
                        last = pe.matmul(ps[:, A_BANKS[m % 2], e * 64:(e + 1) * 64],
                                         ysb[:, (2 * m + e // 4) % 4, e % 4, :], xsb[:, m % 2, e, :],
                                         start=True, stop=True)
                    last.then_inc(s.a_summed, 1)
                    if with_experts:
                        tile_down(u, m)
                        if m < 7:
                            tile_up(u, m + 1, UP_BANKS[0])
                pe.wait_ge(s.a_taken, 8 * v + 8)
                pe.wait_ge(s.values_loaded, 16 * NI * (b * ND + g + 1))
                for q in range(WW):
                    last = pe.matmul(ps[:, OUT_BANK, 0:P], vbd[:, q, :], asb[:, q, :], start=(q == 0), stop=(q == WW - 1))
                last.then_inc(s.dense_out, 1)
                gathered_tile(T, with_experts)
                pe.wait_ge(s.spread_made, v + 1)
                for i in range(4):
                    last = pe.matmul(ps[:, SUM_BANK, i * P:(i + 1) * P], osp[:, i * P:(i + 1) * P], outw_d[:, g, :],
                                     start=True, stop=True)
                last.then_inc(s.dense_summed, 1)

            def gathered_tile(T, with_experts):
                if with_experts:
                    pe.wait_ge(mid.expert_added, E * (T - NT) + E)
                conv_tile(T)

            def plain_tile(T, with_experts):
                if with_experts:
                    tile_experts(T - NT)
                gathered_tile(T, with_experts)

            def attention(b):
                pe.wait_ge(s.tile_normalised, b + 1)
                for t in range(NT):
                    last = pe.transpose(pcol(3, t), tn_tok[:, t, :], ident[:, :])
                last.then_inc(s.tn_turned, 1)
                pe.wait_ge(s.tnT_copied, b + 1)
                for h in range(2):
                    pe.wait_ge(s.xpT_copied, 2 * b + h)
                    for c in range(2):
                        last = pe.matmul(ps[:, 5 + c, :], wxT[:, h * P:(h + 1) * P], tnT[:, c * 512:(c + 1) * 512],
                                         start=True, stop=True)
                    last.then_inc(s.xpT_summed, 1)
                pe.wait_ge(s.xpT_copied, 2 * b + 2)
                for t in range(NT):
                    last = pe.matmul(ps[:, 3 + t // 2, (t % 2) * 256:(t % 2 + 1) * 256],
                                     tnT[:, t * P:(t + 1) * P], wxT[:, :], start=True, stop=True)
                last.then_inc(s.xp_summed, 1)
                pe.wait_ge(s.xp_copied, b + 1)
                for i in range(4):
                    h, c = i // 2, i % 2
                    if i >= 2:
                        pe.wait_ge(s.logits_done, 4 * b + i - 1)
                    pe.matmul(ps[:, 3 + 2 * (i % 2), :], ws_bd[:, :], xpT[:, h, c * 512:(c + 1) * 512],
                              start=True, stop=True)
                    pe.matmul(ps[:, 4 + 2 * (i % 2), :], wt_bd[:, :], xpT[:, h, c * 512:(c + 1) * 512],
                              start=True, stop=True).then_inc(s.logits_summed, 1)
                pe.wait_ge(s.exp_done, 2 * b + 2)
                for t in range(NT):
                    for h in range(2):
                        last = pe.transpose(ps[:, 3 + t // 2, ((t % 2) * 2 + h) * P:((t % 2) * 2 + h + 1) * P],
                                            eT[:, h, t * P:(t + 1) * P], ident[:, :])
                last.then_inc(s.e_turned, 1)
                pe.wait_ge(s.e_copied, b + 1)
                for h in range(2):
                    for t in range(NT):
                        last = pe.matmul(ps[:, 7, h * P:(h + 1) * P], xp_tok[:, t, h * P:(h + 1) * P],
                                         e_tok[:, t, h * P:(h + 1) * P], start=(t == 0), stop=(t == NT - 1))
                last.then_inc(s.slice_sums, 1)
                pe.wait_ge(s.bdE_done, b + 1)
                for h in range(2):
                    last = pe.matmul(ps[:, 3, h * P:(h + 1) * P], bdE[:, h, :], woutT[:, h, :], start=True, stop=True)
                last.then_inc(s.M_summed, 1)
                pe.wait_ge(s.M_copied, 2 * b + 2)
                for t in range(NT):
                    for h in range(2):
                        last = pe.matmul(pcol(5, t), eT[:, h, t * P:(t + 1) * P], Msb[:, h, :],
                                         start=(h == 0), stop=(h == 1))
                last.then_inc(s.attn_out, 1)

            def tile_turn(u):
                pe.wait_ge(mid.xn_chain, u + 1)
                pe.transpose(ps[:, 1, 0:P], tile["xt"][:, 0, :], ident[:, :])
                pe.transpose(ps[:, 1, P:2 * P], tile["xn"][:, 0, :], ident[:, :]).then_inc(mid.turned, 1)

            def tile_router(u):
                pe.wait_ge(mid.turned_copied, 2 * (u + 1))
                pe.matmul(ps[:, TILE_BANK, 0:E], tile["xtT"], wr[:, :], start=True, stop=True)\
                  .then_inc(mid.router_summed, 1)

            def tile_gate(u):
                pe.wait_ge(mid.gate_done, u + 1)
                pe.transpose(ps[0:E, TILE_BANK, 0:P], gate[:, 0, :], ident[:, :]).then_inc(mid.gate_turned, 1)
                pe.wait_ge(mid.gateT_copied, u + 1)
                pe.matmul(ps[:, TILE_BANK, P:P + C], tile["gateT"], b2[:, :], start=True, stop=True)\
                  .then_inc(mid.b2_summed, 1)

            def tile_up(u, e, bank):
                for j in range(HJ):
                    last = pe.matmul(ps[:, bank, j * P:(j + 1) * P], w1[:, e, j * P:(j + 1) * P], tile["xnT"],
                                     start=True, stop=True)
                last.then_inc(mid.hidden_summed, 1)

            def tile_down(u, e):
                if e == 0:
                    pe.wait_ge(mid.b2_added, u + 1)
                else:
                    pe.wait_ge(mid.expert_added, E * u + e)
                for j in range(HJ):
                    pe.wait_ge(mid.hidden_ready, HJ * (E * u + e) + j + 1)
                    last = pe.matmul(ps[:, TILE_BANK, 0:C], tile["hT"][:, e % 2, j, :], w2[:, e * HJ + j, :],
                                     start=(j == 0), stop=(j == HJ - 1))
                last.then_inc(mid.expert_summed, 1)

            def tile_experts(u):
                tile_turn(u)
                tile_router(u)
                tile_up(u, 0, UP_BANKS[0])
                tile_gate(u)
                for e in range(E):
                    if e < E - 1:
                        tile_up(u, e + 1, UP_BANKS[(e + 1) % 2])
                    tile_down(u, e)

            def image_experts(f, u, n, ntok, ar):
                xt_tok, xn_tok, xtT, xnT, hT, gateT = [ar[k] for k in ("xt", "xn", "xtT", "xnT", "hT", "gateT")]
                pe.wait_ge(f.xn_chain, n * (u + 1))
                for t in range(n):
                    pe.transpose(pcol(3, t), xt_tok[:, t, :], ident[:, :])
                for t in range(n):
                    last = pe.transpose(pcol(5, t), xn_tok[:, t, :], ident[:, :])
                last.then_inc(f.turned, 1)
                pe.wait_ge(f.turned_copied, 2 * (u + 1))
                for t in range(n):
                    last = pe.matmul(ps[:, 7, t * E:(t + 1) * E], xtT[:, t * P:(t + 1) * P], wr[:, :],
                                     start=True, stop=True)
                last.then_inc(f.router_summed, 1)
                tiles = ntok // P
                units = [(c, e) for c in range(n // tiles) for e in range(E)]
                FH, FY = len(units) * HJ, len(units) * tiles

                def up(i):
                    c, e = units[i]
                    for j in range(HJ):
                        m = i * HJ + j
                        if m >= 2:
                            pe.wait_ge(f.hidden_ready, FH * u + m - 1)
                        pe.matmul(ps[:, 5 + m % 2, 0:ntok], w1[:, e, j * P:(j + 1) * P],
                                  xnT[:, c * ntok:(c + 1) * ntok], start=True, stop=True).then_inc(f.hidden_summed, 1)

                def down(i):
                    c, e = units[i]
                    for t in range(tiles):
                        m = i * tiles + t
                        if m >= 2:
                            pe.wait_ge(f.expert_added, FY * u + m - 1)
                        for j in range(HJ):
                            if t == 0:
                                pe.wait_ge(f.hidden_ready, FH * u + i * HJ + j + 1)
                            last = pe.matmul(ps[:, Y_BANK[m % 2], 0:C], hT[:, i % 2, j, t * P:(t + 1) * P],
                                             w2[:, e * HJ + j, :], start=(j == 0), stop=(j == HJ - 1))
                        last.then_inc(f.expert_summed, 1)

                up(0)
                pe.wait_ge(f.gate_done, u + 1)
                for t in range(n):
                    last = pe.transpose(ps[0:E, 3 + t // 4, (t % 4) * P:(t % 4 + 1) * P], gate[:, t, :], ident[:, :])
                last.then_inc(f.gate_turned, 1)
                pe.wait_ge(f.gateT_copied, u + 1)
                for t in range(n):
                    last = pe.matmul(pcol(3, t), gateT[:, t * P:(t + 1) * P], b2[:, :], start=True, stop=True)
                last.then_inc(f.b2_summed, 1)
                pe.wait_ge(f.b2_added, u + 1)
                for i in range(1, len(units)):
                    up(i)
                    down(i - 1)
                down(len(units) - 1)

            pe.wait_ge(s.conv_weights_loaded, 16 * loads["conv"])
            pe.wait_ge(s.bias_parts, 8)
            prep(0)
            with pe.Fori(1, EARLY + 1) as b:
                prep(b)
                conv_tile(b - 1)
                pe.wait_ge(s.conv_added, b)
            if EARLY + 1 < B:
                with pe.Fori(EARLY + 1, B) as b:
                    prep(b)
            turn_weights()

            def image(b, with_experts):
                first, step = (0, STEP) if with_experts else (EARLY, 1)
                for g in range(ND):
                    with pe.Fori(0, 2) as h:
                        T = b * NT + first + (2 * g + h) * step
                        dense_tile(b, g, h, T, with_experts)
                        for k in range(1, step):
                            plain_tile(T + k, with_experts)
                rest = first + 2 * ND * step
                if rest < NT:
                    with pe.Fori(rest, NT) as t:
                        plain_tile(b * NT + t, with_experts)
                attention(b)

            image(0, False)
            with pe.Fori(1, B) as b:
                image(b, True)
            image_experts(end, 0, NT, 512, end_arrays)

        @block.scalar
        def _(act):
            def prep(b):
                act.wait_ge(s.group_var, b + 1)
                act.activation(gn_std[:, :], ps[:, 2, 1:2], ACT.Sqrt, bias=eps_col[:, :]).then_inc(s.group_std, 1)
                act.wait_ge(s.offsets_copied, NT * (b + 1))
                act.activation(sig, q_rest[:, 0, :, :].rearrange("p t m -> p (t m)"), ACT.Sigmoid)\
                   .then_inc(s.sigmoid_done, 1)
                for i in range(VALL):
                    v, dy = i // 2, i % 2
                    act.wait_ge(s.patches_summed, VALL * b + i + 1)
                    if dy == 0:
                        if v % 2 == 0:
                            act.wait_ge(s.patch_rows_even, 16 * ((VT + 1) // 2 * b + v // 2))
                        else:
                            act.wait_ge(s.patch_rows_odd, 16 * (VT // 2 * b + v // 2))
                    for dx in range(2):
                        last = act.activation(vrows[0:VM, v % 2, :, 2 * dy + dx, :],
                                              ps[0:VM, 5 + i % 3, dx * RC_:(dx + 1) * RC_]
                                              .rearrange("p (g c) -> p g c", g=G), ACT.Copy)
                    last.then_inc(s.patches_copied, 1)

            def turn_weights():
                act.wait_ge(s.weights_turned, 1)
                act.activation(wxT[:, :], ps[:, 0, 0:256], ACT.Copy).then_inc(s.turned_copied, 1)
                act.activation(woutT[:, :, :].rearrange("p h c -> p (h c)"), ps[:, 1, 0:256], ACT.Copy)\
                   .then_inc(s.turned_copied, 1)
                act.wait_ge(s.ffn_turned, 1)
                act.activation(lnbT[:, :], ps[:, 3, E:2 * E], ACT.Copy).then_inc(s.ln_cols_copied, 1)
                act.activation(lngT[:, :], ps[:, 3, 0:E], ACT.Copy).then_inc(s.ln_cols_copied, 1)
                act.activation(b1_turned[:, :], ps[:, 3, 64:64 + EJ], ACT.Copy).then_inc(s.ln_cols_copied, 1)
                act.wait_ge(s.row_bias_summed, 1)
                act.activation(row_bias[:, :, :].rearrange("p g q -> p (g q)"), ps[0:R, 5, 0:4 * ND], ACT.Copy)\
                   .then_inc(s.row_bias_copied, 1)

            def conv_tile(T):
                act.wait_ge(s.red_turned, T + 1)
                act.activation(redT[:, 0, :], ps[:, 1, 0:P], ACT.Copy).then_inc(s.redT_copied, 1)
                act.activation(redT[0:RC_ - P, 1, :], ps[0:RC_ - P, 1, P:2 * P], ACT.Copy).then_inc(s.redT_copied, 1)

            def tile_turned(u):
                act.wait_ge(mid.turned, u + 1)
                act.activation(tile["xtT"], ps[:, 1, 0:P], ACT.Copy).then_inc(mid.turned_copied, 1)
                act.activation(tile["xnT"], ps[:, 1, P:2 * P], ACT.Copy).then_inc(mid.turned_copied, 1)

            def tile_exp(u):
                act.wait_ge(mid.router_chain, 4 * (u + 1))
                act.activation(g_e[:, 0:1], g_d[:, 0:1], ACT.Exp).then_inc(mid.exp_ready, 1)

            def tile_gelu(u, e, bank):
                if e >= 2:
                    act.wait_ge(mid.expert_summed, E * u + e - 1)
                act.wait_ge(mid.hidden_summed, E * u + e + 1)
                for j in range(HJ):
                    act.activation(tile["hT"][:, e % 2, j, :], ps[:, bank, j * P:(j + 1) * P], ACT.Gelu,
                                   bias=b1_col[:, e * HJ + j:e * HJ + j + 1]).then_inc(mid.hidden_ready, 1)

            def tile_gate(u):
                act.wait_ge(mid.gate_turned, u + 1)
                act.activation(tile["gateT"], ps[0:E, TILE_BANK, 0:P], ACT.Copy).then_inc(mid.gateT_copied, 1)

            def plain_tile(T, with_experts):
                if with_experts:
                    u = T - NT
                    tile_turned(u)
                    tile_exp(u)
                    tile_gelu(u, 0, UP_BANKS[0])
                    tile_gate(u)
                    for e in range(1, E):
                        tile_gelu(u, e, UP_BANKS[e % 2])
                conv_tile(T)

            def dense_tile(b, g, h, T, with_experts):
                v = (b * ND + g) * 2 + h
                u = T - NT
                act.wait_ge(s.rows_summed, v + 1)
                act.activation(r_sig, ps[0:R, 3, 2 * SETS:3 * SETS], ACT.Sigmoid, bias=row_bias[:, g, 2:3])\
                   .then_inc(s.row_sigmoid, 1)
                if with_experts:
                    tile_turned(u)
                act.wait_ge(s.parts_turned, v + 1)
                act.activation(L[:, :, :].rearrange("p i r -> p (i r)"), ps[:, 4, :].bitcast(BF16)[:, 0:6 * R], ACT.Copy)\
                   .then_inc(s.parts_copied, 1)

                def weights(m):
                    act.wait_ge(s.dx_summed, 8 * v + m + 1)
                    d = ps[0:R, X_BANK, :]
                    act.activation(d, d, ACT.Abs).then_inc(s.x_chain, 1)
                    act.wait_ge(s.x_chain, 8 * v + m + 1)
                    if m >= 2:
                        act.wait_ge(s.a_summed, 8 * v + m - 1)
                    act.activation(xsb[:, m % 2, :, :].rearrange("p s n -> p (s n)"), d, ACT.Relu, bias=1.0,
                                   scale=-1.0).then_inc(s.x_taken, 1)
                    for j in (2 * m, 2 * m + 1):
                        act.wait_ge(s.dy_summed, 16 * v + j + 1)
                        d = ps[0:R, Y_BANKS[j % 2], :]
                        act.activation(d, d, ACT.Abs).then_inc(s.y_chain, 1)
                        act.wait_ge(s.y_chain, 16 * v + j + 1)
                        if j >= 4:
                            act.wait_ge(s.a_summed, 8 * v + (j - 4) // 2 + 1)
                        act.activation(ysb[:, j % 4, :, :].rearrange("p s n -> p (s n)"), d, ACT.Relu, bias=1.0,
                                       scale=-1.0).then_inc(s.y_ready, 1)

                weights(0)
                if with_experts:
                    tile_exp(u)
                    tile_gelu(u, 0, UP_BANKS[0])
                    tile_gate(u)
                for m in range(1, 8):
                    weights(m)
                    if with_experts:
                        tile_gelu(u, m, UP_BANKS[0])
                conv_tile(T)

            def attention(b):
                act.wait_ge(s.ln_stats, b + 1)
                act.activation(f_sd[:, :], f_mv[:, :, 1], ACT.Sqrt, bias=eps_col[:, :]).then_inc(s.ln_std, 1)
                act.wait_ge(s.tn_turned, b + 1)
                act.activation(tnT, ps[:, 3:5, :].rearrange("p a n -> p (a n)"), ACT.Copy).then_inc(s.tnT_copied, 1)
                for h in range(2):
                    act.wait_ge(s.xpT_summed, 2 * b + h + 1)
                    act.activation(xpT[:, h, :], ps[:, 5:7, :].rearrange("p a n -> p (a n)"), ACT.Identity,
                                   bias=bx_col[:, h:h + 1]).then_inc(s.xpT_copied, 1)
                act.wait_ge(s.max_done, b + 1)
                for h in range(2):
                    act.activation(eT[:, h, :], eT[:, h, :], ACT.Exp, bias=a_nmax[:, h:h + 1],
                                   accum_out=a_sum[:, h:h + 1]).then_inc(s.exp_done, 1)
                act.wait_ge(s.e_turned, b + 1)
                act.activation(e_tok.rearrange("p t c -> p (t c)"), ps[:, 3:7, :].rearrange("p a n -> p (a n)"),
                               ACT.Copy).then_inc(s.e_copied, 1)
                act.wait_ge(s.M_summed, b + 1)
                act.wait_ge(s.scale_done, b + 1)
                for h in range(2):
                    act.activation(Msb[:, h, :], ps[:, 3, h * P:(h + 1) * P], ACT.Copy, scale=a_sc[:, h:h + 1])\
                       .then_inc(s.M_copied, 1)
                act.wait_ge(s.en_stats1, b + 1)
                act.activation(f_sd[:, :], norms[:, :, 1], ACT.Sqrt, bias=eps_col[:, :]).then_inc(s.en_std1, 1)
                act.wait_ge(s.en_stats2, b + 1)
                act.activation(f_sd[:, :], norms[:, :, 3], ACT.Sqrt, bias=eps_col[:, :]).then_inc(s.en_std2, 1)

            def image_experts(f, u, n, ntok, ar):
                xtT, xnT, hT, gateT = [ar[k] for k in ("xtT", "xnT", "hT", "gateT")]
                act.wait_ge(f.turned, u + 1)
                for dst, bank in ((xtT, 3), (xnT, 5)):
                    if n == NT:
                        src = ps[:, bank:bank + 2, :].rearrange("p a n -> p (a n)")
                    else:
                        src = ps[:, bank, 0:n * P]
                    act.activation(dst[:, 0:n * P], src, ACT.Copy).then_inc(f.turned_copied, 1)
                act.wait_ge(f.router_chain, (2 * n + 2) * (u + 1))
                act.activation(g_e[:, 0:n], g_d[:, 0:n], ACT.Exp).then_inc(f.exp_ready, 1)
                tiles = ntok // P
                units = [(c, e) for c in range(n // tiles) for e in range(E)]
                FH, FY = len(units) * HJ, len(units) * tiles

                def gelu(i):
                    c, e = units[i]
                    if i >= 2:
                        act.wait_ge(f.expert_summed, FY * u + (i - 1) * tiles)
                    for j in range(HJ):
                        m = i * HJ + j
                        act.wait_ge(f.hidden_summed, FH * u + m + 1)
                        act.activation(hT[:, i % 2, j, 0:ntok], ps[:, 5 + m % 2, 0:ntok], ACT.Gelu,
                                       bias=b1_col[:, e * HJ + j:e * HJ + j + 1]).then_inc(f.hidden_ready, 1)

                gelu(0)
                act.wait_ge(f.gate_turned, u + 1)
                if n == NT:
                    src = ps[0:E, 3:5, :].rearrange("p a n -> p (a n)")
                else:
                    src = ps[0:E, 3, 0:n * P]
                act.activation(gateT[:, 0:n * P], src, ACT.Copy).then_inc(f.gateT_copied, 1)
                for i in range(1, len(units)):
                    gelu(i)

            act.wait_ge(s.small_constants, 7)
            prep(0)
            with act.Fori(1, EARLY + 1) as b:
                prep(b)
                conv_tile(b - 1)
            if EARLY + 1 < B:
                with act.Fori(EARLY + 1, B) as b:
                    prep(b)
            turn_weights()
            act.wait_ge(s.setup_done, 1)
            act.wait_ge(s.row_bias_copied, 1)
            tables_stored(act)

            def image(b, with_experts):
                first, step = (0, STEP) if with_experts else (EARLY, 1)
                for g in range(ND):
                    with act.Fori(0, 2) as h:
                        T = b * NT + first + (2 * g + h) * step
                        dense_tile(b, g, h, T, with_experts)
                        for k in range(1, step):
                            plain_tile(T + k, with_experts)
                rest = first + 2 * ND * step
                if rest < NT:
                    with act.Fori(rest, NT) as t:
                        plain_tile(b * NT + t, with_experts)
                attention(b)

            image(0, False)
            with act.Fori(1, B) as b:
                image(b, True)
            image_experts(end, 0, NT, 512, end_arrays)

        @block.vector
        def _(dve):
            def chain(sem, ins, value):
                ins.then_inc(sem, 1)
                dve.wait_ge(sem, value)

            def small_constants():
                dve.memset(eps_col[:, :], EPS).then_inc(s.small_constants, 1)
                dve.memset(idx_all[:, TILES, :], 0).then_inc(s.small_constants, 1)
                dve.wait_ge(s.constants_made, 14)
                dve.tensor_copy(ofs[:, :], ofs_i[:, :]).then_inc(s.small_constants, 1)
                dve.tensor_copy(expert_no[:, :], expert_i[:, :]).then_inc(s.small_constants, 1)
                dve.tensor_scalar(pos_b[:, :, 0], pos_i[:, :, 0], WW - 1, None, ALU.bitwise_and)\
                   .then_inc(s.small_constants, 1)
                chain(s.small_constants, dve.tensor_scalar(pos_b[:, :, 1], pos_i[:, :, 1], 5, None,
                                                           ALU.logical_shift_right), 6)
                chain(s.small_constants, dve.tensor_copy(pos[:, :, :], pos_b[:, :, :]), 7)

            def conv_constants():
                dve.wait_ge(s.conv_weights_loaded, 16 * loads["conv"])
                dve.memset(vb_rows[:, :], 0.0).then_inc(s.bias_parts, 1)
                for i in range(3):
                    if i < 2:
                        chain(s.bias_parts, dve.tensor_copy(vb_parts[:, i, :], vb), 2 + 2 * i)
                        chain(s.bias_parts, dve.tensor_tensor(vb, vb, vb_parts[:, i, :], ALU.subtract),
                              3 + 2 * i)
                    else:
                        chain(s.bias_parts, dve.tensor_copy(vb_parts[:, i, :], vb), 6)
                for i in range(3):
                    last = dve.tensor_copy(vb_rows[32 * i:32 * i + 1, :], vb_parts[32 * i:32 * i + 1, i, :])
                last.then_inc(s.bias_parts, 1)
                dve.tensor_tensor(qbias_off[:, :, :, :].rearrange("p g k d -> p g (k d)"),
                                  qbias_off[:, :, :, :].rearrange("p g k d -> p g (k d)"),
                                  prior_b[:, :, :].rearrange("p (o k) d -> p o (k d)", o=1)
                                  .broadcast_to([P, G, 2 * K]), ALU.add)
                chain(s.bias_parts, dve.tensor_copy(
                    qbias_rest[:, 0, :, :],
                    dscale_b[:, :].rearrange("p (g o) -> p g o", o=1).broadcast_to([P, G, K])), 8)

            def prep(b):
                dve.wait_ge(s.x_transposed, b + 1)
                own_wait(dve)
                for c in range(2):
                    last = dve.bn_stats(gn_stats[:, c, :], ps[:, c, :])
                chain(s.gn_chain, last, 4 * b + 1)
                own_wait(dve)
                dve.bn_aggr(gn_mv[:, :], gn_stats[:, :, :].rearrange("p a s -> p (a s)")).then_inc(s.channel_stats, 1)
                dve.wait_ge(s.group_mean, b + 1)
                dve.tensor_copy(gn_mean[:, :], ps[:, 2, 0:1]).then_inc(s.gn_chain, 1)
                dve.wait_ge(s.channel_stats, b + 1)
                chain(s.gn_chain, dve.tensor_tensor(gn_diff[:, :], gn_mv[:, 0:1], ps[:, 2, 0:1], ALU.subtract),
                      4 * b + 3)
                dve.scalar_tensor_tensor(gn_spread[:, :], gn_diff[:, :], gn_diff[:, :], gn_mv[:, 1:2],
                                         ALU.mult, ALU.add).then_inc(s.spread, 1)
                dve.wait_ge(s.group_std, b + 1)
                chain(s.gn_chain, dve.reciprocal(gn_r[:, :], gn_std[:, :]), 4 * b + 4)
                if not isinstance(b, int):
                    dve.wait_ge(s.math, MATH * b)
                    dve.wait_ge(s.xnorm_stored, 16 * b)
                    dve.wait_ge(s.values_stored, 16 * b)
                dve.tensor_scalar(xnorm, ps[:, 0:2, :].rearrange("p a n -> p (a n)"),
                                  gn_mean[:, :], gn_r[:, :], ALU.subtract, ALU.mult).then_inc(s.normalised, 1)
                dve.wait_ge(s.patches_summed, VALL * b)
                dve.tensor_scalar(interior(xpad), ps[:, 0:2, :].rearrange("p a (h w) -> p (a h) w", w=WW),
                                  gn_mean[:, :], gn_r[:, :], ALU.subtract, ALU.mult).then_inc(s.padded, 1)
                for t in range(NT):
                    dve.wait_ge(s.offsets_summed, NT * b + t + 1)
                    bank = ps[:, 3 + t % 2, :]
                    dve.tensor_tensor(q_off[:, t * 2 * GK:(t + 1) * 2 * GK], bank[:, 0:2 * GK],
                                      qbias_off[:, :, :, :].rearrange("p g k d -> p (g k d)"), ALU.add)
                    dve.tensor_tensor(vd_sb[:, t, :], bank[:, 4 * GK:4 * GK + ND * GC], vbias_d[:, :], ALU.add)
                    dve.tensor_tensor(q_rest[:, :, t, :],
                                      bank[:, 2 * GK:4 * GK].rearrange("p (a m) -> p a m", a=2),
                                      qbias_rest[:, :, :, :].rearrange("p a g k -> p a (g k)"), ALU.add)\
                       .then_inc(s.offsets_copied, 1)
                dve.wait_ge(s.sigmoid_done, b + 1)
                M = NT * GK
                done = [0]

                def math(ins, wait=True):
                    done[0] += 1
                    ins.then_inc(s.math, 1)
                    if wait:
                        dve.wait_ge(s.math, MATH * b + done[0])

                pair = lambda a: a.rearrange("p (m d) -> p m d", d=2)
                tile3 = lambda a: a.rearrange("p (t m d) -> p t m d", t=NT, d=2)
                math(dve.scalar_tensor_tensor(pair(pxy), pair(q_off), MAX_SCALE,
                                              sig.rearrange("p (m o) -> p m o", o=1).broadcast_to([P, M, 2]),
                                              ALU.mult, ALU.mult))
                math(dve.tensor_tensor(tile3(pxy), tile3(pxy),
                                       pos[:, :, :].rearrange("p t (o d) -> p t o d", o=1)
                                       .broadcast_to([P, NT, GK, 2]), ALU.add))
                math(dve.tensor_scalar(pxy, pxy, -1.0, float(WW), ALU.max, ALU.min))
                math(dve.tensor_copy(p_i, pxy))
                math(dve.tensor_tensor(p_f, p_i, pxy, ALU.is_gt))
                math(dve.tensor_tensor(p_f, p_i, p_f, ALU.subtract))
                math(dve.tensor_scalar(p_f, p_f, float(WW - 1), None, ALU.min))
                math(dve.tensor_tensor(p_w1, pxy, p_f, ALU.subtract))
                math(dve.tensor_scalar(p_w0, p_w1, -1.0, 1.0, ALU.mult, ALU.add), wait=False)
                a = pxy[:, 0:M]
                xy = lambda q, d: q.rearrange("p (m d) -> p m d", d=2)[:, :, d]
                math(dve.scalar_tensor_tensor(a, xy(p_f, 1), float(PITCH), xy(p_f, 0), ALU.mult, ALU.add))
                math(dve.tensor_scalar(a, a, float(G), None, ALU.mult))
                math(dve.tensor_tensor(idx_all[:, bass.ds(b * NT, NT), :], a.rearrange("p (t m) -> p t m", t=NT),
                                       ofs[:, :].rearrange("p (o m) -> p o m", o=1).broadcast_to([P, NT, GK]),
                                       ALU.add), wait=False)
                wk = q_rest[:, 1, :, :].rearrange("p t m -> p (t m)")
                u = p_f[:, 0:2 * M].rearrange("p (d m) -> p d m", d=2)
                math(dve.tensor_tensor(u[:, 0, :], wk, xy(p_w0, 1), ALU.mult), wait=False)
                math(dve.tensor_tensor(u[:, 1, :], wk, xy(p_w1, 1), ALU.mult))
                for dy in range(2):
                    for dx in range(2):
                        last = dve.tensor_tensor(
                            w4_all[:, bass.ds(b * NT, NT), :].rearrange("p t (m d) -> p t m d", d=4)
                            [:, :, :, 2 * dy + dx],
                            u[:, dy, :].rearrange("p (t m) -> p t m", t=NT),
                            xy(p_w1 if dx else p_w0, 0).rearrange("p (t m) -> p t m", t=NT), ALU.mult)
                        if dx == 1:
                            math(last, wait=False)
                assert done[0] == MATH

            consts_done = [POOL_CONSTS]

            def step(ins, wait=True):
                consts_done[0] += 1
                ins.then_inc(s.dense_consts, 1)
                if wait:
                    dve.wait_ge(s.dense_consts, consts_done[0])

            def dense_constants():
                dve.wait_ge(s.dense_consts, POOL_CONSTS)
                step(dve.tensor_copy(EY[0:32, :], ey_f), wait=False)
                step(dve.tensor_copy(EX[0:32, :], ex_f), wait=False)
                step(dve.tensor_copy(ident_bf[:, :], ident[:, :]), wait=False)
                step(dve.tensor_scalar(r7[:, :], r7_i[:, :], 0.0, None, ALU.is_ge))
                step(dve.tensor_reduce(blk[:, :], r7[:, :], AX, ALU.add))
                dve.tensor_copy(blk_i[:, 0:1], blk[:, :])
                step(dve.tensor_scalar(npos_i, npos_i, blk[:, :], None, ALU.add))
                dve.tensor_scalar(blk_i[:, 1:2], blk_i[:, 0:1], 1, None, ALU.logical_shift_right)
                dve.tensor_scalar(blk_i[:, 2:3], blk_i[:, 0:1], 1, None, ALU.bitwise_and)
                dve.tensor_scalar(npos_b[:, 0, :], npos_i, WW - 1, None, ALU.bitwise_and)
                step(dve.tensor_scalar(npos_b[:, 1, :], npos_i, 5, None, ALU.logical_shift_right))
                dve.tensor_copy(blk_f[:, :], blk_i[:, 1:3])
                step(dve.tensor_copy(rpos[:, :, :], npos_b))
                assert consts_done[0] == SCRATCH_SPENT, consts_done
                dve.memset(QY[:, :, 12:13], 1.0)
                dve.memset(QX[:, :, 24:25], 1.0)
                no = lambda n, m: expert_no[0:R, 0:n].rearrange("p (o n) -> p o n", o=1).broadcast_to([R, m, n])
                dve.tensor_scalar(QY[:, :, 13:13 + NI], no(NI, SETS // 4), blk_f[:, 0:1], None, ALU.is_equal)
                step(dve.tensor_scalar(QX[:, :, 25:25 + NA], no(NA, SETS // 8), blk_f[:, 1:2], None, ALU.is_equal),
                     wait=False)
                step(dve.tensor_copy(rep9[:, :, :], ident[0:K, 0:K].rearrange("p (o k) -> p o k", o=1)
                                     .broadcast_to([K, TOK, K])), wait=False)

            def dense_weights_laid_out():
                dve.wait_ge(s.weights_loaded, 16 * loads["rest"])
                dve.tensor_copy(bias9[:, :, 2], dscale9[:, :])
                step(dve.tensor_tensor(bias9[:, :, 0:2], bias9[:, :, 0:2],
                                       prior9[:, :].rearrange("k (o d) -> k o d", o=1).broadcast_to([K, ND, 2]),
                                       ALU.add), wait=False)
                nk = ND * K
                dve.tensor_copy(zw[:, :, 0:2, R - K:R].rearrange("p g d k -> p g k d"),
                                wqd_raw[:, 0:2 * nk].rearrange("p (g k d) -> p g k d", g=ND, k=K))
                step(dve.tensor_copy(zw[:, :, 2, R - K:R], wqd_raw[:, 2 * nk:3 * nk].rearrange("p (g k) -> p g k", g=ND)),
                     wait=False)
                step(dve.tensor_copy(zw[:, :, 3, R - K:R], wqd_raw[:, 3 * nk:4 * nk].rearrange("p (g k) -> p g k", g=ND)))
                assert consts_done[0] == DENSE_CONSTS, consts_done

            def finish_setup():
                dve.wait_ge(s.slice_turned, 1)
                dve.tensor_tensor(ws_bd[:, :], ps[:, 2, 0:P], head_mask[:, :], ALU.mult)
                dve.wait_ge(s.weights_loaded, 16 * loads["rest"])
                dve.tensor_scalar(wt_bd[:, :], head_mask[:, :], wt_col[:, :], None, ALU.mult)
                dve.tensor_scalar(bslice_col[:, :], bslice_raw[:, :], -LOG_NEG_LOG_EPS, None, ALU.add)
                dve.wait_ge(s.ffn_bias_summed, 1)
                dve.tensor_tensor(b1_col[:, :], ps[:, 4, 0:EJ], b1_turned[:, :], ALU.add)
                for e in range(E):
                    last = dve.tensor_scalar(w1[:, e, :], w1[:, e, :], lngT[:, e:e + 1], None, ALU.mult)
                last.then_inc(s.setup_done, 1)

            def conv_group(T, g):
                dve.wait_ge(gathered[g], 16 * K * (T + 1))
                w = w4_all[:, bass.ds(T, 1), g * 4 * K:(g + 1) * 4 * K].rearrange("p o m -> p (o m)")
                slot = ring[:, g, :].rearrange("p (m c) -> p m c", c=GC)
                dve.tensor_tensor(slot, slot, w.rearrange("p (m o) -> p m o", o=1).broadcast_to([P, 4 * K, GC]),
                                  ALU.mult).then_inc(s.products, 1)
                dve.wait_ge(s.products, G * T + g + 1)
                dve.tensor_reduce(red[:, g * GC:(g + 1) * GC], ring[:, g, :].rearrange("p (m c) -> p c m", c=GC),
                                  AX, ALU.add).then_inc(s.reduced, 1)
                dve.tensor_copy(idx_now[:, g * K:(g + 1) * K],
                                idx_all[:, bass.ds(T + 1, 1), g * K:(g + 1) * K].rearrange("p o m -> p (o m)"))\
                   .then_inc(s.idx_ready, 1)

            def conv_add(T):
                dve.wait_ge(s.conv_summed, T + 1)
                dve.tensor_tensor(tok(T), tok(T), ps_y.rearrange("p (o c) -> p o c", o=1), ALU.add)\
                   .then_inc(s.conv_added, 1)

            def dense_positions(b, g, h):
                v = (b * ND + g) * 2 + h
                done = [0]

                def step(ins):
                    done[0] += 1
                    ins.then_inc(s.row_math, 1)
                    dve.wait_ge(s.row_math, ROW_MATH * v + done[0])

                q = ps[0:R, 3, 0:4 * SETS].rearrange("p (q s) -> p q s", q=4)
                dve.wait_ge(s.rows_summed, v + 1)
                dve.wait_ge(s.row_sigmoid, v + 1)
                dve.tensor_scalar(r_w, q[:, 3, :], row_bias[:, g, 3:4], None, ALU.add)
                for d in range(2):
                    last = dve.scalar_tensor_tensor(r_off[:, d, :], q[:, d, :], row_bias[:, g, d:d + 1], r_sig,
                                                    ALU.add, ALU.mult)
                step(last)
                step(dve.scalar_tensor_tensor(r_pos, r_off, MAX_SCALE, rpos[:, :, bass.ds(h * SETS, SETS)],
                                              ALU.mult, ALU.add))
                step(dve.tensor_scalar(r_pos, r_pos, -2.0, WW + 1.0, ALU.max, ALU.min))
                yv = r_pos[:, 1, :].rearrange("p (m s) -> p m s", s=4)
                xv = r_pos[:, 0, :].rearrange("p (m s) -> p m s", s=8)
                for m in range(3):
                    yq, xq = QY[:, :, 4 * m:4 * m + 4], QX[:, :, 8 * m:8 * m + 8]
                    dve.tensor_copy(yq, yv)
                    if m == 2:
                        dve.tensor_copy(xq, xv).then_inc(s.parts_made, 1)
                        break
                    step(dve.tensor_copy(xq, xv))
                    dve.tensor_tensor(yv, yv, yq, ALU.subtract)
                    step(dve.tensor_tensor(xv, xv, xq, ALU.subtract))
                assert done[0] == ROW_MATH, done

            def dense_mult(v, m):
                dve.wait_ge(s.x_taken, 8 * v + m + 1)
                dve.tensor_tensor(
                    xsb[:, m % 2, :, :], xsb[:, m % 2, :, :],
                    r_w[:, 8 * m:8 * m + 8].rearrange("p (s o) -> p s o", o=1).broadcast_to([R, 8, 64]),
                    ALU.mult).then_inc(s.x_ready, 1)

            def dense_take(v, m):
                dve.wait_ge(s.a_summed, 8 * v + m + 1)
                dve.tensor_copy(asb[:, :, 16 * m:16 * m + 16].rearrange("p q n -> p n q"),
                                ps[:, A_BANKS[m % 2], :].rearrange("p (n q) -> p n q", q=WW))\
                   .then_inc(s.a_taken, 1)

            def dense_spread(v):
                dve.wait_ge(s.dense_out, v + 1)
                dve.tensor_tensor(
                    osp.rearrange("p (s i a) -> p s i a", i=NI, a=NA),
                    ps[:, OUT_BANK, 0:P].rearrange("p (s o a) -> p s o a", o=1, a=NA).broadcast_to([P, SETS, NI, NA]),
                    quad[:, :].rearrange("p (o i u) -> p o i u", o=1, u=1).broadcast_to([P, SETS, NI, NA]),
                    ALU.mult).then_inc(s.spread_made, 1)

            def dense_add(b, h, v, T):
                dve.wait_ge(s.dense_summed, v + 1)
                dve.wait_ge(s.conv_added, T + 1)
                own_wait(dve)
                x4 = tok(b * NT + 4 * h, 4)
                dve.tensor_tensor(x4, x4, ps[:, SUM_BANK, :].rearrange("p (t c) -> p t c", t=4), ALU.add)\
                   .then_inc(s.dense_added, 1)
                dve.wait_ge(s.dense_added, v + 1)

            def tile_tokens(u, t):
                chain(mid.xt_chain, dve.tensor_copy(norms_now[:, :], norms[:, bass.ds(t, 1), :]
                                                    .rearrange("p o n -> p (o n)")), 2 * u + 1)
                xt, xn = tile["xt"][:, 0, :], tile["xn"][:, 0, :]
                chain(mid.xt_chain, dve.tensor_scalar(xt, tok(u).rearrange("p o c -> p (o c)"), norms_now[:, 0:1],
                                                      norms_now[:, 1:2], ALU.subtract, ALU.mult), 2 * u + 2)
                dve.tensor_scalar(xn, xt, norms_now[:, 2:3], norms_now[:, 3:4], ALU.subtract, ALU.mult)\
                   .then_inc(mid.xn_chain, 1)

            def tile_add(u, e):
                dve.wait_ge(mid.expert_summed, E * u + e + 1)
                if e:
                    dve.wait_ge(mid.expert_added, E * u + e)
                x1 = tok(u).rearrange("p o c -> p (o c)")
                dve.scalar_tensor_tensor(x1, ps[:, TILE_BANK, 0:C], gate[:, 0, e:e + 1], x1, ALU.mult, ALU.add)\
                   .then_inc(mid.expert_added, 1)

            def tile_b2(u):
                dve.wait_ge(mid.b2_summed, u + 1)
                x1 = tok(u).rearrange("p o c -> p (o c)")
                dve.tensor_tensor(x1, x1, ps[:, TILE_BANK, P:P + C], ALU.add).then_inc(mid.b2_added, 1)
                dve.wait_ge(mid.b2_added, u + 1)

            def plain_tile(T, with_experts, t=None):
                u = T - NT
                groups_left = list(range(G))
                if with_experts:
                    tile_tokens(u, t)
                conv_group(T, groups_left.pop(0))
                if with_experts:
                    route(mid, u, 1, ps[:, TILE_BANK, 0:E], lambda: conv_group(T, groups_left.pop(0)))
                    tile_b2(u)
                    dve.wait_ge(mid.gate_done, u + 1)
                    for e in range(E):
                        tile_add(u, e)
                        if e % 2 == 1 and len(groups_left) > 1:
                            conv_group(T, groups_left.pop(0))
                for g in groups_left:
                    conv_group(T, g)
                conv_add(T)

            def dense_tile(b, g, h, T, with_experts, t=None):
                v = (b * ND + g) * 2 + h
                u = T - NT
                groups_left = list(range(G))
                if with_experts:
                    tile_tokens(u, t)
                dense_positions(b, g, h)
                conv_group(T, groups_left.pop(0))
                if with_experts:
                    route(mid, u, 1, ps[:, TILE_BANK, 0:E], lambda: conv_group(T, groups_left.pop(0)))
                    tile_b2(u)
                    dve.wait_ge(mid.gate_done, u + 1)
                for m in range(8):
                    dense_mult(v, m)
                    if m:
                        dense_take(v, m - 1)
                        if with_experts:
                            tile_add(u, m - 1)
                    if m % 2 == 1 and len(groups_left) > 1:
                        conv_group(T, groups_left.pop(0))
                dense_take(v, 7)
                if with_experts:
                    tile_add(u, 7)
                for g in groups_left:
                    conv_group(T, g)
                dense_spread(v)
                conv_add(T)
                dense_add(b, h, v, T)

            def attention(b):
                img = x_tok[:, bass.ds(b * NT, NT), :]
                one = lambda t: tok(b * NT + t).rearrange("p o c -> p (o c)")
                dve.wait_ge(s.conv_added, NT * (b + 1))
                for t in range(NT):
                    own_wait(dve)
                    last = dve.bn_stats(f_stats[:, t, :], one(t))
                chain(s.ln_chain, last, b + 1)
                own_wait(dve)
                for t in range(NT):
                    last = dve.bn_aggr(f_mv[:, t, :], f_stats[:, t, :])
                last.then_inc(s.ln_stats, 1)
                dve.wait_ge(s.ln_std, b + 1)
                chain(s.ln_recip, dve.reciprocal(f_r[:, :], f_sd[:, :]), b + 1)
                for t in range(NT):
                    last = dve.tensor_scalar(tn_tok[:, t, :], one(t), f_mv[:, t, 0:1], f_r[:, t:t + 1],
                                             ALU.subtract, ALU.mult)
                last.then_inc(s.tile_normalised, 1)
                dve.wait_ge(s.xp_summed, b + 1)
                dve.tensor_tensor(xp_tok, ps[:, 3:7, :].rearrange("p a (t c) -> p (a t) c", t=2),
                                  bx_b[:, :].rearrange("p (o c) -> p o c", o=1).broadcast_to([P, NT, 256]),
                                  ALU.add).then_inc(s.xp_copied, 1)
                dve.tensor_tensor(img, img, boutb_b[:, :].rearrange("p (o c) -> p o c", o=1)
                                  .broadcast_to([P, NT, C]), ALU.add).then_inc(s.bout_added, 1)
                for i in range(4):
                    h, c = i // 2, i % 2
                    dve.wait_ge(s.logits_summed, 4 * b + i + 1)
                    pl_, pt = ps[:, 3 + 2 * (i % 2), :], ps[:, 4 + 2 * (i % 2), :]
                    n0 = 3 * (4 * b + i)
                    chain(s.scale_chain, dve.tensor_scalar(temp_sb, pt, btemp_col[:, :], -0.4, ALU.add, ALU.max),
                          n0 + 1)
                    chain(s.scale_chain, dve.tensor_scalar(temp_sb, temp_sb, 0.4, 0.5, ALU.min, ALU.add), n0 + 2)
                    chain(s.scale_chain, dve.reciprocal(rtemp, temp_sb), n0 + 3)
                    dve.scalar_tensor_tensor(eT[:, h, c * 512:(c + 1) * 512], pl_, bslice_col[:, :], rtemp,
                                             ALU.add, ALU.mult).then_inc(s.logits_done, 1)
                dve.wait_ge(s.logits_done, 4 * b + 4)
                chain(s.gn_chain, dve.tensor_reduce(a_max[:, :], eT, AX, ALU.max), 4 * B + 5 * b + 1)
                dve.tensor_scalar(a_nmax[:, :], a_max[:, :], -1.0, None, ALU.mult).then_inc(s.max_done, 1)
                dve.wait_ge(s.exp_done, 2 * b + 2)
                chain(s.gn_chain, dve.reciprocal(a_rs[:, :], a_sum[:, :]), 4 * B + 5 * b + 2)
                chain(s.gn_chain, dve.tensor_tensor(a_norm[:, :], a_sum[:, :], a_rs[:, :], ALU.mult),
                      4 * B + 5 * b + 3)
                chain(s.gn_chain, dve.tensor_scalar(a_norm[:, :], a_norm[:, :], 1e-5, None, ALU.add),
                      4 * B + 5 * b + 4)
                chain(s.gn_chain, dve.reciprocal(a_rn[:, :], a_norm[:, :]), 4 * B + 5 * b + 5)
                dve.tensor_tensor(a_sc[:, :], a_rs[:, :], a_rn[:, :], ALU.mult).then_inc(s.ffn_turned, 1)
                dve.wait_ge(s.ffn_turned, 2 + b)
                dve.tensor_tensor(a_sc[:, :], a_sc[:, :], a_rs[:, :], ALU.mult).then_inc(s.scale_done, 1)
                dve.wait_ge(s.slice_sums, b + 1)
                dve.tensor_tensor(bdE, ps[:, 7, 0:256].rearrange("p (h n) -> p h n", h=2),
                                  head_mask[:, :].rearrange("p (o n) -> p o n", o=1).broadcast_to([P, 2, P]),
                                  ALU.mult).then_inc(s.bdE_done, 1)
                dve.wait_ge(s.attn_out, b + 1)
                dve.wait_ge(s.bout_added, b + 1)
                dve.tensor_tensor(img, img, ps[:, 5:7, :].rearrange("p a (t c) -> p (a t) c", t=4), ALU.add)\
                   .then_inc(s.attn_added, 1)
                dve.wait_ge(s.attn_added, b + 1)
                CH = 4
                own_wait(dve)
                for t in range(NT):
                    last = dve.bn_stats(f_stats[:, t, :], one(t))
                chain(s.en_chain, last, CH * b + 1)
                own_wait(dve)
                for t in range(NT):
                    last = dve.bn_aggr(norms[:, t, 0:2], f_stats[:, t, :])
                last.then_inc(s.en_stats1, 1)
                dve.wait_ge(s.en_std1, b + 1)
                chain(s.en_chain, dve.reciprocal(norms[:, :, 1], f_sd[:, :]), CH * b + 2)
                for t in range(NT):
                    last = dve.tensor_scalar(tn_tok[:, t, :], one(t), norms[:, t, 0:1], norms[:, t, 1:2],
                                             ALU.subtract, ALU.mult)
                chain(s.en_chain, last, CH * b + 3)
                own_wait(dve)
                for t in range(NT):
                    last = dve.bn_stats(f_stats[:, t, :], tn_tok[:, t, :])
                chain(s.en_chain, last, CH * b + 4)
                own_wait(dve)
                for t in range(NT):
                    last = dve.bn_aggr(norms[:, t, 2:4], f_stats[:, t, :])
                last.then_inc(s.en_stats2, 1)
                dve.wait_ge(s.en_std2, b + 1)
                chain(s.en_ready, dve.reciprocal(norms[:, :, 3], f_sd[:, :]), b + 1)

            def route(f, u, n, sums, between=lambda: None):
                RC = 2 * n + 2
                dve.wait_ge(f.router_summed, u + 1)
                chain(f.router_chain, dve.tensor_tensor(
                    rl[:, 0:n, :], sums.rearrange("p (t e) -> p t e", e=E),
                    br_b[:, :].rearrange("p (o e) -> p o e", o=1).broadcast_to([P, n, E]), ALU.add), RC * u + 1)
                own_wait(dve)
                for t in range(n):
                    dve.max(top_v[:, t, :], rl[:, t, :]).then_inc(f.router_chain, 1)
                dve.wait_ge(f.router_chain, RC * u + 1 + n)
                own_wait(dve)
                for t in range(n):
                    dve.max_index(top_i[:, t, :], top_v[:, t, :], rl[:, t, :]).then_inc(f.router_chain, 1)
                dve.tensor_tensor(g_d[:, 0:n], top_v[:, 0:n, 1], top_v[:, 0:n, 0], ALU.subtract)\
                   .then_inc(f.router_chain, 1)
                dve.wait_ge(f.router_chain, RC * u + 1 + 2 * n)
                dve.tensor_copy(top_f[:, 0:n, :], top_i[:, 0:n, 0:2])
                between()
                dve.wait_ge(f.exp_ready, u + 1)
                GC_ = 4
                chain(f.gate_chain, dve.tensor_scalar(g_den[:, 0:n], g_e[:, 0:n], 1.0, None, ALU.add), GC_ * u + 1)
                chain(f.gate_chain, dve.reciprocal(g_w1[:, 0:n], g_den[:, 0:n]), GC_ * u + 2)
                chain(f.gate_chain, dve.tensor_tensor(g_w2[:, 0:n], g_w1[:, 0:n], g_e[:, 0:n], ALU.mult),
                      GC_ * u + 3)
                for t in range(n):
                    dve.tensor_scalar(gate[:, t, :], expert_no[:, :], top_f[:, t, 0:1], g_w1[:, t:t + 1],
                                      ALU.is_equal, ALU.mult)
                    last = dve.tensor_scalar(gate2[:, t, :], expert_no[:, :], top_f[:, t, 1:2], g_w2[:, t:t + 1],
                                             ALU.is_equal, ALU.mult)
                chain(f.gate_chain, last, GC_ * u + 4)
                dve.tensor_tensor(gate[:, 0:n, :], gate[:, 0:n, :], gate2[:, 0:n, :], ALU.add)\
                   .then_inc(f.gate_done, 1)

            def image_experts(f, u, n, ntok, T0, ar):
                xt_tok, xn_tok = ar["xt"], ar["xn"]
                tile_of = lambda t: tok(T0 + t).rearrange("p o c -> p (o c)")
                for t in range(n):
                    last = dve.tensor_scalar(xt_tok[:, t, :], tile_of(t), norms[:, t, 0:1], norms[:, t, 1:2],
                                             ALU.subtract, ALU.mult)
                chain(f.xt_chain, last, u + 1)
                for t in range(n):
                    dve.tensor_scalar(xn_tok[:, t, :], xt_tok[:, t, :], norms[:, t, 2:3], norms[:, t, 3:4],
                                      ALU.subtract, ALU.mult).then_inc(f.xn_chain, 1)
                route(f, u, n, ps[:, 7, 0:n * E])
                dve.wait_ge(f.b2_summed, u + 1)
                for c in range((n + 3) // 4):
                    m = min(4, n)
                    last = dve.tensor_tensor(tok(T0 + 4 * c, m), tok(T0 + 4 * c, m),
                                             ps[:, 3 + c, 0:m * P].rearrange("p (t c) -> p t c", t=m), ALU.add)
                last.then_inc(f.b2_added, 1)
                dve.wait_ge(f.b2_added, u + 1)
                tiles = ntok // P
                units = [(c, e) for c in range(n // tiles) for e in range(E)]
                FY = len(units) * tiles
                dve.wait_ge(f.gate_done, u + 1)
                for i, (c, e) in enumerate(units):
                    for t in range(tiles):
                        m = i * tiles + t
                        tt = c * tiles + t
                        dve.wait_ge(f.expert_summed, FY * u + m + 1)
                        if e:
                            dve.wait_ge(f.expert_added, FY * u + m - tiles + 1)
                        dve.scalar_tensor_tensor(tile_of(tt), ps[:, Y_BANK[m % 2], 0:C], gate[:, tt, e:e + 1],
                                                 tile_of(tt), ALU.mult, ALU.add).then_inc(f.expert_added, 1)

            small_constants()
            conv_constants()
            dense_constants()
            prep(0)
            dve.tensor_copy(idx_now[:, :], idx_all[:, 0, :]).then_inc(s.idx_ready, G)
            dve.wait_ge(s.x_tok_loaded, 16 * B)
            chain(s.out_bias_added, dve.tensor_tensor(
                x_tok[:, :, :], x_tok[:, :, :], outb_b[:, :].rearrange("p (o c) -> p o c", o=1)
                .broadcast_to([P, TILES, C]), ALU.add), 1)
            with dve.Fori(1, EARLY + 1) as b:
                prep(b)
                for g in range(G):
                    conv_group(b - 1, g)
                conv_add(b - 1)
            if EARLY + 1 < B:
                with dve.Fori(EARLY + 1, B) as b:
                    prep(b)
            dense_weights_laid_out()
            finish_setup()
            tables_stored(dve)
            dve.wait_ge(s.xnorm_stored, 16 * B)
            dve.wait_ge(s.values_stored, 16 * B)
            dve.wait_ge(s.row_bias_copied, 1)

            def image(b, with_experts):
                first, step = (0, STEP) if with_experts else (EARLY, 1)
                for g in range(ND):
                    with dve.Fori(0, 2) as h:
                        t = first + (2 * g + h) * step
                        dense_tile(b, g, h, b * NT + t, with_experts, t)
                        for k in range(1, step):
                            plain_tile(b * NT + t + k, with_experts, t + k)
                rest = first + 2 * ND * step
                if rest < NT:
                    with dve.Fori(rest, NT) as t:
                        plain_tile(b * NT + t, with_experts, t)
                attention(b)

            image(0, False)
            with dve.Fori(1, B) as b:
                image(b, True)
            image_experts(end, 0, NT, 512, TILES - NT, end_arrays)


def kernel(**inputs):
    import numpy as _np
    import concourse.bacc as _bacc
    from concourse import mybir as _mybir
    from concourse.bass_utils import run_bass_kernel_spmd as _run

    nc = _bacc.Bacc("TRN2", target_bir_lowering=False, num_devices=1)
    arrays, aps = {}, {}
    for name, value in inputs.items():
        a = _np.ascontiguousarray(value)
        arrays[f"in_{name}"] = a
        aps[name] = nc.dram_tensor(f"in_{name}", a.shape, _mybir.dt.from_np(a.dtype), kind="ExternalInput").ap()
    shape = arrays["in_x"].shape
    out = nc.dram_tensor("out_0", shape, _mybir.dt.float32, kind="ExternalOutput").ap()
    conv_attn_moe(nc, aps, out)
    r = _run(nc, [arrays], core_ids=[0])
    return r.results[0]["out_0"]
```

```python
from contextlib import ExitStack
from collections import namedtuple

import concourse.bass as bass
from concourse import mybir

F32 = mybir.dt.float32
BF16 = mybir.dt.bfloat16
I32 = mybir.dt.int32
U32 = mybir.dt.uint32
ALU = mybir.AluOpType
ACT = mybir.ActivationFunctionType
AX = mybir.AxisListType.X

P = 128
B, HH, WW, C = 4, 32, 32, 128
N = HH * WW
NT = N // P
TILES = B * NT
GALL, GC, K = 8, 32, 9
G = 6
ND = GALL - G
GK = G * K
RC_ = G * GC
SETS = 64
NI, NA = 4, 2
TOK = NI * NA
R = TOK * K
EARLY = 2
assert NT - EARLY == 6 and ND == 2 and G == 6
STEP_GROUPS = [[(0, g) for g in range(6)], [(1, 0), (1, 1), (1, 2)],
               [(1, 3), (1, 4), (1, 5), (2, 0), (2, 1), (2, 2)], [(2, 3), (2, 4), (2, 5)]]
BIG = 64.0
HALF = N // 2
PW = WW + 1
PITCH = WW + 2
PATCHES = PW * PITCH
PROWS = 3
VT = PW // PROWS
VM = PROWS * PITCH
PAD = (HH + 2) * PITCH + 2
VALL = 2 * VT
MAX_SCALE = 6.0
GN_GROUP = 4
HG, S, DH = 4, 32, 32
LOG_NEG_LOG_EPS = 2.625792
EPS = 1e-5
E, HID = 8, 512
HJ = HID // P
EJ = E * HJ
ROW_MATH = 7
POOL_CONSTS = 27
SCRATCH_SPENT = POOL_CONSTS + 8
DENSE_CONSTS = POOL_CONSTS + 13
MATH = 16

EVENTS = """
constants_made small_constants conv_weights_loaded weights_loaded x_loaded x_tok_loaded
bias_parts weights_turned slice_turned ffn_turned ffn_bias_summed turned_copied ln_cols_copied setup_done
x_transposed channel_stats group_mean spread group_var group_std gn_chain normalised padded
offsets_summed offsets_copied sigmoid_done math patches_summed patches_copied
patch_rows_even patch_rows_odd xnorm_stored values_stored
dense_consts quarters_copied row_bias_summed row_bias_copied
idx_ready products reduced red_turned redT_copied conv_summed conv_added
ln_chain ln_stats ln_std ln_recip tile_normalised
xb_loaded values_loaded rows_summed row_sigmoid row_math parts_made parts_turned parts_copied
dx_summed x_chain x_taken x_ready dy_summed y_chain y_ready a_summed a_taken dense_out spread_made
dense_summed dense_added
tn_turned tnT_copied xpT_summed xpT_copied xp_summed xp_copied logits_summed
temps_summed rtemp_ready logits_biased logits_done
max_chain max_done exp_done divisors_chain scale_chain scale_done e_turned e_copied slice_sums bdE_done M_summed M_copied attn_out
attn_added bout_added out_bias_added
en_chain en_stats1 en_std1 en_stats2 en_std2 en_ready
own_wait
rows_stored
"""
ROUTE_EVENTS = """
xn_ready turned turned_copied router_summed router_chain exp_ready gate_chain gate_done gate_turned gateT_copied
b2_summed b2_added
"""
FFN_EVENTS = """
gate_picked hidden_summed hidden_ready expert_summed expert_added
"""


def conv_attn_moe(nc, t_in, out):
    x_d = t_in["x"].rearrange("b h w c -> (b h w) c").rearrange("(b t p) c -> b p t c", t=NT, p=P)
    out_d = out.rearrange("b h w c -> (b h w) c").rearrange("(n p) c -> n p c", p=P)

    with ExitStack() as ctx:
        def sb(name, shape, dt=F32):
            return ctx.enter_context(nc.sbuf_tensor(name, shape, dt))

        def sem(name):
            return ctx.enter_context(nc.semaphore(name))

        s = namedtuple("Events", EVENTS.split())(*[sem(n) for n in EVENTS.split()])
        gathered = [sem(f"gathered_group_{g}") for g in range(G)]
        r = namedtuple("RouteEvents", ROUTE_EVENTS.split())(*[sem(n + "_route") for n in ROUTE_EVENTS.split()])
        ffn_events = namedtuple("ExpertEvents", FFN_EVENTS.split())
        mid = ffn_events(*[sem(n + "_mid") for n in FFN_EVENTS.split()])
        end = ffn_events(*[sem(n + "_end") for n in FFN_EVENTS.split()])

        tables = [nc.dram_tensor(f"patch_table_{b}", [PATCHES * G, 4 * GC], F32, kind="Internal").ap()
                  for b in range(B)]
        xn_dram = nc.dram_tensor("normalised_images", [B, C, N], F32, kind="Internal").ap()
        values_dram = nc.dram_tensor("dense_values", [B, N, ND * GC], F32, kind="Internal").ap()

        ident = sb("ident", [P, P])
        gn_avg = sb("gn_avg", [P, P])
        head_mask = sb("head_mask", [P, P])
        vw = sb("vw", [C, RC_])
        vb_rows = sb("vb_rows", [96, RC_], BF16)
        inside = sb("inside", [96, PAD], BF16)
        wq = sb("wq", [C, 4 * GK + ND * GC])
        qbias_off = sb("qbias_off", [P, G, K, 2])
        prior_b = sb("prior_b", [P, K, 2])
        dscale_b = sb("dscale_b", [P, G])
        qbias_rest = sb("qbias_rest", [P, 2, G, K])
        outw_a = sb("outw_a", [P, C])
        outw_b = sb("outw_b", [RC_ - P, C])
        outw_d = sb("outw_d", [P, ND, C])
        vbias_d = sb("vbias_d", [P, ND * GC])
        outb_b = sb("outb_b", [P, C])
        boutb_b = sb("boutb_b", [P, C])
        bx_b = sb("bx_b", [P, 256])
        bx_col = sb("bx_col", [P, 2])
        bslice_raw = sb("bslice_raw", [P, 1])
        bslice_col = sb("bslice_col", [P, 1])
        btemp_col = sb("btemp_col", [P, 1])
        wxT = sb("wxT", [C, 256])
        woutT = sb("woutT", [P, 2, C])
        ws_bd = sb("ws_bd", [P, P])
        wt_col = sb("wt_col", [P, 1])
        wt_bd = sb("wt_bd", [P, P])
        head_pick = sb("head_pick", [P, P])
        wr = sb("wr", [C, E])
        br_b = sb("br_b", [P, E])
        lngT = sb("lngT", [C, E])
        lnbT = sb("lnbT", [C, E])
        w1 = sb("w1", [C, E, HID])
        b1_turned = sb("b1_turned", [P, EJ])
        b1_col = sb("b1_col", [P, EJ])
        w2 = sb("w2", [P, EJ, C])
        b2 = sb("b2", [E, C])
        eps_col = sb("eps_col", [P, 1])
        ofs_i = sb("ofs_i", [P, GK], I32)
        ofs = sb("ofs", [P, GK])
        pos_i = sb("pos_i", [P, NT, 2], I32)
        pos_b = sb("pos_b", [P, NT, 2], I32)
        pos = sb("pos", [P, NT, 2])
        expert_i = sb("expert_i", [P, E], I32)
        expert_no = sb("expert_no", [P, E])

        x_tok = sb("x_tok", [P, TILES, C])
        idx_all = sb("idx_all", [P, TILES + 1, GK], I32)
        w4_all = sb("w4_all", [P, TILES, GK * 4])
        idx_now = sb("idx_now", [P, GK], I32)
        ring = sb("ring", [P, G, K * 4 * GC])
        red = sb("red", [P, RC_])
        redT = sb("redT", [P, 2, P])

        ident_bf = sb("ident_bf", [P, P], BF16)
        zw = sb("zw", [C, ND, 4, 2 * (R - K) + K])
        row_bias = sb("row_bias", [R, ND, 4])
        rep9 = sb("rep9", [K, TOK, K])
        bias9 = sb("bias9", [K, ND, 4])
        prior9 = sb("prior9", [K, 2])
        dscale9 = sb("dscale9", [K, ND])
        r7_i = sb("r7_i", [R, TOK - 1], I32)
        r7 = sb("r7", [R, TOK - 1])
        blk = sb("blk", [R, 1])
        blk_i = sb("blk_i", [R, 3], I32)
        blk_f = sb("blk_f", [R, 2])
        rpos = sb("rpos", [R, 2, 2 * SETS])
        QYW, QXW = 32, 32
        QY = sb("QY", [R, SETS // 4, QYW], BF16)
        QX = sb("QX", [R, SETS // 8, QXW], BF16)
        L = sb("L", [P, 6, R], BF16)
        EY = sb("EY", [P, 512], BF16)
        EX = sb("EX", [P, 512], BF16)
        quad = sb("quad", [P, NI])
        vbd = sb("vbd", [P, WW, P])

        REGION = 11776
        region = sb("region", [P, REGION])
        at = [0]

        def part(n):
            at[0] += n
            assert at[0] <= REGION, at[0]
            return region[:, at[0] - n:at[0]]

        xin = part(NT * C).rearrange("p (t c) -> p t c", t=NT)
        xpad = part(PAD)
        xnorm = part(N)
        vd_sb = part(NT * ND * GC).rearrange("p (t m) -> p t m", t=NT)
        vrows = part(2 * 4 * G * GC).rearrange("p (r g d c) -> p r g d c", r=2, g=G, d=4)
        q_off = part(NT * GK * 2)
        q_rest = part(2 * NT * GK).rearrange("p (s t m) -> p s t m", s=2, t=NT)
        sig = part(NT * GK)
        pxy = part(NT * GK * 2)
        p_i = part(NT * GK * 2).bitcast(I32)
        p_f = part(NT * GK * 2)
        p_w1 = part(NT * GK * 2)
        p_w0 = q_off
        at[0] = 0
        tn_tok = part(NT * C).rearrange("p (t c) -> p t c", t=NT)
        tnT = part(N)
        xpT = part(2 * N).rearrange("p (h n) -> p h n", h=2)
        xp_tok = part(NT * 256).rearrange("p (t c) -> p t c", t=NT)
        eT = part(2 * N).rearrange("p (h n) -> p h n", h=2)
        e_tok = part(NT * 256).rearrange("p (t c) -> p t c", t=NT)
        temp_sb = part(512)
        rtemp = part(512)
        bdE = part(2 * P).rearrange("p (h n) -> p h n", h=2)
        Msb = part(2 * P).rearrange("p (h n) -> p h n", h=2)
        at[0] = 0
        tile_hT = part(2 * HJ * P).rearrange("p (r j n) -> p r j n", r=2, j=HJ)
        xnT = part(N)
        experts_at = at[0]
        at[0] += N
        xn_tok = part(NT * C).rearrange("p (t c) -> p t c", t=NT)
        xtT = part(N)
        gateT = part(N)[0:E, :]
        at[0] = experts_at
        end_hT = part(2 * HJ * 512).rearrange("p (r j n) -> p r j n", r=2, j=HJ)
        at[0] = experts_at
        xb = part(N)
        asb = part(WW * SETS * NA).rearrange("p (q n) -> p q n", q=WW)
        ysb = part(4 * 512).rearrange("p (r s n) -> p r s n", r=4, s=4)[0:R]
        xsb = part(2 * 512).rearrange("p (r s n) -> p r s n", r=2, s=8)[0:R]
        osp = part(HALF)
        r_off = part(2 * SETS).rearrange("p (d s) -> p d s", d=2)[0:R]
        r_pos = part(2 * SETS).rearrange("p (d s) -> p d s", d=2)[0:R]
        r_sig = part(SETS)[0:R]
        r_w = part(SETS)[0:R]
        stage = sb("stage", [P, 10 * P])
        wx_raw = stage[:, 0:2 * P].rearrange("p (h c) -> p h c", h=2)
        wout_raw = stage[:, 2 * P:4 * P]
        ws_raw = stage[:, 4 * P:5 * P]
        lng = stage[0:E, 5 * P:6 * P]
        lnb = stage[0:E, 6 * P:7 * P]
        b1_raw = stage[0:EJ, 7 * P:8 * P]
        wqd_raw = stage[:, 8 * P:8 * P + 4 * ND * K]
        vb = ring[0:96, 0, 0:RC_]
        vb_parts = ring[0:96, 1, 0:3 * RC_ // 2].bitcast(BF16).rearrange("p (a c) -> p a c", a=3)
        ey_i = ring[0:32, 2, 0:512].bitcast(I32)
        ey_f = ring[0:32, 3, 0:512]
        ex_f = ring[0:32, 3, 512:1024]
        npos_i = ring[0:R, 4, 0:2 * SETS].bitcast(I32)
        npos_b = ring[0:R, 4, 2 * SETS:6 * SETS].bitcast(I32).rearrange("p (d s) -> p d s", d=2)

        gn_stats = sb("gn_stats", [P, 2, 6])
        gn_mv = sb("gn_mv", [P, 2])
        gn_diff = sb("gn_diff", [P, 1])
        gn_mean = sb("gn_mean", [P, 1])
        gn_spread = sb("gn_spread", [P, 1])
        gn_std = sb("gn_std", [P, 1])
        gn_r = sb("gn_r", [P, 1])
        f_stats = sb("f_stats", [P, NT, 6])
        f_mv = sb("f_mv", [P, NT, 2])
        f_sd = sb("f_sd", [P, NT])
        f_r = sb("f_r", [P, NT])
        norms = sb("norms", [P, NT, 4])
        gate_now = sb("gate_now", [P, E])
        a_max = sb("a_max", [P, 2])
        a_nmax = sb("a_nmax", [P, 2])
        a_sum = sb("a_sum", [P, 2])
        a_rs = sb("a_rs", [P, 2])
        a_norm = sb("a_norm", [P, 2])
        a_rn = sb("a_rn", [P, 2])
        a_sc = sb("a_sc", [P, 2])
        gate = sb("gate", [P, NT, E])
        gate2 = sb("gate2", [P, NT, E])
        rl = sb("rl", [P, NT, E])
        top_v = sb("top_v", [P, NT, 8])
        top_i = sb("top_i", [P, NT, 8], U32)
        top_f = sb("top_f", [P, NT, 2])
        g_d = sb("g_d", [P, NT])
        g_e = sb("g_e", [P, NT])
        g_den = sb("g_den", [P, NT])
        g_w1 = sb("g_w1", [P, NT])
        g_w2 = sb("g_w2", [P, NT])

        ps = ctx.enter_context(nc.psum_tensor("ps", [P, 8, 512], F32))
        TILE_BANK, UP_BANKS = 2, (1, 3)
        Y_BANKS, X_BANK, A_BANKS, OUT_BANK, SUM_BANK = (6, 7), 5, (3, 0), 4, 5
        Y_BANK = [7, 4]

        def pcol(bank, t):
            return ps[:, bank + t // 4, (t % 4) * P:(t % 4 + 1) * P]

        def interior(a):
            return a[:, PITCH:(HH + 1) * PITCH].rearrange("p (h w) -> p h w", w=PITCH)[:, :, 1:WW + 1]

        def tok(T, n=1):
            return x_tok[:, bass.ds(T, n), :]

        def own_wait(eng):
            eng.sem_inc(s.own_wait, 1)

        def tables_stored(eng):
            eng.wait_ge(s.patch_rows_even, 16 * B * ((VT + 1) // 2))
            eng.wait_ge(s.patch_rows_odd, 16 * B * (VT // 2))

        block = ctx.enter_context(nc.Block())
        loads = {"conv": 0, "rest": 0}

        @block.sync
        def _(sp):
            def load(dst, src, which="rest"):
                loads[which] += 1
                sp.dma_start(dst, src).then_inc(s.weights_loaded if which == "rest" else s.conv_weights_loaded, 16)

            def bc(ap, n, rows=P):
                return ap.rearrange("(o n) -> o n", o=1).broadcast_to([rows, n])

            def store_patches(b):
                for v in range(VT):
                    sp.wait_ge(s.patches_copied, VALL * b + 2 * v + 2)
                    sp.dma_start(tables[b].rearrange("(n g) d -> n (g d)", g=G)[v * VM:(v + 1) * VM, :],
                                 vrows[0:VM, v % 2, :, :, :].rearrange("p g d c -> p (g d c)"))\
                      .then_inc(s.patch_rows_odd if v % 2 else s.patch_rows_even, 16)

            def groups(ap, a, b, per):
                return ap[:, a * per:b * per]

            sp.dma_start(xin, x_d[0]).then_inc(s.x_loaded, 16)
            load(wq[:, 0:2 * GK], groups(t_in["L0_conv_qd_w"], 0, G, 2 * K), "conv")
            load(wq[:, 2 * GK:3 * GK], groups(t_in["L0_conv_qs_w"], 0, G, K), "conv")
            load(wq[:, 3 * GK:4 * GK], groups(t_in["L0_conv_qw_w"], 0, G, K), "conv")
            load(wq[:, 4 * GK:4 * GK + ND * GC], groups(t_in["L0_conv_v_w"], G, GALL, GC), "conv")
            load(vw[:, :], groups(t_in["L0_conv_v_w"], 0, G, GC), "conv")
            load(vb, bc(t_in["L0_conv_v_b"][0:RC_], RC_, 96), "conv")
            load(vbias_d[:, :], bc(t_in["L0_conv_v_b"][RC_:], ND * GC), "conv")
            load(qbias_off[:, :, :, :].rearrange("p g k d -> p (g k d)"), bc(t_in["L0_conv_qd_b"][0:2 * GK], 2 * GK),
                 "conv")
            load(prior_b[:, :, :].rearrange("p k d -> p (k d)"),
                 bc(t_in["L0_conv_prior"].rearrange("a b c d k x -> (a b c d k x)"), 2 * K), "conv")
            dscale = t_in["L0_conv_dscale"].rearrange("a b c g k x -> (a b c g k x)")
            load(dscale_b[:, :], bc(dscale[0:G], G), "conv")
            load(qbias_rest[:, 1, :, :].rearrange("p g k -> p (g k)"), bc(t_in["L0_conv_qw_b"][0:GK], GK), "conv")
            load(outb_b[:, :], bc(t_in["L0_conv_out_b"], C), "conv")
            load(wqd_raw[:, 0:2 * ND * K], groups(t_in["L0_conv_qd_w"], G, GALL, 2 * K))
            load(wqd_raw[:, 2 * ND * K:3 * ND * K], groups(t_in["L0_conv_qs_w"], G, GALL, K))
            load(wqd_raw[:, 3 * ND * K:4 * ND * K], groups(t_in["L0_conv_qw_w"], G, GALL, K))
            with nc.allow_non_contiguous_dma(reason="biases of the dense groups, a hundred numbers"):
                for g in range(ND):
                    load(bias9[:, g, 0:2],
                         t_in["L0_conv_qd_b"][(G + g) * 2 * K:(G + g + 1) * 2 * K].rearrange("(k d) -> k d", d=2))
                    load(bias9[:, g, 3:4], t_in["L0_conv_qw_b"][(G + g) * K:(G + g + 1) * K]
                         .rearrange("(k o) -> k o", o=1))
                load(prior9[:, :], t_in["L0_conv_prior"].rearrange("a b c d k x -> (a b c d k) x"))
                load(dscale9[:, :], bc(dscale[G:GALL], ND, K))
            load(outw_a[:, :], t_in["L0_conv_out_w"][0:P, :])
            load(outw_b[:, :], t_in["L0_conv_out_w"][P:RC_, :])
            for d in range(NI):
                load(outw_d[d * GC:(d + 1) * GC, :, :],
                     t_in["L0_conv_out_w"][RC_:, :].rearrange("(g c) o -> c g o", g=ND))
            for b in range(B):
                sp.dma_start(x_tok[:, b * NT:(b + 1) * NT, :], x_d[b]).then_inc(s.x_tok_loaded, 16)

            def load_attention_and_experts():
                load(boutb_b[:, :], bc(t_in["L1_attn_b_out"], C))
                load(bx_b[:, :], bc(t_in["L1_attn_b_x"], 256))
                with nc.allow_non_contiguous_dma(reason="bias columns of a few hundred numbers"):
                    load(bx_col[:, :], t_in["L1_attn_b_x"].rearrange("(h p) -> p h", p=P))
                    for h in range(HG):
                        load(bslice_raw[h * S:(h + 1) * S, :], t_in["L1_attn_b_slice"].rearrange("(p o) -> p o", o=1))
                        load(wt_col[h * S:(h + 1) * S, :], t_in["L1_attn_W_temp"].rearrange("o p -> p o"))
                load(btemp_col[:, :], bc(t_in["L1_attn_b_temp"], 1))
                load(wx_raw, t_in["L1_attn_W_x"].rearrange("(h p) c -> p h c", p=P))
                load(wout_raw, t_in["L1_attn_W_out"])
                for h in range(HG):
                    load(ws_raw[h * S:(h + 1) * S, :].rearrange("p (j d) -> p j d", j=HG),
                         t_in["L1_attn_W_slice"].rearrange("g (o d) -> g o d", o=1).broadcast_to([S, HG, DH]))
                load(wr[:, :], t_in["L1_ffn_Wr"])
                load(br_b[:, :], bc(t_in["L1_ffn_br"], E))
                load(lng, t_in["L1_ffn_ln_g"])
                load(lnb, t_in["L1_ffn_ln_b"])
                load(w1[:, :, :], t_in["L1_ffn_W1"].rearrange("e d h -> d e h"))
                load(b1_raw, t_in["L1_ffn_b1"].rearrange("e (j p) -> (e j) p", p=P))
                load(w2[:, :, :], t_in["L1_ffn_W2"].rearrange("e (j p) d -> p (e j) d", p=P))
                load(b2[:, :], t_in["L1_ffn_b2"])

            for b in range(B):
                if b < B - 1:
                    sp.wait_ge(s.x_transposed, b + 1)
                    sp.dma_start(xin, x_d[b + 1]).then_inc(s.x_loaded, 16)
                sp.wait_ge(s.normalised, b + 1)
                sp.dma_start(xn_dram[b], xnorm).then_inc(s.xnorm_stored, 16)
                sp.wait_ge(s.offsets_copied, NT * (b + 1))
                sp.dma_start(values_dram[b].rearrange("(t p) m -> p t m", p=P), vd_sb).then_inc(s.values_stored, 16)
                store_patches(b)
                if b == 0:
                    load_attention_and_experts()
                    sp.wait_ge(s.dense_consts, SCRATCH_SPENT)
                    for q in range(1, 4):
                        sp.dma_start(EY[32 * q:32 * q + 32, :], EY[0:32, :]).then_inc(s.quarters_copied, 16)
                        sp.dma_start(EX[32 * q:32 * q + 32, :], EX[0:32, :]).then_inc(s.quarters_copied, 16)

            def load_dense(b):
                first_image = isinstance(b, int)
                sp.dma_start(xb, xn_dram[bass.ds(b, 1)].rearrange("o c n -> (o c) n")).then_inc(s.xb_loaded, 16)
                for h in range(2):
                    for g in range(ND):
                        if g or h or not first_image:
                            sp.wait_ge(s.dense_out, (b * 2 + h) * ND + g)
                        v = values_dram[bass.ds(b, 1)].rearrange("o (y x) (g c) -> (o y) x g c", x=WW, g=ND)
                        for i in range(NI):
                            sp.dma_start(vbd[i * GC:(i + 1) * GC, :, i * GC:(i + 1) * GC], v[:, :, g, :])\
                              .then_inc(s.values_loaded, 16)

            sp.wait_ge(s.xnorm_stored, 16 * B)
            sp.wait_ge(s.values_stored, 16 * B)
            sp.wait_ge(s.patches_copied, VALL * B)
            tables_stored(sp)
            sp.wait_ge(s.dense_consts, DENSE_CONSTS)
            load_dense(0)
            with sp.Fori(1, B) as b:
                sp.wait_ge(r.b2_added, b)
                load_dense(b)
                sp.wait_ge(mid.expert_added, E * NT * b)
                sp.dma_start(out_d[bass.ds(b * NT - NT, NT), :, :].rearrange("n p c -> p n c"),
                             tok(b * NT - NT, NT)).then_inc(s.rows_stored, 16)
            for h in range(2):
                T0 = TILES - NT + 4 * h
                sp.wait_ge(end.expert_added, (h + 1) * E * 4)
                sp.dma_start(out_d[T0:T0 + 4, :, :].rearrange("n p c -> p n c"),
                             x_tok[:, T0:T0 + 4, :]).then_inc(s.rows_stored, 16)
            sp.wait_ge(s.rows_stored, 16 * (B - 1 + 2))

        @block.gpsimd
        def _(pl):
            pl.memset(xpad, 0.0).then_inc(s.constants_made, 1)
            pl.memset(ident[:, :], 0.0).then_inc(s.constants_made, 1)
            pl.memset(gn_avg[:, :], 1.0 / GN_GROUP).then_inc(s.constants_made, 1)
            pl.memset(head_mask[:, :], 1.0).then_inc(s.constants_made, 1)
            pl.memset(inside[:, :], 0.0).then_inc(s.constants_made, 1)
            pl.iota(ofs_i[:, :].rearrange("p (g k) -> p g k", g=G), pattern=[[1, G], [0, K]],
                    base=(PITCH + 1) * G, channel_multiplier=0).then_inc(s.constants_made, 1)
            pl.iota(pos_i[:, :, :], pattern=[[P, NT], [0, 2]], base=0, channel_multiplier=1)\
              .then_inc(s.constants_made, 1)
            pl.iota(expert_i[:, :], pattern=[[1, E]], base=0, channel_multiplier=0).then_inc(s.constants_made, 1)
            pl.wait_ge(s.constants_made, 8)
            pl.memset(interior(inside), 1.0).then_inc(s.constants_made, 1)
            pl.affine_select(out=ident[:, :], in_=ident[:, :], compare_op=ALU.not_equal, fill=1.0, base=0,
                             pattern=[[-1, P]], channel_multiplier=1).then_inc(s.constants_made, 1)

            def block_diagonal(m, size, done):
                v = m[:, :].rearrange("p (a c) -> p a c", c=size)
                pl.affine_select(out=v, in_=v, compare_op=ALU.is_ge, fill=0.0, base=0,
                                 pattern=[[-size, P // size], [0, size]], channel_multiplier=1)\
                  .then_inc(s.constants_made, 1)
                pl.wait_ge(s.constants_made, done + 1)
                pl.affine_select(out=v, in_=v, compare_op=ALU.is_ge, fill=0.0, base=size - 1,
                                 pattern=[[size, P // size], [0, size]], channel_multiplier=-1)\
                  .then_inc(s.constants_made, 1)

            block_diagonal(gn_avg, GN_GROUP, 10)
            block_diagonal(head_mask, DH, 12)

            pl.memset(zw[:, :, :, :], 0.0).then_inc(s.dense_consts, 1)
            pl.memset(vbd[:, :, :], 0.0).then_inc(s.dense_consts, 1)
            pl.memset(QY[:, :, :], 0.0).then_inc(s.dense_consts, 1)
            pl.memset(QX[:, :, :], 0.0).then_inc(s.dense_consts, 1)
            pl.memset(quad[:, :], 1.0).then_inc(s.dense_consts, 1)
            pl.iota(r7_i[:, :], pattern=[[-K, TOK - 1]], base=-K, channel_multiplier=1).then_inc(s.dense_consts, 1)
            pl.iota(npos_i, pattern=[[TOK, 2 * SETS]], base=0, channel_multiplier=0).then_inc(s.dense_consts, 1)
            pl.iota(ey_i.rearrange("p (m q) -> p m q", q=HH), pattern=[[0, 16], [-1, HH]], base=-int(BIG),
                    channel_multiplier=0).then_inc(s.dense_consts, 1)
            pl.wait_ge(s.dense_consts, 8)
            pl.tensor_copy(ey_f, ey_i).then_inc(s.dense_consts, 1)
            pl.tensor_copy(ex_f, ey_i).then_inc(s.dense_consts, 1)
            pl.affine_select(out=quad[:, :], in_=quad[:, :], compare_op=ALU.is_ge, fill=0.0, base=0,
                             pattern=[[-GC, NI]], channel_multiplier=1).then_inc(s.dense_consts, 1)
            pl.wait_ge(s.dense_consts, 11)
            pl.affine_select(out=quad[:, :], in_=quad[:, :], compare_op=ALU.is_ge, fill=0.0, base=GC - 1,
                             pattern=[[GC, NI]], channel_multiplier=-1).then_inc(s.dense_consts, 1)
            done = 12
            pl.wait_ge(s.dense_consts, done)
            for e, sets, blocks in ((ey_f, 4, NI), (ex_f, 8, NA)):
                steps = [(ALU.is_equal, 0.0, -3 * sets, [[0, sets], [0, blocks], [0, HH]])]
                steps += [(ALU.not_equal, 1.0, -m * sets, [[-1, sets], [0, blocks], [0, HH]]) for m in range(3)]
                steps += [(ALU.not_equal, BIG, -3 * sets - 1, [[0, sets], [-1, blocks], [0, HH]])]
                for op, fill, base, pattern in steps:
                    v = e.rearrange("p (s b c) -> p s b c", s=sets, b=blocks)
                    pl.affine_select(out=v, in_=v, compare_op=op, fill=fill, base=base, pattern=pattern,
                                     channel_multiplier=1).then_inc(s.dense_consts, 1)
                    done += 1
                    pl.wait_ge(s.dense_consts, done)
            pl.memset(head_pick[:, :], 0.0).then_inc(s.dense_consts, 1)
            for q in range(4):
                done += 1
                pl.wait_ge(s.dense_consts, done)
                v = head_pick[:, :].rearrange("p (j g) -> p j g", g=S)
                pl.affine_select(out=v, in_=v, compare_op=ALU.not_equal, fill=1.0, base=-32 * q,
                                 pattern=[[-S // HG, HG], [0, S]], channel_multiplier=1).then_inc(s.dense_consts, 1)
            done += 1
            assert done == POOL_CONSTS

            pl.wait_ge(s.dense_consts, SCRATCH_SPENT)
            pl.wait_ge(s.bias_parts, 8)
            for b in range(B):
                pl.wait_ge(s.patch_rows_even, 16 * (VT + 1) // 2 * (b + 1))
                pl.wait_ge(s.patch_rows_odd, 16 * (VT // 2) * (b + 1))
                with pl.Fori(0, NT) as t:
                    for g in range(G):
                        pl.wait_ge(s.idx_ready, G * (NT * b + t) + g + 1)
                        own_wait(pl)
                        for k in range(K):
                            pl.indirect_dma_start(
                                ring[:, g, k * 4 * GC:(k + 1) * 4 * GC], None, tables[b],
                                bass.IndirectOffsetOnAxis(
                                    ap=idx_now[:, g * K + k:g * K + k + 1].bitcast(U32), axis=0))\
                              .then_inc(gathered[g], 16)

        @block.tensor
        def _(pe):
            pe.wait_ge(s.constants_made, 14)

            def prep(b):
                pe.wait_ge(s.x_loaded, 16 * (b + 1))
                pe.wait_ge(s.padded, b)
                for t in range(NT):
                    last = pe.transpose(pcol(0, t), xin[:, t, :], ident[:, :])
                last.then_inc(s.x_transposed, 1)
                pe.wait_ge(s.channel_stats, b + 1)
                pe.matmul(ps[:, 2, 0:1], gn_avg[:, :], gn_mv[:, 0:1], start=True, stop=True)\
                  .then_inc(s.group_mean, 1)
                pe.wait_ge(s.spread, b + 1)
                pe.matmul(ps[:, 2, 1:2], gn_avg[:, :], gn_spread[:, :], start=True, stop=True)\
                  .then_inc(s.group_var, 1)
                pe.wait_ge(s.normalised, b + 1)
                for t in range(NT):
                    pe.wait_ge(s.offsets_copied, NT * b + (t - 1 if t >= 2 else 0))
                    pe.matmul(ps[:, 3 + t % 2, 0:4 * GK + ND * GC], xnorm[:, t * P:(t + 1) * P],
                              wq[:, :], start=True, stop=True).then_inc(s.offsets_summed, 1)
                for i in range(VALL):
                    pe.wait_ge(s.patches_copied, VALL * b + (i - 2 if i >= 3 else 0))
                    if i == 0:
                        pe.wait_ge(s.padded, b + 1)
                    r0 = (PROWS * (i // 2) + i % 2) * PITCH
                    for dx in range(2):
                        o = ps[0:VM, 5 + i % 3, dx * RC_:(dx + 1) * RC_]
                        pe.matmul(o, xpad[:, r0 + dx:r0 + dx + VM], vw[:, :], start=(dx == 0), stop=False,
                                  skip_group_check=True)
                        last = pe.matmul(o, inside[:, r0 + dx:r0 + dx + VM], vb_rows[:, :],
                                         start=False, stop=True, skip_group_check=True)
                    last.then_inc(s.patches_summed, 1)

            def turn_weights(images):
                pe.wait_ge(s.weights_loaded, 16 * loads["rest"])
                pe.wait_ge(s.padded, images)
                pe.wait_ge(s.offsets_copied, images * NT)
                pe.wait_ge(s.patches_copied, images * VALL)
                for h in range(2):
                    pe.transpose(ps[:, 0, h * P:(h + 1) * P], wx_raw[:, h, :], ident[:, :])
                    last = pe.transpose(ps[:, 1, h * P:(h + 1) * P], wout_raw[:, h * P:(h + 1) * P], ident[:, :])
                last.then_inc(s.weights_turned, 1)
                pe.transpose(ps[:, 2, 0:P], ws_raw, ident[:, :]).then_inc(s.slice_turned, 1)
                pe.transpose(ps[:, 3, 0:E], lng, ident[0:E, 0:E])
                pe.transpose(ps[:, 3, E:2 * E], lnb, ident[0:E, 0:E])
                pe.transpose(ps[:, 3, 64:64 + EJ], b1_raw, ident[0:EJ, 0:EJ]).then_inc(s.ffn_turned, 1)
                pe.wait_ge(s.ln_cols_copied, 3)
                for i in range(EJ):
                    last = pe.matmul(ps[:, 4, i:i + 1], w1[:, i // HJ, (i % HJ) * P:(i % HJ + 1) * P],
                                     lnbT[:, i // HJ:i // HJ + 1], start=True, stop=True)
                last.then_inc(s.ffn_bias_summed, 1)
                pe.wait_ge(s.quarters_copied, 16 * 6)
                pe.wait_ge(s.dense_consts, DENSE_CONSTS)
                pe.matmul(ps[0:R, 5, 0:4 * ND], rep9[:, :, :].rearrange("k b j -> k (b j)"),
                          bias9[:, :, :].rearrange("k g q -> k (g q)"), start=True, stop=True)\
                  .then_inc(s.row_bias_summed, 1)
                pe.wait_ge(s.turned_copied, 2)
                pe.wait_ge(s.row_bias_copied, 1)
                pe.wait_ge(s.setup_done, 1)

            def conv_turn(T, bank):
                pe.wait_ge(s.reduced, G * (T + 1))
                pe.transpose(ps[:, bank, 0:P], red[:, 0:P], ident[:, :])
                pe.transpose(ps[0:RC_ - P, bank, P:2 * P], red[:, P:RC_], ident[:, :]).then_inc(s.red_turned, 1)

            def conv_project(T, bank):
                pe.wait_ge(s.redT_copied, 2 * (T + 1))
                pe.wait_ge(s.conv_added, T)
                pe.matmul(ps[:, bank, 0:C], redT[:, 0, :], outw_a[:, :], start=True, stop=False)
                pe.matmul(ps[:, bank, 0:C], redT[0:RC_ - P, 1, :], outw_b[:, :], start=False, stop=True)\
                  .then_inc(s.conv_summed, 1)

            def conv_tile(T):
                conv_turn(T, 1)
                conv_project(T, 2)

            def dense_step(b, h, step, T, u, with_experts):
                g, t = step // 2, 4 * h + step
                v = (b * 2 + h) * ND + g
                pe.wait_ge(s.xb_loaded, 16 * (b + 1))
                x_sets = xb[:, bass.ds(h * HALF, HALF)].rearrange("p (s e) -> p s e", e=TOK)
                for q in range(4):
                    for k in range(TOK):
                        first = (R - K) - K * k
                        last = pe.matmul(ps[0:R, 3, q * SETS:(q + 1) * SETS], zw[:, g, q, first:first + R],
                                         x_sets[:, :, k], start=(k == 0), stop=(k == TOK - 1))
                last.then_inc(s.rows_summed, 1)
                if with_experts:
                    pe.wait_ge(s.conv_added, T + (0, 1, 1, 2)[step])
                    tile_up(u, 0, UP_BANKS[0], t)
                pe.wait_ge(s.parts_made, v + 1)
                lps = ps[:, 4, :].bitcast(BF16)
                for i in range(4):
                    pe.transpose(lps[:, i * R:(i + 1) * R], QY[:, 4 * i:4 * i + 4, :].rearrange("p q n -> p (q n)"),
                                 ident_bf[0:R, 0:R])
                for i in range(2):
                    last = pe.transpose(lps[:, (4 + i) * R:(5 + i) * R],
                                        QX[:, 4 * i:4 * i + 4, :].rearrange("p q n -> p (q n)"), ident_bf[0:R, 0:R])
                last.then_inc(s.parts_turned, 1)
                pe.wait_ge(s.parts_copied, v + 1)
                pe.wait_ge(s.dense_added, v)

                def distances(m):
                    if m:
                        pe.wait_ge(s.x_taken, 8 * v + m)
                    q = 32 * (m % 4)
                    pe.matmul(ps[0:R, X_BANK, :], L[q:q + 32, 4 + m // 4, :], EX[q:q + 32, :], start=True, stop=True)\
                      .then_inc(s.dx_summed, 1)
                    for j in (2 * m, 2 * m + 1):
                        if j >= 2:
                            pe.wait_ge(s.y_ready, 16 * v + j - 1)
                        q = 32 * (j % 4)
                        pe.matmul(ps[0:R, Y_BANKS[j % 2], :], L[q:q + 32, j // 4, :], EY[q:q + 32, :],
                                  start=True, stop=True).then_inc(s.dy_summed, 1)

                distances(0)
                for m in range(8):
                    if m < 7:
                        distances(m + 1)
                    pe.wait_ge(s.x_ready, 8 * v + m + 1)
                    pe.wait_ge(s.y_ready, 16 * v + 2 * m + 2)
                    if m >= 2:
                        pe.wait_ge(s.a_taken, 8 * v + m - 1)
                    for e in range(8):
                        last = pe.matmul(ps[:, A_BANKS[m % 2], e * 64:(e + 1) * 64],
                                         ysb[:, (2 * m + e // 4) % 4, e % 4, :], xsb[:, m % 2, e, :],
                                         start=True, stop=True)
                    last.then_inc(s.a_summed, 1)
                    if with_experts:
                        tile_down(u, m)
                        if m < 7:
                            tile_up(u, m + 1, UP_BANKS[0], t)
                    if step == 2 and m == 4:
                        conv_turn(T + 1, OUT_BANK)
                    if step == 2 and m == 5:
                        conv_project(T + 1, OUT_BANK)
                pe.wait_ge(s.a_taken, 8 * v + 8)
                pe.wait_ge(s.values_loaded, 16 * NI * (v + 1))
                if step == 2:
                    pe.wait_ge(s.conv_added, T + 2)
                for q in range(WW):
                    last = pe.matmul(ps[:, OUT_BANK, 0:P], vbd[:, q, :], asb[:, q, :],
                                     start=(q == 0), stop=(q == WW - 1))
                last.then_inc(s.dense_out, 1)
                if step == 0:
                    if with_experts:
                        pe.wait_ge(mid.expert_added, E * u + E)
                    conv_tile(T)
                pe.wait_ge(s.spread_made, v + 1)
                for i in range(4):
                    last = pe.matmul(ps[:, SUM_BANK, i * P:(i + 1) * P], osp[:, i * P:(i + 1) * P], outw_d[:, g, :],
                                     start=True, stop=True)
                last.then_inc(s.dense_summed, 1)

            def attention(b, next_image):
                pe.wait_ge(s.tile_normalised, b + 1)
                for t in range(NT):
                    last = pe.transpose(pcol(3, t), tn_tok[:, t, :], ident[:, :])
                last.then_inc(s.tn_turned, 1)
                pe.wait_ge(s.tnT_copied, b + 1)
                for h in range(2):
                    pe.wait_ge(s.xpT_copied, 2 * b + h)
                    for c in range(2):
                        last = pe.matmul(ps[:, 5 + c, :], wxT[:, h * P:(h + 1) * P], tnT[:, c * 512:(c + 1) * 512],
                                         start=True, stop=True)
                    last.then_inc(s.xpT_summed, 1)
                pe.wait_ge(s.xpT_copied, 2 * b + 2)
                for i in range(4):
                    h, c = i // 2, i % 2
                    last = pe.matmul(ps[32 * i:32 * i + 32, 7, :],
                                     wt_bd[:, :].rearrange("p (m f) -> p m f", f=HG)[:, :, 0],
                                     xpT[:, h, c * 512:(c + 1) * 512], start=True, stop=True)
                last.then_inc(s.temps_summed, 1)
                for t in range(NT):
                    last = pe.matmul(ps[:, 3 + t // 2, (t % 2) * 256:(t % 2 + 1) * 256],
                                     tnT[:, t * P:(t + 1) * P], wxT[:, :], start=True, stop=True)
                last.then_inc(s.xp_summed, 1)
                pe.wait_ge(s.xp_copied, b + 1)
                pe.wait_ge(s.rtemp_ready, b + 1)
                for i in range(4):
                    h, c = i // 2, i % 2
                    if i >= 2:
                        pe.wait_ge(s.logits_done, 4 * b + i - 1)
                    pe.matmul(ps[:, 3 + 2 * (i % 2), :], ws_bd[:, :], xpT[:, h, c * 512:(c + 1) * 512],
                              start=True, stop=True)
                    pe.matmul(ps[:, 4 + 2 * (i % 2), :], head_pick[32 * i:32 * i + 32, :], rtemp[32 * i:32 * i + 32, :],
                              start=True, stop=True).then_inc(s.logits_summed, 1)
                pe.wait_ge(s.exp_done, 2 * b + 2)
                for t in range(NT):
                    for h in range(2):
                        last = pe.transpose(ps[:, 3 + t // 2, ((t % 2) * 2 + h) * P:((t % 2) * 2 + h + 1) * P],
                                            eT[:, h, t * P:(t + 1) * P], ident[:, :])
                last.then_inc(s.e_turned, 1)
                pe.wait_ge(s.e_copied, b + 1)
                for h in range(2):
                    for t in range(NT):
                        last = pe.matmul(ps[:, 7, h * P:(h + 1) * P], xp_tok[:, t, h * P:(h + 1) * P],
                                         e_tok[:, t, h * P:(h + 1) * P], start=(t == 0), stop=(t == NT - 1))
                last.then_inc(s.slice_sums, 1)
                if next_image:
                    conv_tile(NT * (b + 1))
                pe.wait_ge(s.bdE_done, b + 1)
                for h in range(2):
                    last = pe.matmul(ps[:, 3, h * P:(h + 1) * P], bdE[:, h, :], woutT[:, h, :], start=True, stop=True)
                last.then_inc(s.M_summed, 1)
                pe.wait_ge(s.M_copied, 2 * b + 2)
                for t in range(NT):
                    for h in range(2):
                        last = pe.matmul(pcol(5, t), eT[:, h, t * P:(t + 1) * P], Msb[:, h, :],
                                         start=(h == 0), stop=(h == 1))
                last.then_inc(s.attn_out, 1)

            def route(b, next_image, between=lambda: None):
                pe.wait_ge(s.en_chain, 4 * b + 3)
                for t in range(NT):
                    pe.transpose(pcol(3, t), tn_tok[:, t, :], ident[:, :])
                pe.wait_ge(r.xn_ready, b + 1)
                for t in range(NT):
                    last = pe.transpose(pcol(5, t), xn_tok[:, t, :], ident[:, :])
                last.then_inc(r.turned, 1)
                pe.wait_ge(r.turned_copied, 2 * (b + 1))
                for t in range(NT):
                    last = pe.matmul(ps[:, 7, t * E:(t + 1) * E], xtT[:, t * P:(t + 1) * P], wr[:, :],
                                     start=True, stop=True)
                last.then_inc(r.router_summed, 1)
                between()
                pe.wait_ge(r.gate_done, b + 1)
                for t in range(NT):
                    last = pe.transpose(ps[0:E, 3 + t // 4, (t % 4) * P:(t % 4 + 1) * P], gate[:, t, :], ident[:, :])
                last.then_inc(r.gate_turned, 1)
                pe.wait_ge(r.gateT_copied, b + 1)
                for t in range(NT):
                    last = pe.matmul(pcol(3, t), gateT[:, t * P:(t + 1) * P], b2[:, :], start=True, stop=True)
                last.then_inc(r.b2_summed, 1)
                if next_image:
                    conv_tile(NT * (b + 1) + 1)
                pe.wait_ge(r.b2_added, b + 1)
                own_wait(pe)

            def tile_up(u, e, bank, t):
                for j in range(HJ):
                    last = pe.matmul(ps[:, bank, j * P:(j + 1) * P], w1[:, e, j * P:(j + 1) * P],
                                     xnT[:, bass.ds(t * P, P)],
                                     start=True, stop=True)
                last.then_inc(mid.hidden_summed, 1)

            def tile_down(u, e):
                if e:
                    pe.wait_ge(mid.expert_added, E * u + e)
                for j in range(HJ):
                    pe.wait_ge(mid.hidden_ready, HJ * (E * u + e) + j + 1)
                    last = pe.matmul(ps[:, TILE_BANK, 0:C], tile_hT[:, e % 2, j, :], w2[:, e * HJ + j, :],
                                     start=(j == 0), stop=(j == HJ - 1))
                last.then_inc(mid.expert_summed, 1)

            def tile_experts(u, t):
                tile_up(u, 0, UP_BANKS[0], t)
                for e in range(E):
                    if e < E - 1:
                        tile_up(u, e + 1, UP_BANKS[(e + 1) % 2], t)
                    tile_down(u, e)
                pe.wait_ge(mid.expert_added, E * u + E)

            def plain_step(h, step, T, u, with_experts):
                if with_experts:
                    pe.wait_ge(s.conv_added, T + (0, 1, 1, 2)[step])
                    tile_experts(u, 4 * h + step)
                if step == 3:
                    conv_tile(T + 2)

            f, ntok, hT = end, 512, end_hT
            tiles = ntok // P
            units = [(c, e) for c in range(NT // tiles) for e in range(E)]

            def up(i):
                c, e = units[i]
                for j in range(HJ):
                    m = i * HJ + j
                    if m >= 2:
                        pe.wait_ge(f.hidden_ready, m - 1)
                    pe.matmul(ps[:, 5 + m % 2, 0:ntok], w1[:, e, j * P:(j + 1) * P],
                              xnT[:, c * ntok:(c + 1) * ntok], start=True, stop=True).then_inc(f.hidden_summed, 1)

            def down(i):
                c, e = units[i]
                for t in range(tiles):
                    m = i * tiles + t
                    if m >= 2:
                        pe.wait_ge(f.expert_added, m - 1)
                    for j in range(HJ):
                        if t == 0:
                            pe.wait_ge(f.hidden_ready, i * HJ + j + 1)
                        last = pe.matmul(ps[:, Y_BANK[m % 2], 0:C], hT[:, i % 2, j, t * P:(t + 1) * P],
                                         w2[:, e * HJ + j, :], start=(j == 0), stop=(j == HJ - 1))
                    last.then_inc(f.expert_summed, 1)

            def image_experts():
                for i in range(1, len(units)):
                    up(i)
                    down(i - 1)
                down(len(units) - 1)

            pe.wait_ge(s.conv_weights_loaded, 16 * loads["conv"])
            pe.wait_ge(s.bias_parts, 8)
            prep(0)
            for b in range(1, B):
                prep(b)
                if b == EARLY:
                    turn_weights(b + 1)
                if b <= EARLY:
                    conv_tile(b - 1)
                    pe.wait_ge(s.conv_added, b)

            def image(b, with_experts):
                with pe.Fori(0, 2) as h:
                    T = b * NT + EARLY + 3 * h
                    for step in range(4):
                        u = b * NT - NT + 4 * h + step
                        if step % 2 == 0:
                            dense_step(b, h, step, T, u, with_experts)
                        else:
                            plain_step(h, step, T, u, with_experts)

            pe.wait_ge(s.offsets_copied, B * NT)
            pe.wait_ge(s.patches_copied, B * VALL)
            image(0, False)
            with pe.Fori(1, B) as b:
                attention(b - 1, True)
                route(b - 1, True)
                image(b, True)
            attention(B - 1, False)
            route(B - 1, False, between=lambda: up(0))
            image_experts()

        @block.scalar
        def _(act):
            def prep(b):
                act.wait_ge(s.group_var, b + 1)
                act.activation(gn_std[:, :], ps[:, 2, 1:2], ACT.Sqrt, bias=eps_col[:, :]).then_inc(s.group_std, 1)
                act.wait_ge(s.offsets_copied, NT * (b + 1))
                act.activation(sig, q_rest[:, 0, :, :].rearrange("p t m -> p (t m)"), ACT.Sigmoid)\
                   .then_inc(s.sigmoid_done, 1)
                for i in range(VALL):
                    v, dy = i // 2, i % 2
                    act.wait_ge(s.patches_summed, VALL * b + i + 1)
                    if dy == 0:
                        if v % 2 == 0:
                            act.wait_ge(s.patch_rows_even, 16 * ((VT + 1) // 2 * b + v // 2))
                        else:
                            act.wait_ge(s.patch_rows_odd, 16 * (VT // 2 * b + v // 2))
                    act.activation(vrows[0:VM, v % 2, :, 2 * dy:2 * dy + 2, :].rearrange("p g d c -> p d g c"),
                                   ps[0:VM, 5 + i % 3, 0:2 * RC_].rearrange("p (d g c) -> p d g c", d=2, g=G),
                                   ACT.Copy).then_inc(s.patches_copied, 1)

            def turn_weights():
                act.wait_ge(s.weights_turned, 1)
                act.activation(wxT[:, :], ps[:, 0, 0:256], ACT.Copy).then_inc(s.turned_copied, 1)
                act.activation(woutT[:, :, :].rearrange("p h c -> p (h c)"), ps[:, 1, 0:256], ACT.Copy)\
                   .then_inc(s.turned_copied, 1)
                act.wait_ge(s.ffn_turned, 1)
                act.activation(lnbT[:, :], ps[:, 3, E:2 * E], ACT.Copy).then_inc(s.ln_cols_copied, 1)
                act.activation(lngT[:, :], ps[:, 3, 0:E], ACT.Copy).then_inc(s.ln_cols_copied, 1)
                act.activation(b1_turned[:, :], ps[:, 3, 64:64 + EJ], ACT.Copy).then_inc(s.ln_cols_copied, 1)
                act.wait_ge(s.row_bias_summed, 1)
                act.activation(row_bias[:, :, :].rearrange("p g q -> p (g q)"), ps[0:R, 5, 0:4 * ND], ACT.Copy)\
                   .then_inc(s.row_bias_copied, 1)

            def conv_tile(T, bank=1):
                act.wait_ge(s.red_turned, T + 1)
                act.activation(redT[:, 0, :], ps[:, bank, 0:P], ACT.Copy).then_inc(s.redT_copied, 1)
                act.activation(redT[0:RC_ - P, 1, :], ps[0:RC_ - P, bank, P:2 * P], ACT.Copy)\
                   .then_inc(s.redT_copied, 1)

            def route(b, next_image, between=lambda: None):
                act.wait_ge(r.turned, b + 1)
                for dst, bank in ((xtT, 3), (xnT, 5)):
                    act.activation(dst, ps[:, bank:bank + 2, :].rearrange("p a n -> p (a n)"), ACT.Copy)\
                       .then_inc(r.turned_copied, 1)
                act.wait_ge(r.router_chain, (2 * NT + 2) * (b + 1))
                act.activation(g_e[:, :], g_d[:, :], ACT.Exp).then_inc(r.exp_ready, 1)
                between()
                act.wait_ge(r.gate_turned, b + 1)
                act.activation(gateT, ps[0:E, 3:5, :].rearrange("p a n -> p (a n)"), ACT.Copy)\
                   .then_inc(r.gateT_copied, 1)
                if next_image:
                    conv_tile(NT * (b + 1) + 1)

            def tile_gelu(u, e, bank):
                if e >= 2:
                    act.wait_ge(mid.expert_summed, E * u + e - 1)
                act.wait_ge(mid.hidden_summed, E * u + e + 1)
                for j in range(HJ):
                    act.activation(tile_hT[:, e % 2, j, :], ps[:, bank, j * P:(j + 1) * P], ACT.Gelu,
                                   bias=b1_col[:, e * HJ + j:e * HJ + j + 1]).then_inc(mid.hidden_ready, 1)

            def tile_experts(u):
                for e in range(E):
                    tile_gelu(u, e, UP_BANKS[e % 2])

            def plain_step(h, step, T, u, with_experts):
                if with_experts:
                    tile_experts(u)
                if step == 3:
                    conv_tile(T + 2)

            def dense_step(b, h, step, T, u, with_experts):
                g = step // 2
                v = (b * 2 + h) * ND + g
                act.wait_ge(s.rows_summed, v + 1)
                act.activation(r_sig, ps[0:R, 3, 2 * SETS:3 * SETS], ACT.Sigmoid, bias=row_bias[:, g, 2:3])\
                   .then_inc(s.row_sigmoid, 1)
                if with_experts:
                    tile_gelu(u, 0, UP_BANKS[0])
                act.wait_ge(s.parts_turned, v + 1)
                act.activation(L[:, :, :].rearrange("p i r -> p (i r)"), ps[:, 4, :].bitcast(BF16)[:, 0:6 * R],
                               ACT.Copy).then_inc(s.parts_copied, 1)

                def weights(m):
                    act.wait_ge(s.dx_summed, 8 * v + m + 1)
                    d = ps[0:R, X_BANK, :]
                    act.activation(d, d, ACT.Abs).then_inc(s.x_chain, 1)
                    act.wait_ge(s.x_chain, 8 * v + m + 1)
                    if m >= 2:
                        act.wait_ge(s.a_summed, 8 * v + m - 1)
                    act.activation(xsb[:, m % 2, :, :].rearrange("p s n -> p (s n)"), d, ACT.Relu, bias=1.0,
                                   scale=-1.0).then_inc(s.x_taken, 1)
                    for j in (2 * m, 2 * m + 1):
                        act.wait_ge(s.dy_summed, 16 * v + j + 1)
                        d = ps[0:R, Y_BANKS[j % 2], :]
                        act.activation(d, d, ACT.Abs).then_inc(s.y_chain, 1)
                        act.wait_ge(s.y_chain, 16 * v + j + 1)
                        if j >= 4:
                            act.wait_ge(s.a_summed, 8 * v + (j - 4) // 2 + 1)
                        act.activation(ysb[:, j % 4, :, :].rearrange("p s n -> p (s n)"), d, ACT.Relu, bias=1.0,
                                       scale=-1.0).then_inc(s.y_ready, 1)

                weights(0)
                for m in range(1, 8):
                    weights(m)
                    if with_experts:
                        tile_gelu(u, m, UP_BANKS[0])
                    if step == 2 and m == 5:
                        conv_tile(T + 1, OUT_BANK)
                if step == 0:
                    conv_tile(T)

            def attention(b, next_image):
                act.wait_ge(s.ln_stats, b + 1)
                act.activation(f_sd[:, :], f_mv[:, :, 1], ACT.Sqrt, bias=eps_col[:, :]).then_inc(s.ln_std, 1)
                act.wait_ge(s.tn_turned, b + 1)
                act.activation(tnT, ps[:, 3:5, :].rearrange("p a n -> p (a n)"), ACT.Copy).then_inc(s.tnT_copied, 1)
                for h in range(2):
                    act.wait_ge(s.xpT_summed, 2 * b + h + 1)
                    act.activation(xpT[:, h, :], ps[:, 5:7, :].rearrange("p a n -> p (a n)"), ACT.Identity,
                                   bias=bx_col[:, h:h + 1]).then_inc(s.xpT_copied, 1)
                for i in range(4):
                    h, c = i // 2, i % 2
                    act.wait_ge(s.logits_summed, 4 * b + i + 1)
                    act.activation(eT[:, h, c * 512:(c + 1) * 512], ps[:, 3 + 2 * (i % 2), :], ACT.Identity,
                                   bias=bslice_col[:, :]).then_inc(s.logits_biased, 1)
                for h in range(2):
                    act.wait_ge(s.max_done, 2 * b + h + 1)
                    act.activation(eT[:, h, :], eT[:, h, :], ACT.Exp, bias=a_nmax[:, h:h + 1],
                                   accum_out=a_sum[:, h:h + 1]).then_inc(s.exp_done, 1)
                act.wait_ge(s.e_turned, b + 1)
                act.activation(e_tok.rearrange("p t c -> p (t c)"), ps[:, 3:7, :].rearrange("p a n -> p (a n)"),
                               ACT.Copy).then_inc(s.e_copied, 1)
                if next_image:
                    conv_tile(NT * (b + 1))
                act.wait_ge(s.M_summed, b + 1)
                act.wait_ge(s.scale_done, b + 1)
                for h in range(2):
                    act.activation(Msb[:, h, :], ps[:, 3, h * P:(h + 1) * P], ACT.Copy, scale=a_sc[:, h:h + 1])\
                       .then_inc(s.M_copied, 1)
                act.wait_ge(s.en_stats1, b + 1)
                act.activation(f_sd[:, :], norms[:, :, 1], ACT.Sqrt, bias=eps_col[:, :]).then_inc(s.en_std1, 1)
                act.wait_ge(s.en_stats2, b + 1)
                act.activation(f_sd[:, :], norms[:, :, 3], ACT.Sqrt, bias=eps_col[:, :]).then_inc(s.en_std2, 1)

            f, ntok, hT = end, 512, end_hT
            tiles = ntok // P
            units = [(c, e) for c in range(NT // tiles) for e in range(E)]

            def gelu(i):
                c, e = units[i]
                if i >= 2:
                    act.wait_ge(f.expert_summed, (i - 1) * tiles)
                for j in range(HJ):
                    m = i * HJ + j
                    act.wait_ge(f.hidden_summed, m + 1)
                    act.activation(hT[:, i % 2, j, 0:ntok], ps[:, 5 + m % 2, 0:ntok], ACT.Gelu,
                                   bias=b1_col[:, e * HJ + j:e * HJ + j + 1]).then_inc(f.hidden_ready, 1)

            def image_experts():
                for i in range(1, len(units)):
                    gelu(i)

            act.wait_ge(s.small_constants, 7)
            prep(0)
            for b in range(1, B):
                prep(b)
                if b == EARLY:
                    turn_weights()
                    act.wait_ge(s.setup_done, 1)
                    act.wait_ge(s.row_bias_copied, 1)
                if b <= EARLY:
                    conv_tile(b - 1)
            tables_stored(act)

            def image(b, with_experts):
                with act.Fori(0, 2) as h:
                    T = b * NT + EARLY + 3 * h
                    for step in range(4):
                        u = b * NT - NT + 4 * h + step
                        if step % 2 == 0:
                            dense_step(b, h, step, T, u, with_experts)
                        else:
                            plain_step(h, step, T, u, with_experts)

            image(0, False)
            with act.Fori(1, B) as b:
                attention(b - 1, True)
                route(b - 1, True)
                image(b, True)
            attention(B - 1, False)
            route(B - 1, False, between=lambda: gelu(0))
            image_experts()

        @block.vector
        def _(dve):
            def chain(sem, ins, value):
                ins.then_inc(sem, 1)
                dve.wait_ge(sem, value)

            def small_constants():
                dve.memset(eps_col[:, :], EPS).then_inc(s.small_constants, 1)
                dve.memset(idx_all[:, TILES, :], 0).then_inc(s.small_constants, 1)
                dve.wait_ge(s.constants_made, 14)
                dve.tensor_copy(ofs[:, :], ofs_i[:, :]).then_inc(s.small_constants, 1)
                dve.tensor_copy(expert_no[:, :], expert_i[:, :]).then_inc(s.small_constants, 1)
                dve.tensor_scalar(pos_b[:, :, 0], pos_i[:, :, 0], WW - 1, None, ALU.bitwise_and)\
                   .then_inc(s.small_constants, 1)
                chain(s.small_constants, dve.tensor_scalar(pos_b[:, :, 1], pos_i[:, :, 1], 5, None,
                                                           ALU.logical_shift_right), 6)
                chain(s.small_constants, dve.tensor_copy(pos[:, :, :], pos_b[:, :, :]), 7)

            def conv_constants():
                dve.wait_ge(s.conv_weights_loaded, 16 * loads["conv"])
                dve.memset(vb_rows[:, :], 0.0).then_inc(s.bias_parts, 1)
                for i in range(3):
                    if i < 2:
                        chain(s.bias_parts, dve.tensor_copy(vb_parts[:, i, :], vb), 2 + 2 * i)
                        chain(s.bias_parts, dve.tensor_tensor(vb, vb, vb_parts[:, i, :], ALU.subtract),
                              3 + 2 * i)
                    else:
                        chain(s.bias_parts, dve.tensor_copy(vb_parts[:, i, :], vb), 6)
                for i in range(3):
                    last = dve.tensor_copy(vb_rows[32 * i:32 * i + 1, :], vb_parts[32 * i:32 * i + 1, i, :])
                last.then_inc(s.bias_parts, 1)
                dve.tensor_tensor(qbias_off[:, :, :, :].rearrange("p g k d -> p g (k d)"),
                                  qbias_off[:, :, :, :].rearrange("p g k d -> p g (k d)"),
                                  prior_b[:, :, :].rearrange("p (o k) d -> p o (k d)", o=1)
                                  .broadcast_to([P, G, 2 * K]), ALU.add)
                chain(s.bias_parts, dve.tensor_copy(
                    qbias_rest[:, 0, :, :],
                    dscale_b[:, :].rearrange("p (g o) -> p g o", o=1).broadcast_to([P, G, K])), 8)

            def prep(b):
                dve.wait_ge(s.x_transposed, b + 1)
                own_wait(dve)
                for c in range(2):
                    last = dve.bn_stats(gn_stats[:, c, :], ps[:, c, :])
                chain(s.gn_chain, last, 4 * b + 1)
                own_wait(dve)
                dve.bn_aggr(gn_mv[:, :], gn_stats[:, :, :].rearrange("p a s -> p (a s)")).then_inc(s.channel_stats, 1)
                dve.wait_ge(s.group_mean, b + 1)
                dve.tensor_copy(gn_mean[:, :], ps[:, 2, 0:1]).then_inc(s.gn_chain, 1)
                dve.wait_ge(s.channel_stats, b + 1)
                chain(s.gn_chain, dve.tensor_tensor(gn_diff[:, :], gn_mv[:, 0:1], ps[:, 2, 0:1], ALU.subtract),
                      4 * b + 3)
                dve.scalar_tensor_tensor(gn_spread[:, :], gn_diff[:, :], gn_diff[:, :], gn_mv[:, 1:2],
                                         ALU.mult, ALU.add).then_inc(s.spread, 1)
                dve.wait_ge(s.group_std, b + 1)
                chain(s.gn_chain, dve.reciprocal(gn_r[:, :], gn_std[:, :]), 4 * b + 4)
                if not (isinstance(b, int) and b == 0):
                    dve.wait_ge(s.math, MATH * b)
                    dve.wait_ge(s.xnorm_stored, 16 * b)
                    dve.wait_ge(s.values_stored, 16 * b)
                dve.tensor_scalar(xnorm, ps[:, 0:2, :].rearrange("p a n -> p (a n)"),
                                  gn_mean[:, :], gn_r[:, :], ALU.subtract, ALU.mult).then_inc(s.normalised, 1)
                dve.wait_ge(s.patches_summed, VALL * b)
                dve.tensor_scalar(interior(xpad), ps[:, 0:2, :].rearrange("p a (h w) -> p (a h) w", w=WW),
                                  gn_mean[:, :], gn_r[:, :], ALU.subtract, ALU.mult).then_inc(s.padded, 1)
                for t in range(NT):
                    dve.wait_ge(s.offsets_summed, NT * b + t + 1)
                    bank = ps[:, 3 + t % 2, :]
                    dve.tensor_tensor(q_off[:, t * 2 * GK:(t + 1) * 2 * GK], bank[:, 0:2 * GK],
                                      qbias_off[:, :, :, :].rearrange("p g k d -> p (g k d)"), ALU.add)
                    dve.tensor_tensor(vd_sb[:, t, :], bank[:, 4 * GK:4 * GK + ND * GC], vbias_d[:, :], ALU.add)
                    dve.tensor_tensor(q_rest[:, :, t, :],
                                      bank[:, 2 * GK:4 * GK].rearrange("p (a m) -> p a m", a=2),
                                      qbias_rest[:, :, :, :].rearrange("p a g k -> p a (g k)"), ALU.add)\
                       .then_inc(s.offsets_copied, 1)
                dve.wait_ge(s.sigmoid_done, b + 1)
                M = NT * GK
                done = [0]

                def math(ins, wait=True):
                    done[0] += 1
                    ins.then_inc(s.math, 1)
                    if wait:
                        dve.wait_ge(s.math, MATH * b + done[0])

                pair = lambda a: a.rearrange("p (m d) -> p m d", d=2)
                tile3 = lambda a: a.rearrange("p (t m d) -> p t m d", t=NT, d=2)
                math(dve.scalar_tensor_tensor(pair(pxy), pair(q_off), MAX_SCALE,
                                              sig.rearrange("p (m o) -> p m o", o=1).broadcast_to([P, M, 2]),
                                              ALU.mult, ALU.mult))
                math(dve.tensor_tensor(tile3(pxy), tile3(pxy),
                                       pos[:, :, :].rearrange("p t (o d) -> p t o d", o=1)
                                       .broadcast_to([P, NT, GK, 2]), ALU.add))
                math(dve.tensor_scalar(pxy, pxy, -1.0, float(WW), ALU.max, ALU.min))
                math(dve.tensor_copy(p_i, pxy))
                math(dve.tensor_tensor(p_f, p_i, pxy, ALU.is_gt))
                math(dve.tensor_tensor(p_f, p_i, p_f, ALU.subtract))
                math(dve.tensor_scalar(p_f, p_f, float(WW - 1), None, ALU.min))
                math(dve.tensor_tensor(p_w1, pxy, p_f, ALU.subtract))
                math(dve.tensor_scalar(p_w0, p_w1, -1.0, 1.0, ALU.mult, ALU.add), wait=False)
                a = pxy[:, 0:M]
                xy = lambda q, d: q.rearrange("p (m d) -> p m d", d=2)[:, :, d]
                math(dve.scalar_tensor_tensor(a, xy(p_f, 1), float(PITCH), xy(p_f, 0), ALU.mult, ALU.add))
                math(dve.tensor_scalar(a, a, float(G), None, ALU.mult))
                math(dve.tensor_tensor(idx_all[:, bass.ds(b * NT, NT), :], a.rearrange("p (t m) -> p t m", t=NT),
                                       ofs[:, :].rearrange("p (o m) -> p o m", o=1).broadcast_to([P, NT, GK]),
                                       ALU.add), wait=False)
                wk = q_rest[:, 1, :, :].rearrange("p t m -> p (t m)")
                u = p_f[:, 0:2 * M].rearrange("p (d m) -> p d m", d=2)
                math(dve.tensor_tensor(u[:, 0, :], wk, xy(p_w0, 1), ALU.mult), wait=False)
                math(dve.tensor_tensor(u[:, 1, :], wk, xy(p_w1, 1), ALU.mult))
                for dy in range(2):
                    for dx in range(2):
                        last = dve.tensor_tensor(
                            w4_all[:, bass.ds(b * NT, NT), :].rearrange("p t (m d) -> p t m d", d=4)
                            [:, :, :, 2 * dy + dx],
                            u[:, dy, :].rearrange("p (t m) -> p t m", t=NT),
                            xy(p_w1 if dx else p_w0, 0).rearrange("p (t m) -> p t m", t=NT), ALU.mult)
                        if dx == 1:
                            math(last, wait=False)
                assert done[0] == MATH

            consts_done = [POOL_CONSTS]

            def step(ins, wait=True):
                consts_done[0] += 1
                ins.then_inc(s.dense_consts, 1)
                if wait:
                    dve.wait_ge(s.dense_consts, consts_done[0])

            def dense_constants():
                dve.wait_ge(s.dense_consts, POOL_CONSTS)
                step(dve.tensor_copy(EY[0:32, :], ey_f), wait=False)
                step(dve.tensor_copy(EX[0:32, :], ex_f), wait=False)
                step(dve.tensor_copy(ident_bf[:, :], ident[:, :]), wait=False)
                step(dve.tensor_scalar(r7[:, :], r7_i[:, :], 0.0, None, ALU.is_ge))
                step(dve.tensor_reduce(blk[:, :], r7[:, :], AX, ALU.add))
                dve.tensor_copy(blk_i[:, 0:1], blk[:, :])
                step(dve.tensor_scalar(npos_i, npos_i, blk[:, :], None, ALU.add))
                dve.tensor_scalar(blk_i[:, 1:2], blk_i[:, 0:1], 1, None, ALU.logical_shift_right)
                dve.tensor_scalar(blk_i[:, 2:3], blk_i[:, 0:1], 1, None, ALU.bitwise_and)
                dve.tensor_scalar(npos_b[:, 0, :], npos_i, WW - 1, None, ALU.bitwise_and)
                step(dve.tensor_scalar(npos_b[:, 1, :], npos_i, 5, None, ALU.logical_shift_right))
                dve.tensor_copy(blk_f[:, :], blk_i[:, 1:3])
                step(dve.tensor_copy(rpos[:, :, :], npos_b))
                assert consts_done[0] == SCRATCH_SPENT, consts_done
                dve.memset(QY[:, :, 12:13], 1.0)
                dve.memset(QX[:, :, 24:25], 1.0)
                no = lambda n, m: expert_no[0:R, 0:n].rearrange("p (o n) -> p o n", o=1).broadcast_to([R, m, n])
                dve.tensor_scalar(QY[:, :, 13:13 + NI], no(NI, SETS // 4), blk_f[:, 0:1], None, ALU.is_equal)
                step(dve.tensor_scalar(QX[:, :, 25:25 + NA], no(NA, SETS // 8), blk_f[:, 1:2], None, ALU.is_equal),
                     wait=False)
                step(dve.tensor_copy(rep9[:, :, :], ident[0:K, 0:K].rearrange("p (o k) -> p o k", o=1)
                                     .broadcast_to([K, TOK, K])), wait=False)

            def dense_weights_laid_out():
                dve.wait_ge(s.weights_loaded, 16 * loads["rest"])
                dve.tensor_copy(bias9[:, :, 2], dscale9[:, :])
                step(dve.tensor_tensor(bias9[:, :, 0:2], bias9[:, :, 0:2],
                                       prior9[:, :].rearrange("k (o d) -> k o d", o=1).broadcast_to([K, ND, 2]),
                                       ALU.add), wait=False)
                nk = ND * K
                dve.tensor_copy(zw[:, :, 0:2, R - K:R].rearrange("p g d k -> p g k d"),
                                wqd_raw[:, 0:2 * nk].rearrange("p (g k d) -> p g k d", g=ND, k=K))
                rest = wqd_raw[:, 2 * nk:4 * nk].rearrange("p (q g k) -> p q g k", q=2, g=ND)
                step(dve.tensor_copy(zw[:, :, 2, R - K:R], rest[:, 0, :, :]), wait=False)
                step(dve.tensor_copy(zw[:, :, 3, R - K:R], rest[:, 1, :, :]))
                assert consts_done[0] == DENSE_CONSTS, consts_done

            def finish_setup():
                dve.wait_ge(s.slice_turned, 1)
                dve.tensor_tensor(ws_bd[:, :], ps[:, 2, 0:P], head_mask[:, :], ALU.mult)
                dve.wait_ge(s.weights_loaded, 16 * loads["rest"])
                dve.tensor_scalar(wt_bd[:, :], head_mask[:, :], wt_col[:, :], None, ALU.mult)
                dve.tensor_scalar(bslice_col[:, :], bslice_raw[:, :], -LOG_NEG_LOG_EPS, None, ALU.add)
                dve.wait_ge(s.ffn_bias_summed, 1)
                dve.tensor_tensor(b1_col[:, :], ps[:, 4, 0:EJ], b1_turned[:, :], ALU.add)
                for e in range(E):
                    last = dve.tensor_scalar(w1[:, e, :], w1[:, e, :], lngT[:, e:e + 1], None, ALU.mult)
                last.then_inc(s.setup_done, 1)

            def conv_group(T, g):
                dve.wait_ge(gathered[g], 16 * K * (T + 1))
                w = w4_all[:, bass.ds(T, 1), g * 4 * K:(g + 1) * 4 * K].rearrange("p o m -> p (o m)")
                slot = ring[:, g, :].rearrange("p (m c) -> p m c", c=GC)
                dve.tensor_tensor(slot, slot, w.rearrange("p (m o) -> p m o", o=1).broadcast_to([P, 4 * K, GC]),
                                  ALU.mult).then_inc(s.products, 1)
                dve.wait_ge(s.products, G * T + g + 1)
                dve.tensor_reduce(red[:, g * GC:(g + 1) * GC], ring[:, g, :].rearrange("p (m c) -> p c m", c=GC),
                                  AX, ALU.add).then_inc(s.reduced, 1)
                dve.tensor_copy(idx_now[:, g * K:(g + 1) * K],
                                idx_all[:, bass.ds(T + 1, 1), g * K:(g + 1) * K].rearrange("p o m -> p (o m)"))\
                   .then_inc(s.idx_ready, 1)

            def conv_add(T, bank=2):
                dve.wait_ge(s.conv_summed, T + 1)
                dve.tensor_tensor(tok(T), tok(T), ps[:, bank, 0:C].rearrange("p (o c) -> p o c", o=1), ALU.add)\
                   .then_inc(s.conv_added, 1)

            def dense_positions(v, g, h):
                done = [0]

                def step(ins):
                    done[0] += 1
                    ins.then_inc(s.row_math, 1)
                    dve.wait_ge(s.row_math, ROW_MATH * v + done[0])

                q = ps[0:R, 3, 0:4 * SETS].rearrange("p (q s) -> p q s", q=4)
                dve.wait_ge(s.rows_summed, v + 1)
                dve.wait_ge(s.row_sigmoid, v + 1)
                dve.tensor_scalar(r_w, q[:, 3, :], row_bias[:, g, 3:4], None, ALU.add)
                for d in range(2):
                    last = dve.scalar_tensor_tensor(r_off[:, d, :], q[:, d, :], row_bias[:, g, d:d + 1], r_sig,
                                                    ALU.add, ALU.mult)
                step(last)
                step(dve.scalar_tensor_tensor(r_pos, r_off, MAX_SCALE, rpos[:, :, bass.ds(h * SETS, SETS)],
                                              ALU.mult, ALU.add))
                step(dve.tensor_scalar(r_pos, r_pos, -2.0, WW + 1.0, ALU.max, ALU.min))
                yv = r_pos[:, 1, :].rearrange("p (m s) -> p m s", s=4)
                xv = r_pos[:, 0, :].rearrange("p (m s) -> p m s", s=8)
                for m in range(3):
                    yq, xq = QY[:, :, 4 * m:4 * m + 4], QX[:, :, 8 * m:8 * m + 8]
                    dve.tensor_copy(yq, yv)
                    if m == 2:
                        dve.tensor_copy(xq, xv).then_inc(s.parts_made, 1)
                        break
                    step(dve.tensor_copy(xq, xv))
                    dve.tensor_tensor(yv, yv, yq, ALU.subtract)
                    step(dve.tensor_tensor(xv, xv, xq, ALU.subtract))
                assert done[0] == ROW_MATH, done

            def dense_mult(v, m):
                dve.wait_ge(s.x_taken, 8 * v + m + 1)
                dve.tensor_tensor(
                    xsb[:, m % 2, :, :], xsb[:, m % 2, :, :],
                    r_w[:, 8 * m:8 * m + 8].rearrange("p (s o) -> p s o", o=1).broadcast_to([R, 8, 64]),
                    ALU.mult).then_inc(s.x_ready, 1)

            def dense_take(v, m):
                dve.wait_ge(s.a_summed, 8 * v + m + 1)
                dve.tensor_copy(asb[:, :, 16 * m:16 * m + 16].rearrange("p q n -> p n q"),
                                ps[:, A_BANKS[m % 2], :].rearrange("p (n q) -> p n q", q=WW))\
                   .then_inc(s.a_taken, 1)

            def dense_spread(v):
                dve.wait_ge(s.dense_out, v + 1)
                dve.tensor_tensor(
                    osp.rearrange("p (s i a) -> p s i a", i=NI, a=NA),
                    ps[:, OUT_BANK, 0:P].rearrange("p (s o a) -> p s o a", o=1, a=NA).broadcast_to([P, SETS, NI, NA]),
                    quad[:, :].rearrange("p (o i u) -> p o i u", o=1, u=1).broadcast_to([P, SETS, NI, NA]),
                    ALU.mult).then_inc(s.spread_made, 1)

            def dense_add(b, h, v, T):
                dve.wait_ge(s.dense_summed, v + 1)
                dve.wait_ge(s.conv_added, T + 1)
                own_wait(dve)
                x4 = tok(b * NT + 4 * h, 4)
                dve.tensor_tensor(x4, x4, ps[:, SUM_BANK, :].rearrange("p (t c) -> p t c", t=4), ALU.add)\
                   .then_inc(s.dense_added, 1)
                dve.wait_ge(s.dense_added, v + 1)

            def tile_gate(u, t):
                dve.wait_ge(mid.expert_added, E * u)
                dve.tensor_copy(gate_now[:, :], gate[:, bass.ds(t, 1), :].rearrange("p o e -> p (o e)"))\
                   .then_inc(mid.gate_picked, 1)
                dve.wait_ge(mid.gate_picked, u + 1)

            def tile_add(u, e):
                dve.wait_ge(mid.expert_summed, E * u + e + 1)
                if e:
                    dve.wait_ge(mid.expert_added, E * u + e)
                x1 = tok(u).rearrange("p o c -> p (o c)")
                dve.scalar_tensor_tensor(x1, ps[:, TILE_BANK, 0:C], gate_now[:, e:e + 1], x1, ALU.mult, ALU.add)\
                   .then_inc(mid.expert_added, 1)

            def plain_step(h, step, T, u, with_experts):
                left = list(STEP_GROUPS[step])
                if with_experts:
                    tile_gate(u, 4 * h + step)
                    for e in range(E):
                        tile_add(u, e)
                        if e in (1, 4):
                            k, g = left.pop(0)
                            conv_group(T + k, g)
                for k, g in left:
                    conv_group(T + k, g)
                if step == 3:
                    conv_add(T + 2)

            def dense_step(b, h, step, T, u, with_experts):
                g = step // 2
                v = (b * 2 + h) * ND + g
                left = list(STEP_GROUPS[step])

                def next_group():
                    k, gg = left.pop(0)
                    if (k, gg) == (2, 0):
                        dve.wait_ge(s.red_turned, T + 2)
                    conv_group(T + k, gg)

                if with_experts:
                    tile_gate(u, 4 * h + step)
                next_group()
                if not with_experts:
                    tables_stored(dve)
                    dve.wait_ge(s.xnorm_stored, 16 * B)
                    dve.wait_ge(s.values_stored, 16 * B)
                dense_positions(v, g, h)
                for m in range(8):
                    dense_mult(v, m)
                    if m:
                        dense_take(v, m - 1)
                        if with_experts:
                            tile_add(u, m - 1)
                    if m in ((1, 3, 5, 7) if step == 0 else (1, 3, 6)):
                        next_group()
                    if step == 2 and m == 7:
                        conv_add(T + 1, OUT_BANK)
                        next_group()
                dense_take(v, 7)
                if with_experts:
                    tile_add(u, 7)
                next_group()
                dense_spread(v)
                if step == 0:
                    conv_add(T)
                dense_add(b, h, v, T if step == 0 else T + 1)

            def attention(b, next_image):
                def meanwhile(i):
                    if next_image and i < EARLY * G:
                        conv_group(NT * (b + 1) + i // G, i % G)

                img = x_tok[:, bass.ds(b * NT, NT), :]
                one = lambda t: tok(b * NT + t).rearrange("p o c -> p (o c)")
                dve.wait_ge(s.conv_added, NT * (b + 1))
                for t in range(NT):
                    own_wait(dve)
                    last = dve.bn_stats(f_stats[:, t, :], one(t))
                chain(s.ln_chain, last, b + 1)
                own_wait(dve)
                for t in range(NT):
                    last = dve.bn_aggr(f_mv[:, t, :], f_stats[:, t, :])
                last.then_inc(s.ln_stats, 1)
                dve.wait_ge(s.ln_std, b + 1)
                chain(s.ln_recip, dve.reciprocal(f_r[:, :], f_sd[:, :]), b + 1)
                for t in range(NT):
                    last = dve.tensor_scalar(tn_tok[:, t, :], one(t), f_mv[:, t, 0:1], f_r[:, t:t + 1],
                                             ALU.subtract, ALU.mult)
                last.then_inc(s.tile_normalised, 1)
                meanwhile(0)
                dve.wait_ge(s.temps_summed, b + 1)
                chain(s.scale_chain, dve.tensor_scalar(temp_sb, ps[:, 7, :], btemp_col[:, :], -0.4, ALU.add, ALU.max),
                      2 * b + 1)
                chain(s.scale_chain, dve.tensor_scalar(temp_sb, temp_sb, 0.4, 0.5, ALU.min, ALU.add), 2 * b + 2)
                dve.reciprocal(rtemp, temp_sb).then_inc(s.rtemp_ready, 1)
                dve.wait_ge(s.xp_summed, b + 1)
                dve.tensor_tensor(xp_tok, ps[:, 3:7, :].rearrange("p a (t c) -> p (a t) c", t=2),
                                  bx_b[:, :].rearrange("p (o c) -> p o c", o=1).broadcast_to([P, NT, 256]),
                                  ALU.add).then_inc(s.xp_copied, 1)
                dve.tensor_tensor(img, img, boutb_b[:, :].rearrange("p (o c) -> p o c", o=1)
                                  .broadcast_to([P, NT, C]), ALU.add).then_inc(s.bout_added, 1)
                for i in range(4):
                    h, c = i // 2, i % 2
                    if i in (1, 2):
                        meanwhile(i)
                    dve.wait_ge(s.logits_biased, 4 * b + i + 1)
                    half = eT[:, h, c * 512:(c + 1) * 512]
                    dve.tensor_tensor(half, half, ps[:, 4 + 2 * (i % 2), :], ALU.mult).then_inc(s.logits_done, 1)
                    if c == 1:
                        dve.wait_ge(s.logits_done, 4 * b + i + 1)
                        chain(s.max_chain, dve.tensor_reduce(a_max[:, h:h + 1], eT[:, h, :], AX, ALU.max),
                              2 * b + h + 1)
                        dve.tensor_scalar(a_nmax[:, h:h + 1], a_max[:, h:h + 1], -1.0, None, ALU.mult)\
                           .then_inc(s.max_done, 1)
                meanwhile(3)
                dve.wait_ge(s.exp_done, 2 * b + 2)
                chain(s.gn_chain, dve.reciprocal(a_rs[:, :], a_sum[:, :]), 4 * B + 4 * b + 1)
                chain(s.gn_chain, dve.tensor_tensor(a_norm[:, :], a_sum[:, :], a_rs[:, :], ALU.mult),
                      4 * B + 4 * b + 2)
                chain(s.gn_chain, dve.tensor_scalar(a_norm[:, :], a_norm[:, :], 1e-5, None, ALU.add),
                      4 * B + 4 * b + 3)
                chain(s.gn_chain, dve.reciprocal(a_rn[:, :], a_norm[:, :]), 4 * B + 4 * b + 4)
                chain(s.divisors_chain, dve.tensor_tensor(a_sc[:, :], a_rs[:, :], a_rn[:, :], ALU.mult), b + 1)
                dve.tensor_tensor(a_sc[:, :], a_sc[:, :], a_rs[:, :], ALU.mult).then_inc(s.scale_done, 1)
                meanwhile(4)
                meanwhile(5)
                dve.wait_ge(s.slice_sums, b + 1)
                dve.tensor_tensor(bdE, ps[:, 7, 0:256].rearrange("p (h n) -> p h n", h=2),
                                  head_mask[:, :].rearrange("p (o n) -> p o n", o=1).broadcast_to([P, 2, P]),
                                  ALU.mult).then_inc(s.bdE_done, 1)
                if next_image:
                    conv_add(NT * (b + 1))
                meanwhile(6)
                dve.wait_ge(s.attn_out, b + 1)
                dve.wait_ge(s.bout_added, b + 1)
                dve.tensor_tensor(img, img, ps[:, 5:7, :].rearrange("p a (t c) -> p (a t) c", t=4), ALU.add)\
                   .then_inc(s.attn_added, 1)
                dve.wait_ge(s.attn_added, b + 1)
                CH = 4
                own_wait(dve)
                for t in range(NT):
                    last = dve.bn_stats(f_stats[:, t, :], one(t))
                chain(s.en_chain, last, CH * b + 1)
                own_wait(dve)
                for t in range(NT):
                    last = dve.bn_aggr(norms[:, t, 0:2], f_stats[:, t, :])
                last.then_inc(s.en_stats1, 1)
                meanwhile(7)
                dve.wait_ge(s.en_std1, b + 1)
                chain(s.en_chain, dve.reciprocal(norms[:, :, 1], f_sd[:, :]), CH * b + 2)
                for t in range(NT):
                    last = dve.tensor_scalar(tn_tok[:, t, :], one(t), norms[:, t, 0:1], norms[:, t, 1:2],
                                             ALU.subtract, ALU.mult)
                chain(s.en_chain, last, CH * b + 3)
                own_wait(dve)
                for t in range(NT):
                    last = dve.bn_stats(f_stats[:, t, :], tn_tok[:, t, :])
                chain(s.en_chain, last, CH * b + 4)
                own_wait(dve)
                for t in range(NT):
                    last = dve.bn_aggr(norms[:, t, 2:4], f_stats[:, t, :])
                last.then_inc(s.en_stats2, 1)
                meanwhile(8)
                dve.wait_ge(s.en_std2, b + 1)
                chain(s.en_ready, dve.reciprocal(norms[:, :, 3], f_sd[:, :]), b + 1)

            def route(b, next_image, between=lambda: None):
                for t in range(NT):
                    last = dve.tensor_scalar(xn_tok[:, t, :], tn_tok[:, t, :], norms[:, t, 2:3], norms[:, t, 3:4],
                                             ALU.subtract, ALU.mult)
                last.then_inc(r.xn_ready, 1)
                RC = 2 * NT + 2
                if next_image:
                    conv_group(NT * (b + 1) + 1, G - 3)
                    conv_group(NT * (b + 1) + 1, G - 2)
                dve.wait_ge(r.router_summed, b + 1)
                chain(r.router_chain, dve.tensor_tensor(
                    rl[:, 0:NT, :], ps[:, 7, 0:NT * E].rearrange("p (t e) -> p t e", e=E),
                    br_b[:, :].rearrange("p (o e) -> p o e", o=1).broadcast_to([P, NT, E]), ALU.add), RC * b + 1)
                own_wait(dve)
                for t in range(NT):
                    dve.max(top_v[:, t, :], rl[:, t, :]).then_inc(r.router_chain, 1)
                dve.wait_ge(r.router_chain, RC * b + 1 + NT)
                own_wait(dve)
                for t in range(NT):
                    dve.max_index(top_i[:, t, :], top_v[:, t, :], rl[:, t, :]).then_inc(r.router_chain, 1)
                dve.tensor_tensor(g_d[:, 0:NT], top_v[:, 0:NT, 1], top_v[:, 0:NT, 0], ALU.subtract)\
                   .then_inc(r.router_chain, 1)
                dve.wait_ge(r.router_chain, RC * b + 1 + 2 * NT)
                dve.tensor_copy(top_f[:, 0:NT, :], top_i[:, 0:NT, 0:2])
                dve.wait_ge(r.exp_ready, b + 1)
                chain(r.gate_chain, dve.tensor_scalar(g_den[:, 0:NT], g_e[:, 0:NT], 1.0, None, ALU.add), 5 * b + 1)
                chain(r.gate_chain, dve.reciprocal(g_w1[:, 0:NT], g_den[:, 0:NT]), 5 * b + 2)
                chain(r.gate_chain, dve.tensor_tensor(g_w2[:, 0:NT], g_w1[:, 0:NT], g_e[:, 0:NT], ALU.mult),
                      5 * b + 3)
                experts_8 = expert_no[:, :].rearrange("p (o e) -> p o e", o=1).broadcast_to([P, NT, E])
                wide = lambda a: a.rearrange("p (t o) -> p t o", o=1).broadcast_to([P, NT, E])
                dve.tensor_tensor(gate[:, :, :], experts_8, wide(top_f[:, :, 0]), ALU.is_equal)
                chain(r.gate_chain, dve.tensor_tensor(gate2[:, :, :], experts_8, wide(top_f[:, :, 1]),
                                                      ALU.is_equal), 5 * b + 4)
                dve.tensor_tensor(gate[:, :, :], gate[:, :, :], wide(g_w1[:, :]), ALU.mult)
                chain(r.gate_chain, dve.tensor_tensor(gate2[:, :, :], gate2[:, :, :], wide(g_w2[:, :]), ALU.mult),
                      5 * b + 5)
                dve.tensor_tensor(gate[:, :, :], gate[:, :, :], gate2[:, :, :], ALU.add).then_inc(r.gate_done, 1)
                if next_image:
                    conv_group(NT * (b + 1) + 1, G - 1)
                dve.wait_ge(r.b2_summed, b + 1)
                img = x_tok[:, bass.ds(b * NT, NT), :]
                dve.tensor_tensor(img, img, ps[:, 3:5, :].rearrange("p a (t c) -> p (a t) c", t=4), ALU.add)\
                   .then_inc(r.b2_added, 1)
                dve.wait_ge(r.b2_added, b + 1)
                if next_image:
                    conv_add(NT * (b + 1) + 1)

            def image_experts(f, n, ntok, T0):
                tile_of = lambda t: tok(T0 + t).rearrange("p o c -> p (o c)")
                tiles = ntok // P
                units = [(c, e) for c in range(n // tiles) for e in range(E)]
                dve.wait_ge(r.gate_done, B)
                for i, (c, e) in enumerate(units):
                    for t in range(tiles):
                        m = i * tiles + t
                        tt = c * tiles + t
                        dve.wait_ge(f.expert_summed, m + 1)
                        if e:
                            dve.wait_ge(f.expert_added, m - tiles + 1)
                        dve.scalar_tensor_tensor(tile_of(tt), ps[:, Y_BANK[m % 2], 0:C], gate[:, tt, e:e + 1],
                                                 tile_of(tt), ALU.mult, ALU.add).then_inc(f.expert_added, 1)

            small_constants()
            conv_constants()
            prep(0)
            dense_constants()
            dve.tensor_copy(idx_now[:, :], idx_all[:, 0, :]).then_inc(s.idx_ready, G)
            dve.wait_ge(s.x_tok_loaded, 16 * B)
            chain(s.out_bias_added, dve.tensor_tensor(
                x_tok[:, :, :], x_tok[:, :, :], outb_b[:, :].rearrange("p (o c) -> p o c", o=1)
                .broadcast_to([P, TILES, C]), ALU.add), 1)
            for b in range(1, B):
                prep(b)
                if b == EARLY:
                    dense_weights_laid_out()
                    for g in range(G):
                        conv_group(b - 1, g)
                    finish_setup()
                    dve.wait_ge(s.row_bias_copied, 1)
                    conv_add(b - 1)
                elif b < EARLY:
                    for g in range(G):
                        conv_group(b - 1, g)
                    conv_add(b - 1)

            def image(b, with_experts):
                with dve.Fori(0, 2) as h:
                    T = b * NT + EARLY + 3 * h
                    for step in range(4):
                        u = b * NT - NT + 4 * h + step
                        if step % 2 == 0:
                            dense_step(b, h, step, T, u, with_experts)
                        else:
                            plain_step(h, step, T, u, with_experts)

            image(0, False)
            with dve.Fori(1, B) as b:
                attention(b - 1, True)
                route(b - 1, True)
                image(b, True)
            attention(B - 1, False)
            route(B - 1, False)
            image_experts(end, NT, 512, TILES - NT)


def kernel(**inputs):
    import numpy as _np
    import concourse.bacc as _bacc
    from concourse import mybir as _mybir
    from concourse.bass_utils import run_bass_kernel_spmd as _run

    nc = _bacc.Bacc("TRN2", target_bir_lowering=False, num_devices=1)
    arrays, aps = {}, {}
    for name, value in inputs.items():
        a = _np.ascontiguousarray(value)
        arrays[f"in_{name}"] = a
        aps[name] = nc.dram_tensor(f"in_{name}", a.shape, _mybir.dt.from_np(a.dtype), kind="ExternalInput").ap()
    shape = arrays["in_x"].shape
    out = nc.dram_tensor("out_0", shape, _mybir.dt.float32, kind="ExternalOutput").ap()
    conv_attn_moe(nc, aps, out)
    r = _run(nc, [arrays], core_ids=[0])
    return r.results[0]["out_0"]
```
